# Optimizing a Trainium2 kernel written in Bass

```python
import numpy as np
import jax
import jax.numpy as jnp

def _softmax(x, axis=-1):
    return jax.nn.softmax(x, axis=axis)

def _gelu(x):
    return jax.nn.gelu(x, approximate=True)

def _silu(x):
    return jax.nn.silu(x)

def _sigmoid(x):
    return jax.nn.sigmoid(x)

def _layernorm(x, axis=-1, eps=1e-05):
    m = jnp.mean(x, axis=axis, keepdims=True)
    v = jnp.var(x, axis=axis, keepdims=True)
    return (x - m) / jnp.sqrt(v + eps)

def _scatter_add(tgt, idx, src, axis=0):
    return tgt.at[idx].add(src)

def _segment_sum(src, seg, n):
    return jax.ops.segment_sum(src, seg, n)
kernel_name = 'mk_early_fusion_d4_tok_img256_r4_f56d0d'

def setup_inputs(seed: int=0):
    np.random.seed(seed)
    _w = jnp.asarray

    def _rec_inputs():
        import jax
        import jax.numpy as jnp
        _rk = jax.random.key(seed)
        x = -0.0003702 + 0.999946 * jax.random.normal(jax.random.fold_in(_rk, 1), (16, 1, 64, 1000), jnp.float32)
        txt = 0.281643 + 0.58738 * jax.random.normal(jax.random.fold_in(_rk, 2), (16, 128, 64), jnp.float32)
        return (x, txt)
    x, txt = _rec_inputs()

    def _L0_tok_setup():
        import jax, jax.numpy as jnp
        import numpy as np
        PH, PW = (64, 25)
        SH, SW = (64, 12)

        def _unfold(x, ph, pw, sh, sw):
            B, C, H, W = x.shape
            nh = (H - ph) // sh + 1
            nw = (W - pw) // sw + 1
            rows = jnp.arange(nh)[:, None] * sh + jnp.arange(ph)[None, :]
            cols = jnp.arange(nw)[:, None] * sw + jnp.arange(pw)[None, :]
            p = x[:, :, rows, :]
            p = p[:, :, :, :, cols]
            p = jnp.transpose(p, (0, 2, 4, 1, 3, 5))
            return p.reshape(B, nh * nw, C * ph * pw)
        key = jax.random.key(seed)
        kx, kw = jax.random.split(key, 2)
        x = jax.random.normal(kx, (64, 1, 64, 1000), dtype=jnp.float32)
        in_dim = 1 * PH * PW
        weight = jax.random.normal(kw, (in_dim, 64), dtype=jnp.float32) / np.sqrt(in_dim).astype(np.float32)
        bias = jnp.zeros((64,), dtype=jnp.float32)
        return {'x': x, 'weight': weight, 'bias': bias}
    _L0_tok_all = _L0_tok_setup()
    _L0_tok_in = {k: v for k, v in _L0_tok_all.items() if k in ('weight', 'bias')}
    del _L0_tok_all

    def _L0_attn_setup():
        import jax, jax.numpy as jnp
        import numpy as np
        BATCH, T, IN, OUT, H = (16, 1024, 64, 64, 128)

        def _reference_tuple_inner(X, nu_log, theta_log, B_re, B_im, C_re, C_im, D, bh_re, bh_im, bias_output):
            lam = jnp.exp(-jnp.exp(nu_log) + 1j * jnp.exp(theta_log))
            gamma = jnp.sqrt(1.0 - jnp.abs(lam) ** 2)
            Bc = (B_re + 1j * B_im).astype(jnp.complex64)
            Cc = (C_re + 1j * C_im).astype(jnp.complex64)
            bh = (bh_re + 1j * bh_im).astype(jnp.complex64)
            u = gamma * (jnp.einsum('bti,hi->bth', X.astype(jnp.complex64), Bc) + bh)

            def step(h, u_t):
                h = lam * h + u_t + bh
                return (h, h)
            h0 = jnp.zeros((X.shape[0], lam.shape[0]), dtype=jnp.complex64)
            h_N, ys = jax.lax.scan(step, h0, jnp.swapaxes(u, 0, 1))
            Y = jnp.real(jnp.einsum('tbh,oh->bto', ys, Cc))
            Y = Y + jnp.einsum('bti,oi->bto', X, D) + bias_output
            return (Y, h_N)
        key = jax.random.key(seed)
        ks = jax.random.split(key, 8)
        gB = float(np.sqrt(6.0 / (H + IN)))
        gC = float(np.sqrt(6.0 / (OUT + H)))
        gD = float(np.sqrt(6.0 / (OUT + IN)))
        return {'X': jax.random.normal(ks[0], (BATCH, T, IN), dtype=jnp.float32), 'nu_log': jax.random.uniform(ks[1], (H,), dtype=jnp.float32), 'theta_log': jax.random.uniform(ks[2], (H,), dtype=jnp.float32), 'B_re': jax.random.uniform(ks[3], (H, IN), jnp.float32, -gB, gB), 'B_im': jax.random.uniform(ks[4], (H, IN), jnp.float32, -gB, gB), 'C_re': jax.random.uniform(ks[5], (OUT, H), jnp.float32, -gC, gC), 'C_im': jax.random.uniform(ks[6], (OUT, H), jnp.float32, -gC, gC), 'D': jax.random.uniform(ks[7], (OUT, IN), jnp.float32, -gD, gD), 'bh_re': jnp.zeros((H,), jnp.float32), 'bh_im': jnp.zeros((H,), jnp.float32), 'bias_output': jnp.zeros((OUT,), jnp.float32)}
    _L0_attn_all = _L0_attn_setup()
    _L0_attn_in = {k: v for k, v in _L0_attn_all.items() if k in ('nu_log', 'theta_log', 'B_re', 'B_im', 'C_re', 'C_im', 'D', 'bh_re', 'bh_im', 'bias_output')}
    del _L0_attn_all

    def _L0_ffn_setup():
        import jax, jax.numpy as jnp
        import numpy as np
        B, K, D = (128, 16, 64)
        E = 32
        H = int(D * 0.25)
        key = jax.random.key(seed)
        ks = jax.random.split(key, 7)
        d_rs = D ** (-0.5)
        h_rs = H ** (-0.5)
        x = jax.random.normal(ks[0], (B, K, D), dtype=jnp.float32)
        router_w = jax.random.uniform(ks[1], (E, D), jnp.float32, -d_rs, d_rs)
        router_b = jax.random.uniform(ks[2], (E,), jnp.float32, -d_rs, d_rs)
        W1 = jax.random.uniform(ks[3], (E, D, H), jnp.float32, -h_rs, h_rs)
        b1 = jax.random.uniform(ks[4], (E, H), jnp.float32, -h_rs, h_rs)
        W2 = jax.random.uniform(ks[5], (E, H, D), jnp.float32, -d_rs, d_rs)
        b2 = jax.random.uniform(ks[6], (E, D), jnp.float32, -d_rs, d_rs)
        return {'x': x, 'router_w': router_w, 'router_b': router_b, 'W1': W1, 'b1': b1, 'W2': W2, 'b2': b2}
    _L0_ffn_all = _L0_ffn_setup()
    _L0_ffn_in = {k: v for k, v in _L0_ffn_all.items() if k in ('router_w', 'router_b', 'W1', 'b1', 'W2', 'b2')}
    del _L0_ffn_all

    def _L1_attn_setup():
        import jax, jax.numpy as jnp
        import numpy as np
        B, S, C = (8, 256, 64)
        H, KD = (8, 64)
        HEAD_DIM = KD // H
        key = jax.random.key(seed)
        ks = jax.random.split(key, 5)
        sc = 0.02
        return {'x': jax.random.normal(ks[0], (B, S, C), dtype=jnp.float32), 'Wq': jax.random.normal(ks[1], (H * KD, C), dtype=jnp.float32) * sc, 'Wk': jax.random.normal(ks[2], (KD, C), dtype=jnp.float32) * sc, 'Wv': jax.random.normal(ks[3], (KD, C), dtype=jnp.float32) * sc, 'Wo': jax.random.normal(ks[4], (C, H * KD), dtype=jnp.float32) * sc}
    _L1_attn_all = _L1_attn_setup()
    _L1_attn_in = {k: v for k, v in _L1_attn_all.items() if k in ('Wq', 'Wk', 'Wv', 'Wo')}
    del _L1_attn_all

    def _L1_ffn_setup():
        import jax, jax.numpy as jnp
        import numpy as np
        E = 8
        K = 2
        D = 64
        H = 128
        DOUT = 64
        EPS = 1e-05
        key = jax.random.key(seed)
        ks = jax.random.split(key, 9)
        s = 0.02
        return {'x': jax.random.normal(ks[0], (4, 2048, D), jnp.float32), 'gamma': 1.0 + 0.05 * jax.random.normal(ks[1], (D,), jnp.float32), 'beta': 0.05 * jax.random.normal(ks[2], (D,), jnp.float32), 'Wr': 0.01 * jax.random.normal(ks[3], (D, E), jnp.float32), 'br': jnp.zeros((E,), jnp.float32), 'W1': s * jax.random.normal(ks[4], (E, D, H), jnp.float32), 'b1': s * jax.random.normal(ks[5], (E, H), jnp.float32), 'W2': s * jax.random.normal(ks[6], (E, H, DOUT), jnp.float32), 'b2': s * jax.random.normal(ks[7], (E, DOUT), jnp.float32)}
    _L1_ffn_all = _L1_ffn_setup()
    _L1_ffn_in = {k: v for k, v in _L1_ffn_all.items() if k in ('gamma', 'beta', 'Wr', 'br', 'W1', 'b1', 'W2', 'b2')}
    del _L1_ffn_all

    def _L2_attn_setup():
        import jax, jax.numpy as jnp
        import numpy as np
        key = jax.random.key(seed)
        k1, k2, k3 = jax.random.split(key, 3)
        b, n_t, n, n_h = (8, 256, 64, 8)
        s = jax.random.normal(k1, (b, n_t, n), dtype=jnp.float32)
        Q = jax.random.normal(k2, (n_h, n, n), dtype=jnp.float32) * 0.02
        E = jax.random.normal(k3, (n_h, n, n), dtype=jnp.float32) * 0.02
        return {'s': s, 'Q': Q, 'E': E}
    _L2_attn_all = _L2_attn_setup()
    _L2_attn_in = {k: v for k, v in _L2_attn_all.items() if k in ('Q', 'E')}
    del _L2_attn_all

    def _L2_ffn_setup():
        import jax, jax.numpy as jnp
        import numpy as np
        D_MODEL = 64
        EXPERT_DIM = 128
        NUM_EXPERTS = 8
        TOP_K = 2
        SEQ_LEN = 512
        BATCH = 2
        key = jax.random.key(seed)
        ks = jax.random.split(key, 8)
        s = 0.02
        x = jax.random.normal(ks[0], (SEQ_LEN, BATCH, D_MODEL), dtype=jnp.float32)
        Wg = jax.random.normal(ks[1], (D_MODEL, NUM_EXPERTS), dtype=jnp.float32) * s
        bg = jax.random.normal(ks[2], (NUM_EXPERTS,), dtype=jnp.float32) * s
        bias = jnp.zeros((NUM_EXPERTS,), dtype=jnp.float32)
        W1 = jax.random.normal(ks[3], (NUM_EXPERTS, D_MODEL, EXPERT_DIM), dtype=jnp.float32) * s
        b1 = jax.random.normal(ks[4], (NUM_EXPERTS, EXPERT_DIM), dtype=jnp.float32) * s
        W2 = jax.random.normal(ks[5], (NUM_EXPERTS, EXPERT_DIM, D_MODEL), dtype=jnp.float32) * s
        b2 = jax.random.normal(ks[6], (NUM_EXPERTS, D_MODEL), dtype=jnp.float32) * s
        return {'x': x, 'Wg': Wg, 'bg': bg, 'bias': bias, 'W1': W1, 'b1': b1, 'W2': W2, 'b2': b2}
    _L2_ffn_all = _L2_ffn_setup()
    _L2_ffn_in = {k: v for k, v in _L2_ffn_all.items() if k in ('Wg', 'bg', 'bias', 'W1', 'b1', 'W2', 'b2')}
    del _L2_ffn_all

    def _L3_attn_setup():
        import jax, jax.numpy as jnp
        import numpy as np
        key = jax.random.key(seed)
        k1, k2 = jax.random.split(key)
        B, N, D = (4, 1024, 64)
        inp = jax.random.normal(k1, (B, N, D), dtype=jnp.float32)
        q_weight = jax.random.normal(k2, (D, D), dtype=jnp.float32)
        return {'input': inp, 'q_weight': q_weight}
    _L3_attn_all = _L3_attn_setup()
    _L3_attn_in = {k: v for k, v in _L3_attn_all.items() if k in ('q_weight',)}
    del _L3_attn_all

    def _L3_ffn_setup():
        import jax, jax.numpy as jnp
        import numpy as np
        B, S, D = (8, 1024, 64)
        H = 4 * D
        CAPACITY = 0.5
        key = jax.random.key(seed)
        ks = jax.random.split(key, 6)
        x = jax.random.normal(ks[0], (B, S, D), dtype=jnp.float32)
        attention_mask = jnp.zeros((B, 1, 1, S), dtype=jnp.float32)
        wr = jax.random.normal(ks[1], (D, 1), dtype=jnp.float32) * 0.02
        br = jnp.zeros((1,), dtype=jnp.float32)
        w1 = jax.random.normal(ks[2], (D, H), dtype=jnp.float32) * 0.02
        b1 = jnp.zeros((H,), dtype=jnp.float32)
        w2 = jax.random.normal(ks[3], (H, D), dtype=jnp.float32) * 0.02
        b2 = jnp.zeros((D,), dtype=jnp.float32)
        return {'x': x, 'attention_mask': attention_mask, 'wr': wr, 'br': br, 'w1': w1, 'b1': b1, 'w2': w2, 'b2': b2}
    _L3_ffn_all = _L3_ffn_setup()
    _L3_ffn_in = {k: v for k, v in _L3_ffn_all.items() if k in ('attention_mask', 'wr', 'br', 'w1', 'b1', 'w2', 'b2')}
    del _L3_ffn_all
    return {'x': x, 'txt': txt, 'L0_tok_weight': _L0_tok_in['weight'], 'L0_tok_bias': _L0_tok_in['bias'], 'L0_attn_nu_log': _L0_attn_in['nu_log'], 'L0_attn_theta_log': _L0_attn_in['theta_log'], 'L0_attn_B_re': _L0_attn_in['B_re'], 'L0_attn_B_im': _L0_attn_in['B_im'], 'L0_attn_C_re': _L0_attn_in['C_re'], 'L0_attn_C_im': _L0_attn_in['C_im'], 'L0_attn_D': _L0_attn_in['D'], 'L0_attn_bh_re': _L0_attn_in['bh_re'], 'L0_attn_bh_im': _L0_attn_in['bh_im'], 'L0_attn_bias_output': _L0_attn_in['bias_output'], 'L0_ffn_router_w': _L0_ffn_in['router_w'], 'L0_ffn_router_b': _L0_ffn_in['router_b'], 'L0_ffn_W1': _L0_ffn_in['W1'], 'L0_ffn_b1': _L0_ffn_in['b1'], 'L0_ffn_W2': _L0_ffn_in['W2'], 'L0_ffn_b2': _L0_ffn_in['b2'], 'L1_attn_Wq': _L1_attn_in['Wq'], 'L1_attn_Wk': _L1_attn_in['Wk'], 'L1_attn_Wv': _L1_attn_in['Wv'], 'L1_attn_Wo': _L1_attn_in['Wo'], 'L1_ffn_gamma': _L1_ffn_in['gamma'], 'L1_ffn_beta': _L1_ffn_in['beta'], 'L1_ffn_Wr': _L1_ffn_in['Wr'], 'L1_ffn_br': _L1_ffn_in['br'], 'L1_ffn_W1': _L1_ffn_in['W1'], 'L1_ffn_b1': _L1_ffn_in['b1'], 'L1_ffn_W2': _L1_ffn_in['W2'], 'L1_ffn_b2': _L1_ffn_in['b2'], 'L2_attn_Q': _L2_attn_in['Q'], 'L2_attn_E': _L2_attn_in['E'], 'L2_ffn_Wg': _L2_ffn_in['Wg'], 'L2_ffn_bg': _L2_ffn_in['bg'], 'L2_ffn_bias': _L2_ffn_in['bias'], 'L2_ffn_W1': _L2_ffn_in['W1'], 'L2_ffn_b1': _L2_ffn_in['b1'], 'L2_ffn_W2': _L2_ffn_in['W2'], 'L2_ffn_b2': _L2_ffn_in['b2'], 'L3_attn_q_weight': _L3_attn_in['q_weight'], 'L3_ffn_attention_mask': _L3_ffn_in['attention_mask'], 'L3_ffn_wr': _L3_ffn_in['wr'], 'L3_ffn_br': _L3_ffn_in['br'], 'L3_ffn_w1': _L3_ffn_in['w1'], 'L3_ffn_b1': _L3_ffn_in['b1'], 'L3_ffn_w2': _L3_ffn_in['w2'], 'L3_ffn_b2': _L3_ffn_in['b2']}

def reference(x, txt, L0_tok_weight, L0_tok_bias, L0_attn_nu_log, L0_attn_theta_log, L0_attn_B_re, L0_attn_B_im, L0_attn_C_re, L0_attn_C_im, L0_attn_D, L0_attn_bh_re, L0_attn_bh_im, L0_attn_bias_output, L0_ffn_router_w, L0_ffn_router_b, L0_ffn_W1, L0_ffn_b1, L0_ffn_W2, L0_ffn_b2, L1_attn_Wq, L1_attn_Wk, L1_attn_Wv, L1_attn_Wo, L1_ffn_gamma, L1_ffn_beta, L1_ffn_Wr, L1_ffn_br, L1_ffn_W1, L1_ffn_b1, L1_ffn_W2, L1_ffn_b2, L2_attn_Q, L2_attn_E, L2_ffn_Wg, L2_ffn_bg, L2_ffn_bias, L2_ffn_W1, L2_ffn_b1, L2_ffn_W2, L2_ffn_b2, L3_attn_q_weight, L3_ffn_attention_mask, L3_ffn_wr, L3_ffn_br, L3_ffn_w1, L3_ffn_b1, L3_ffn_w2, L3_ffn_b2):
    import jax
    import jax.numpy as jnp

    def _L0_tok_ref(x, weight, bias):
        import jax, jax.numpy as jnp
        import numpy as np
        PH, PW = (64, 25)
        SH, SW = (64, 12)

        def _unfold(x, ph, pw, sh, sw):
            B, C, H, W = x.shape
            nh = (H - ph) // sh + 1
            nw = (W - pw) // sw + 1
            rows = jnp.arange(nh)[:, None] * sh + jnp.arange(ph)[None, :]
            cols = jnp.arange(nw)[:, None] * sw + jnp.arange(pw)[None, :]
            p = x[:, :, rows, :]
            p = p[:, :, :, :, cols]
            p = jnp.transpose(p, (0, 2, 4, 1, 3, 5))
            return p.reshape(B, nh * nw, C * ph * pw)
        p = _unfold(x, PH, PW, SH, SW)
        return jax.nn.gelu(jnp.einsum('bnk,kd->bnd', p, weight) + bias, approximate=False)

    def _L0_attn_ref(X, nu_log, theta_log, B_re, B_im, C_re, C_im, D, bh_re, bh_im, bias_output):
        import jax, jax.numpy as jnp
        import numpy as np
        BATCH, T, IN, OUT, H = (16, 1024, 64, 64, 128)

        def _reference_tuple_inner(X, nu_log, theta_log, B_re, B_im, C_re, C_im, D, bh_re, bh_im, bias_output):
            lam = jnp.exp(-jnp.exp(nu_log) + 1j * jnp.exp(theta_log))
            gamma = jnp.sqrt(1.0 - jnp.abs(lam) ** 2)
            Bc = (B_re + 1j * B_im).astype(jnp.complex64)
            Cc = (C_re + 1j * C_im).astype(jnp.complex64)
            bh = (bh_re + 1j * bh_im).astype(jnp.complex64)
            u = gamma * (jnp.einsum('bti,hi->bth', X.astype(jnp.complex64), Bc) + bh)

            def step(h, u_t):
                h = lam * h + u_t + bh
                return (h, h)
            h0 = jnp.zeros((X.shape[0], lam.shape[0]), dtype=jnp.complex64)
            h_N, ys = jax.lax.scan(step, h0, jnp.swapaxes(u, 0, 1))
            Y = jnp.real(jnp.einsum('tbh,oh->bto', ys, Cc))
            Y = Y + jnp.einsum('bti,oi->bto', X, D) + bias_output
            return (Y, h_N)
        return _reference_tuple_inner(X, nu_log, theta_log, B_re, B_im, C_re, C_im, D, bh_re, bh_im, bias_output)[0]

    def _L0_ffn_ref(x, router_w, router_b, W1, b1, W2, b2):
        import jax, jax.numpy as jnp
        import numpy as np
        B, K, D = (128, 16, 64)
        E = 32
        H = int(D * 0.25)
        xf = x.reshape(-1, D)
        logits = xf @ router_w.T + router_b
        idx = jnp.argmax(logits, axis=-1)
        w1t = jnp.take(W1, idx, axis=0)
        h = jnp.einsum('nd,ndh->nh', xf, w1t) + jnp.take(b1, idx, axis=0)
        h = jax.nn.relu(h)
        w2t = jnp.take(W2, idx, axis=0)
        out = jnp.einsum('nh,nhd->nd', h, w2t) + jnp.take(b2, idx, axis=0)
        out = jax.nn.relu(out)
        return out.reshape(x.shape)

    def _L1_attn_ref(x, Wq, Wk, Wv, Wo):
        import jax, jax.numpy as jnp
        import numpy as np
        B, S, C = (8, 256, 64)
        H, KD = (8, 64)
        HEAD_DIM = KD // H
        b, s, c = x.shape
        q = jnp.einsum('bsc,oc->bso', x, Wq).reshape(b, s, H, KD).transpose(0, 2, 1, 3)
        k = jnp.einsum('bsc,oc->bos', x, Wk)
        v_conv = jnp.einsum('bsc,oc->bos', x, Wv)
        v = v_conv.reshape(b, s, KD)
        scale = 1.0 / np.sqrt(HEAD_DIM).astype(np.float32)
        scores = jnp.einsum('bhsd,bdt->bhst', q, k) * scale
        attn = jax.nn.softmax(scores, axis=-1)
        ctx = jnp.einsum('bhst,btd->bhsd', attn, v)
        ctx = ctx.transpose(0, 2, 1, 3).reshape(b, H * KD, s)
        out = jnp.einsum('bcp,oc->bop', ctx, Wo)
        return out.transpose(0, 2, 1)

    def _L1_ffn_ref(x, gamma, beta, Wr, br, W1, b1, W2, b2):
        import jax, jax.numpy as jnp
        import numpy as np
        E = 8
        K = 2
        D = 64
        H = 128
        DOUT = 64
        EPS = 1e-05
        mu = jnp.mean(x, axis=-1, keepdims=True)
        var = jnp.mean(jnp.square(x - mu), axis=-1, keepdims=True)
        xn = (x - mu) * jax.lax.rsqrt(var + EPS) * gamma + beta
        logits = jnp.einsum('bsd,de->bse', xn, Wr) + br
        top_vals, top_idx = jax.lax.top_k(logits, K)
        w = jax.nn.softmax(top_vals, axis=-1)
        w_full = jnp.einsum('bsk,bske->bse', w, jax.nn.one_hot(top_idx, E, dtype=w.dtype))
        y = jnp.zeros(x.shape[:-1] + (DOUT,), x.dtype)
        for e in range(E):
            h = jax.nn.gelu(jnp.einsum('bsd,dh->bsh', xn, W1[e]) + b1[e], approximate=False)
            y_e = jnp.einsum('bsh,hd->bsd', h, W2[e]) + b2[e]
            y = y + y_e * w_full[..., e, None]
        return y

    def _L2_attn_ref(s, Q, E):
        import jax, jax.numpy as jnp
        import numpy as np
        n_t = s.shape[1]
        qs = jnp.einsum('bti,hij->bhtj', s, Q)
        Omega = jnp.einsum('bhtj,buj->bhtu', qs, s)
        mask = jnp.tril(jnp.ones((n_t, n_t), dtype=s.dtype))
        Omega = Omega * mask
        es = jnp.einsum('hij,buj->bhui', E, s)
        r = jnp.einsum('bhtu,bhui->bti', Omega, es)
        return r

    def _L2_ffn_ref(x, Wg, bg, bias, W1, b1, W2, b2):
        import jax, jax.numpy as jnp
        import numpy as np
        D_MODEL = 64
        EXPERT_DIM = 128
        NUM_EXPERTS = 8
        TOP_K = 2
        SEQ_LEN = 512
        BATCH = 2
        x_flat = x.reshape(-1, D_MODEL)
        gate_logits = x_flat @ Wg + bg + bias
        topk_vals, topk_idx = jax.lax.top_k(gate_logits, TOP_K)
        topk_w = jax.nn.softmax(topk_vals, axis=-1)
        combine = (jax.nn.one_hot(topk_idx, NUM_EXPERTS, dtype=x.dtype) * topk_w[..., None]).sum(axis=1)
        h = jax.nn.relu(jnp.einsum('td,edh->teh', x_flat, W1) + b1)
        y = jnp.einsum('teh,ehd->ted', h, W2) + b2
        out = jnp.einsum('ted,te->td', y, combine)
        return out.reshape(x.shape)

    def _L3_attn_ref(input, q_weight):
        import jax, jax.numpy as jnp
        import numpy as np
        query = jnp.einsum('bnd,de->bne', input, q_weight)
        att = jax.nn.sigmoid(jnp.einsum('bnd,bmd->bnm', query, input))
        value = jnp.einsum('bnm,bmd->bnd', att, input)
        return value

    def _L3_ffn_ref(x, attention_mask, wr, br, w1, b1, w2, b2):
        import jax, jax.numpy as jnp
        import numpy as np
        B, S, D = (8, 1024, 64)
        H = 4 * D
        CAPACITY = 0.5
        b, s, d = x.shape
        weights = (jnp.einsum('bsd,do->bso', x, wr) + br)[..., 0]
        k = max(1, int(CAPACITY * s))
        kk = k - 1 if k > 1 else 1
        _, idx = jax.lax.top_k(weights, k)
        sel_idx = idx[:, :kk]
        sel = jnp.take_along_axis(x, sel_idx[:, :, None], axis=1)
        h = jax.nn.gelu(jnp.einsum('bkd,dh->bkh', sel, w1) + b1)
        y = jnp.einsum('bkh,hd->bkd', h, w2) + b2
        w_sel = jnp.take_along_axis(weights, sel_idx, axis=1)
        y = y * w_sel[..., None]
        batch_idx = jnp.arange(b)[:, None]
        processed = jnp.zeros_like(x).at[batch_idx, sel_idx].set(y)
        return processed + x
    h = _L0_tok_ref(x, L0_tok_weight, L0_tok_bias)
    h = jnp.concatenate([h, txt], axis=1)
    h = h + _L0_attn_ref(_layernorm(h, axis=-1), L0_attn_nu_log, L0_attn_theta_log, L0_attn_B_re, L0_attn_B_im, L0_attn_C_re, L0_attn_C_im, L0_attn_D, L0_attn_bh_re, L0_attn_bh_im, L0_attn_bias_output)
    h = h + _L0_ffn_ref(_layernorm(h, axis=-1), L0_ffn_router_w, L0_ffn_router_b, L0_ffn_W1, L0_ffn_b1, L0_ffn_W2, L0_ffn_b2)
    h = h + _L1_attn_ref(_layernorm(h, axis=-1), L1_attn_Wq, L1_attn_Wk, L1_attn_Wv, L1_attn_Wo)
    h = h + _L1_ffn_ref(_layernorm(h, axis=-1), L1_ffn_gamma, L1_ffn_beta, L1_ffn_Wr, L1_ffn_br, L1_ffn_W1, L1_ffn_b1, L1_ffn_W2, L1_ffn_b2)
    h = h + _L2_attn_ref(_layernorm(h, axis=-1), L2_attn_Q, L2_attn_E)
    h = h + _L2_ffn_ref(_layernorm(h, axis=-1), L2_ffn_Wg, L2_ffn_bg, L2_ffn_bias, L2_ffn_W1, L2_ffn_b1, L2_ffn_W2, L2_ffn_b2)
    h = h + _L3_attn_ref(_layernorm(h, axis=-1), L3_attn_q_weight)
    h = h + _L3_ffn_ref(_layernorm(h, axis=-1), L3_ffn_attention_mask, L3_ffn_wr, L3_ffn_br, L3_ffn_w1, L3_ffn_b1, L3_ffn_w2, L3_ffn_b2)
    return h

_drawn_inputs = setup_inputs


def setup_inputs(seed=0):
    import zlib

    import numpy as np

    out = dict(_drawn_inputs(seed))
    spreads = {'L0_tok_bias': (0.0, 0.1),
     'L0_attn_bh_re': (0.0, 0.1),
     'L0_attn_bh_im': (0.0, 0.1),
     'L0_attn_bias_output': (0.0, 0.1),
     'L1_ffn_br': (0.0, 0.284),
     'L2_ffn_bias': (0.0, 0.8),
     'L3_ffn_b1': (0.0, 0.8),
     'L3_ffn_b2': (0.0, 0.8)}
    factors = {'L1_attn_Wq': 8.0,
     'L1_attn_Wk': 8.0,
     'L1_attn_Wv': 7.441,
     'L1_attn_Wo': 8.0,
     'L1_ffn_gamma': 8.0,
     'L1_ffn_beta': 8.0,
     'L1_ffn_Wr': 2.779,
     'L1_ffn_W1': 2.797,
     'L1_ffn_b1': 8.0,
     'L1_ffn_W2': 2.734,
     'L2_ffn_Wg': 8.0,
     'L2_ffn_bg': 8.0,
     'L2_ffn_W1': 8.0,
     'L2_ffn_b1': 8.0,
     'L2_ffn_W2': 8.0,
     'L2_ffn_b2': 8.0,
     'L3_ffn_wr': 8.0,
     'L3_ffn_w1': 8.0,
     'L3_ffn_w2': 8.0,
     'L1_ffn_b2': 3.117}
    for name, (base, spread) in spreads.items():
        noise = np.random.default_rng([zlib.crc32(name.encode()), seed]).standard_normal(out[name].shape)
        drawn = base * np.exp(spread * noise) if base else spread * noise
        out[name] = jnp.asarray(drawn.astype(out[name].dtype))
    for name, factor in factors.items():
        out[name] = (out[name] * factor).astype(out[name].dtype)
    return out
```

```python
from contextlib import ExitStack

import numpy as np
import concourse.bass as bass
from concourse import mybir

ALU = mybir.AluOpType
ACT = mybir.ActivationFunctionType
F32 = mybir.dt.float32
AX_X = mybir.AxisListType.X

B, T, D = 16, 210, 64
HT = T // 2
PAIRS = B // 2
NT = 4
W = 2 * T
PAIR = NT * D
PATCHES, KPAR, XM = 82, 13, 500
PSTEP = 6
HL = 128
E1, H1 = 32, 16
NH, KD = 8, 64
E2, H2 = 8, 128
H3 = 256
KEEP = T // 2 - 1
EPS = 1e-5
BIG = 1e30
LOWEST = -3e38

PACK64 = [("B_reT", HL), ("B_imT", HL), ("DT", D), ("routerT", E1), ("WqT", NH * KD), ("WkT2", 2 * KD), ("WvT", KD),
          ("L1WrT", E2), ("L1W1", E2 * H2), ("gamma", 1), ("beta", 1), ("Q", NH * D), ("ET", NH * D),
          ("L2WgT", E2), ("L2W1", E2 * H2), ("qw2", 2 * D), ("wr_rep", HT), ("L3w1", H3)]
PACK128 = [("tokw", KPAR * D), ("C_reT", D), ("C_imT", D), ("nu_log", 1), ("theta_log", 1), ("bh_re", 1),
           ("bh_im", 1), ("L0W2", 4 * D), ("WoT", 4 * D), ("L1W2", E2 * D), ("L1b1", E2), ("L2W2", E2 * D),
           ("L2b1", E2), ("L3w2", 2 * D), ("L3b1", 2), ("ident", 128), ("desc8", PAIRS * NT * E2),
           ("desc32", NT * E1), ("causal", T), ("earlier", 2 * T)]
PACK1 = [("tok_b", 2 * D), ("router_b", NT * E1), ("lru_b", PAIR), ("L1br", NT * E2), ("L1b2", E2 * D),
         ("L2bg", NT * E2), ("L2bias", NT * E2), ("L2b2", E2 * D), ("L3br", T), ("L3b2", PAIR)]
PACK96 = [("L0W1", E1 * H1), ("L0notmine", E1 * H1)]


def offsets(pack):
    at, o = {}, 0
    for name, n in pack:
        at[name] = (o, n)
        o += n
    return at, o


class Named:

    def __init__(self, tensor, pack):
        self.t, (self.at, _) = tensor, offsets(pack)

    def __call__(self, name, p0=0, p1=128, a=0, n=None):
        o, size = self.at[name]
        return self.t[p0:p1, o + a:o + a + (size - a if n is None else n)]


def split(ap, **kw):
    return ap.rearrange("p (t e) -> p t e", **kw)


def spread(ap, n):
    return ap.unsqueeze(2).to_broadcast([ap.shape[0], ap.shape[1], n])


def wait_reuse(eng, sem, value):
    if not isinstance(value, int) or value > 0:
        eng.wait_ge(sem, value)


def pipelined(eng, prologue, body):
    prologue()
    with eng.Fori(0, PAIRS // 2 - 1) as j:
        body(2 * j, 0, True)
        body(2 * j + 1, 1, True)
    body(PAIRS - 2, 0, True)
    body(PAIRS - 1, 1, False)


class Stage:

    def __init__(self, nc, ctx, name):
        self.nc, self.ctx, self.name = nc, ctx, name

    def sb(self, name, shape, dt=F32):
        return self.ctx.enter_context(self.nc.sbuf_tensor(f"{self.name}_{name}", shape, dt))

    def bank(self, name):
        return self.ctx.enter_context(self.nc.psum_tensor(f"{self.name}_{name}", [128, 512], F32))

    def sem(self, name):
        return self.ctx.enter_context(self.nc.semaphore(f"{self.name}_{name}"))


class Norm:

    def __init__(self, nc, st, res):
        self.nc, self.res = nc, res
        self.sum = st.sb("ln_sum", [128, 4, NT])
        self.sq = st.sb("ln_sq", [128, PAIR])
        self.var = st.sb("ln_var", [128, 2, NT])
        self.var_ready = st.sem("ln_var_ready")
        self.rstd_done = st.sem("ln_rstd_done")

    def stats(self, dve, n, p):
        nc, R = self.nc, self.res
        h = R.h[0:HT, bass.ds(n * PAIR, PAIR)]
        hc = R.hc[0:HT, bass.ds(n * PAIR, PAIR)]
        nc.vector.reduce_sum(self.sum[0:HT, p, :], split(h, t=NT), axis=AX_X)
        dve.drain()
        nc.vector.scalar_tensor_tensor(out=split(hc, t=NT), in0=spread(self.sum[0:HT, p, :], D), scalar=-1.0 / D,
                                       in1=split(h, t=NT), op0=ALU.mult, op1=ALU.add)
        dve.drain()
        nc.vector.tensor_tensor(self.sq[0:HT, :], hc, hc, ALU.mult)
        dve.drain()
        nc.vector.reduce_sum(self.sum[0:HT, 2 + p, :], split(self.sq[0:HT, :], t=NT), axis=AX_X)
        dve.drain()
        dve.wait_ge(self.rstd_done, n + 1)
        nc.vector.tensor_scalar(self.var[0:HT, p, :], self.sum[0:HT, 2 + p, :], 1.0 / D, EPS, ALU.mult, ALU.add)\
            .then_inc(self.var_ready, 1)

    def rstd(self, pool, n, p):
        pool.wait_ge(self.var_ready, n + 1)
        self.nc.gpsimd.tensor_tensor(self.res.rstd[0:HT, bass.ds(n * NT, NT)], self.var[0:HT, p, :],
                                     self.res.neghalf[0:HT, 0:NT], ALU.pow).then_inc(self.rstd_done, 1)

    def finish(self, pool):
        pool.sem_inc(self.rstd_done, 1)
        with pool.Fori(0, PAIRS // 2) as j:
            self.rstd(pool, 2 * j, 0)
            self.rstd(pool, 2 * j + 1, 1)


def normalise(nc, R, n, out):
    return nc.vector.tensor_tensor(split(out, t=NT), split(R.hc[0:HT, bass.ds(n * PAIR, PAIR)], t=NT),
                                   spread(R.rstd[0:HT, bass.ds(n * NT, NT)], D), ALU.mult)


def turn_pair(nc, R, bank, x):
    for smp in range(2):
        mm = nc.tensor.transpose(bank[0:2 * D, smp * HT:(smp + 1) * HT], x[0:HT, smp * 2 * D:(smp + 1) * 2 * D],
                                 R.c128("ident", 0, HT, 0, HT))
    return mm


def half_columns(xT, bank, half):
    return (xT.rearrange("p (s two c) -> p s two c", s=2, two=2)[:, :, half, :],
            bank[half * D:(half + 1) * D, 0:2 * HT].rearrange("p (s c) -> p s c", s=2))


class Head:

    def __init__(self, nc, st, res, dup=False):
        self.nc, self.res, self.dup = nc, res, dup
        self.xn = [st.sb(f"xn{p}", [128, PAIR]) for p in range(2)]
        self.xT = [st.sb(f"xT{p}", [128, W]) for p in range(2)]
        self.turned = st.bank("turned")
        self.xn_ready = st.sem("xn_ready")
        self.turned_ready = st.sem("turned_ready")
        self.xT_ready = st.sem("xT_ready")

    def dve(self, dve, n, q):
        normalise(self.nc, self.res, n, self.xn[q][0:HT, :]).then_inc(self.xn_ready, 1)

    def pe(self, pe, n, q):
        pe.wait_ge(self.xn_ready, n + 1)
        wait_reuse(pe, self.xT_ready, n)
        turn_pair(self.nc, self.res, self.turned, self.xn[q]).then_inc(self.turned_ready, 1)

    def act(self, act, n, q):
        act.wait_ge(self.turned_ready, n + 1)
        for rows in range(2 if self.dup else 1):
            for half in range(2):
                out, in_ = half_columns(self.xT[q][rows * D:(rows + 1) * D, :], self.turned, half)
                done = self.nc.scalar.copy(out, in_)
        done.then_inc(self.xT_ready, 1)


def products_bias(nc, out, R, row, tiles=1):
    return nc.tensor.matmul(out, R.ones[0:1, 0:HT], row, start=True, stop=False, skip_group_check=True)


def add(nc, out, lhsT, rhs, stop):
    return nc.tensor.matmul(out, lhsT, rhs, start=False, stop=stop, skip_group_check=True)


def hpair(R, n):
    return R.h[0:HT, bass.ds(n * PAIR, PAIR)]


def tokenizer(nc, R, x, txt, loads):
    with ExitStack() as ctx:
        st = Stage(nc, ctx, "tok")
        ln = Norm(nc, st, R)
        xs = [st.sb(f"x{p}", [128, 2, XM]) for p in range(2)]
        y = [st.bank(f"y{p}") for p in range(2)]
        pw = st.sb("pw", [128, 9, 2])
        tmp = st.sb("tmp", [128, T])
        ang = st.sb("ang", [128, 8])
        first_loaded, rest_loaded = st.sem("first_loaded"), st.sem("rest_loaded")
        x_loaded = [st.sem(f"x_loaded{p}") for p in range(2)]
        y_ready, y_used = st.sem("y_ready"), st.sem("y_used")
        consts, angle, turn, unit = st.sem("consts"), st.sem("angle"), st.sem("turn"), st.sem("unit")
        decay_sq, gamma_done = st.sem("decay_sq"), st.sem("gamma_done")
        block = ctx.enter_context(nc.Block())
        c128 = R.c128

        @block.sync
        def _(sp):
            for dst, src in loads[:2]:
                sp.dma_start(dst, src).then_inc(first_loaded, 16)

            def load(n, p):
                sp.wait_ge(y_ready, n - 1)
                sp.dma_start(xs[p][:], x[bass.ds(n, 1)].rearrange("a p s m -> (a p) s m")).then_inc(x_loaded[p], 16)

            for p in range(2):
                sp.dma_start(xs[p][:], x[p]).then_inc(x_loaded[p], 16)
            with sp.Fori(1, PAIRS // 2) as j:
                load(2 * j, 0)
                load(2 * j + 1, 1)

        @block.scalar
        def _(act):
            for dst, src in loads[2:]:
                act.dma_start(dst, src).then_inc(rest_loaded, 16)
            tokens = R.h[:].rearrange("p (b two d) -> p b two d", two=2, d=D)
            act.dma_start(tokens[PATCHES:HT, 0:B, 0, :], txt[:, 0:HT - PATCHES, :].rearrange("b t d -> t b d"))\
                .then_inc(rest_loaded, 16)
            act.dma_start(tokens[0:HT, 0:B, 1, :], txt[:, HT - PATCHES:, :].rearrange("b t d -> t b d"))\
                .then_inc(rest_loaded, 16)
            act.wait_ge(first_loaded, 32)
            nc.scalar.activation(ang[:, 0:1], c128("nu_log"), ACT.Exp)
            nc.scalar.activation(ang[:, 1:2], c128("theta_log"), ACT.Exp)
            act.drain()
            nc.scalar.activation(R.lru[:, 0:1], ang[:, 0:1], ACT.Exp, scale=-1.0).then_inc(angle, 1)
            act.wait_ge(turn, 1)
            nc.scalar.activation(ang[:, 4:5], ang[:, 2:3], ACT.Sin)
            nc.scalar.activation(ang[:, 5:6], ang[:, 2:3], ACT.Sin, scale=0.5).then_inc(unit, 1)
            act.wait_ge(rest_loaded, 16 * (len(loads)))

            def gelu(n, p):
                act.wait_ge(y_ready, n + 1)
                out = R.h[0:PATCHES, bass.ds(n * PAIR, PAIR)].rearrange("p (s two d) -> p s two d", two=2, d=D)
                act.nop(nofuse=True)
                nc.scalar.activation(out[:, :, 0, :], split(y[p][0:PATCHES, 0:2 * D], t=2), ACT.Gelu)\
                    .then_inc(y_used, 1)

            with act.Fori(0, PAIRS // 2) as j:
                gelu(2 * j, 0)
                gelu(2 * j + 1, 1)

        @block.tensor
        def _(pe):
            pe.wait_ge(consts, 1)
            pe.wait_ge(first_loaded, 32)
            pe.wait_ge(rest_loaded, 16 * (len(loads)))

            def patches(n, p, turn_no):
                pe.wait_ge(x_loaded[p], 16 * turn_no)
                pe.wait_ge(y_used, n + 1)
                nc.tensor.matmul(y[p][0:PATCHES, 0:2 * D], R.ones[0:1, 0:PATCHES], R.c1("tok_b", 0, 1),
                                 start=True, stop=False, skip_group_check=True)
                for s in range(2):
                    for c in range(KPAR):
                        k = 128 if c < KPAR - 1 else D
                        mm = add(nc, y[p][0:PATCHES, s * D:(s + 1) * D],
                                 xs[p][0:k, s, c:c + PSTEP * (PATCHES - 1) + 1:PSTEP],
                                 c128("tokw", 0, k, c * D, D), stop=c == KPAR - 1)
                mm.then_inc(y_ready, 1)

            with pe.Fori(0, PAIRS // 2) as j:
                patches(2 * j, 0, j + 1)
                patches(2 * j + 1, 1, j + 1)

        @block.vector
        def _(dve):
            nc.vector.memset(R.neghalf[:], -0.5)
            nc.vector.memset(R.half[:], 0.5)
            nc.vector.memset(R.euler[:], float(np.e))
            nc.vector.memset(R.ones[:], 1.0).then_inc(consts, 1)
            dve.sem_inc(y_used, 2)
            dve.wait_ge(angle, 1)
            nc.vector.tensor_tensor(ang[:, 6:7], R.lru[:, 0:1], R.lru[:, 0:1], ALU.mult)
            nc.vector.tensor_scalar(ang[:, 3:4], ang[:, 1:2], 1.0 / (2 * np.pi), None, ALU.mult)
            dve.drain()
            nc.vector.tensor_scalar(ang[:, 7:8], ang[:, 6:7], -1.0, 1.0, ALU.mult, ALU.add).then_inc(decay_sq, 1)
            nc.vector.tensor_scalar(ang[:, 3:4], ang[:, 3:4], 12582912.0, None, ALU.add)
            dve.drain()
            nc.vector.tensor_scalar(ang[:, 3:4], ang[:, 3:4], -12582912.0, None, ALU.add)
            dve.drain()
            nc.vector.scalar_tensor_tensor(out=ang[:, 2:3], in0=ang[:, 3:4], scalar=-6.28125, in1=ang[:, 1:2],
                                           op0=ALU.mult, op1=ALU.add)
            dve.drain()
            nc.vector.scalar_tensor_tensor(out=ang[:, 2:3], in0=ang[:, 3:4], scalar=-(2 * np.pi - 6.28125),
                                           in1=ang[:, 2:3], op0=ALU.mult, op1=ALU.add).then_inc(turn, 1)
            nc.vector.memset(R.decay[:], 1.0)
            dve.drain()
            nc.vector.tensor_scalar(R.decay[:], R.decay[:], R.lru[:, 0:1], None, ALU.mult)
            dve.drain()
            nc.vector.memset(R.decay[:, 0:W:T], 0.0)
            nc.vector.tensor_scalar(R.negC[:, 0:D], c128("C_reT"), -1.0, None, ALU.mult)
            nc.vector.tensor_scalar(R.negC[:, D:2 * D], c128("C_imT"), -1.0, None, ALU.mult)
            nc.vector.memset(R.cos[:, 0:1], 1.0)
            nc.vector.memset(R.sin[:, 0:1], 0.0)
            dve.wait_ge(unit, 1)
            nc.vector.tensor_copy(pw[:, 0, 1:2], ang[:, 4:5])
            nc.vector.tensor_tensor(ang[:, 3:4], ang[:, 5:6], ang[:, 5:6], ALU.mult)
            dve.drain()
            nc.vector.tensor_scalar(pw[:, 0, 0:1], ang[:, 3:4], -2.0, 1.0, ALU.mult, ALU.add)
            m, k = 1, 0
            while m < T:
                n = min(m, T - m)
                dve.drain()
                c, s = pw[:, k, 0:1], pw[:, k, 1:2]
                nc.vector.tensor_tensor(ang[:, 3:4], c, c, ALU.mult)
                dve.drain()
                nc.vector.scalar_tensor_tensor(out=ang[:, 3:4], in0=s, scalar=s, in1=ang[:, 3:4],
                                               op0=ALU.mult, op1=ALU.add)
                dve.drain()
                nc.vector.tensor_scalar(ang[:, 3:4], ang[:, 3:4], -0.5, 1.5, ALU.mult, ALU.add)
                dve.drain()
                nc.vector.tensor_scalar(pw[:, k, 0:2], pw[:, k, 0:2], ang[:, 3:4], None, ALU.mult)
                dve.drain()
                nc.vector.tensor_scalar(tmp[:, 0:n], R.sin[:, 0:n], s, None, ALU.mult)
                nc.vector.tensor_scalar(R.sin[:, m:m + n], R.sin[:, 0:n], c, None, ALU.mult)
                nc.vector.tensor_tensor(pw[:, k + 1, 0:1], s, s, ALU.mult)
                nc.vector.tensor_scalar(pw[:, k + 1, 1:2], c, s, 2.0, ALU.mult, ALU.mult)
                dve.drain()
                nc.vector.scalar_tensor_tensor(out=R.cos[:, m:m + n], in0=R.cos[:, 0:n], scalar=c, in1=tmp[:, 0:n],
                                               op0=ALU.mult, op1=ALU.subtract)
                nc.vector.scalar_tensor_tensor(out=R.sin[:, m:m + n], in0=R.cos[:, 0:n], scalar=s,
                                               in1=R.sin[:, m:m + n], op0=ALU.mult, op1=ALU.add)
                nc.vector.scalar_tensor_tensor(out=pw[:, k + 1, 0:1], in0=c, scalar=c, in1=pw[:, k + 1, 0:1],
                                               op0=ALU.mult, op1=ALU.subtract)
                m, k = m + n, k + 1
            dve.wait_ge(gamma_done, 1)
            nc.vector.tensor_scalar(R.lru[:, 2:3], R.lru[:, 1:2], 1.0, c128("bh_re"), ALU.add, ALU.mult)
            nc.vector.tensor_scalar(R.lru[:, 3:4], R.lru[:, 1:2], 1.0, c128("bh_im"), ALU.add, ALU.mult)
            dve.wait_ge(rest_loaded, 16 * (len(loads)))
            nc.vector.tensor_tensor(R.w96("L0W1", 0, 96), R.w96("L0W1", 0, 96), R.w96("L0notmine", 0, 96), ALU.add)

            def stats(n, p):
                dve.wait_ge(y_used, n + 3)
                ln.stats(dve, n, p)

            with dve.Fori(0, PAIRS // 2) as j:
                stats(2 * j, 0)
                stats(2 * j + 1, 1)

        @block.gpsimd
        def _(pool):
            pool.wait_ge(consts, 1)
            pool.wait_ge(decay_sq, 1)
            nc.gpsimd.tensor_tensor(R.lru[:, 1:2], ang[:, 7:8], R.half[:, 0:1], ALU.pow).then_inc(gamma_done, 1)
            ln.finish(pool)


def lru(nc, R):
    with ExitStack() as ctx:
        st = Stage(nc, ctx, "lru")
        ln, head = Norm(nc, st, R), Head(nc, st, R)
        u = [st.bank("u_re"), st.bank("u_im")]
        y = [st.bank(f"y{p}") for p in range(2)]
        v = [[st.sb(f"v{i}{p}", [128, W]) for i in range(2)] for p in range(2)]
        a = [st.sb(f"a{i}", [128, W]) for i in range(2)]
        m = [st.sb(f"m{i}", [128, W]) for i in range(4)]
        g = [st.sb(f"g{i}", [128, W]) for i in range(2)]
        out = [[st.sb(f"out{k}{p}", [128, W]) for k in range(4)] for p in range(2)]
        u_ready, v_ready, turned_in = st.sem("u_ready"), st.sem("v_ready"), st.sem("turned_in")
        pool_in, scanned, pool_out = st.sem("pool_in"), st.sem("scanned"), st.sem("pool_out")
        states, y_ready = st.sem("states"), st.sem("y_ready")
        block = ctx.enter_context(nc.Block())
        two = lambda ap: split(ap[:, 0:W], t=2)
        table = lambda t: t[:, 0:T].unsqueeze(1).to_broadcast([128, 2, T])
        COS, SIN = table(R.cos), table(R.sin)

        @block.vector
        def _(dve):
            def pro():
                head.dve(dve, 0, 0)

            def body(n, p, more):
                if more:
                    head.dve(dve, n + 1, 1 - p)
                dve.wait_ge(v_ready, n + 1)
                nc.vector.tensor_tensor(two(m[0]), two(v[p][0]), COS, ALU.mult)
                nc.vector.tensor_tensor(two(m[1]), two(v[p][1]), SIN, ALU.mult)
                nc.vector.tensor_tensor(two(m[2]), two(v[p][1]), COS, ALU.mult)
                dve.drain()
                nc.vector.tensor_tensor(a[0][:], m[0][:], m[1][:], ALU.add)
                dve.wait_ge(pool_in, n + 1)
                nc.vector.tensor_tensor(a[1][:], m[2][:], m[3][:], ALU.subtract)
                dve.drain()
                nc.vector.tensor_tensor_scan(g[0][:], R.decay[:], a[0][:], 0.0, ALU.mult, ALU.add)
                nc.vector.tensor_tensor_scan(g[1][:], R.decay[:], a[1][:], 0.0, ALU.mult, ALU.add).then_inc(scanned, 1)
                dve.drain()
                nc.vector.tensor_tensor(two(out[p][0]), two(g[0]), COS, ALU.mult)
                nc.vector.tensor_tensor(two(out[p][1]), two(g[1]), SIN, ALU.mult)
                nc.vector.tensor_tensor(two(out[p][2]), two(g[0]), SIN, ALU.mult).then_inc(states, 1)
                dve.wait_ge(y_ready, n + 1)
                nc.vector.tensor_tensor(hpair(R, n), hpair(R, n), y[p][0:HT, 0:PAIR], ALU.add)
                dve.drain()
                ln.stats(dve, n, p)
                dve.wait_ge(pool_out, n + 1)

            pipelined(dve, pro, body)

        @block.gpsimd
        def _(pool):
            def pair(n, p):
                pool.wait_ge(v_ready, n + 1)
                nc.gpsimd.tensor_tensor(two(m[3]), two(v[p][0]), SIN, ALU.mult).then_inc(pool_in, 1)
                pool.wait_ge(scanned, n + 1)
                nc.gpsimd.tensor_tensor(two(out[p][3]), two(g[1]), COS, ALU.mult).then_inc(pool_out, 1)
                ln.rstd(pool, n, p)

            pool.sem_inc(ln.rstd_done, 1)
            with pool.Fori(0, PAIRS // 2) as j:
                pair(2 * j, 0)
                pair(2 * j + 1, 1)

        @block.scalar
        def _(act):
            def front(n, q):
                act.wait_ge(u_ready, n + 1)
                nc.scalar.activation(v[q][0][:], u[0][:, 0:W], ACT.Identity, bias=R.lru[:, 2:3], scale=R.lru[:, 1:2])
                nc.scalar.activation(v[q][1][:], u[1][:, 0:W], ACT.Identity, bias=R.lru[:, 3:4], scale=R.lru[:, 1:2])\
                    .then_inc(v_ready, 1)

            def pro():
                head.act(act, 0, 0)
                front(0, 0)

            def body(n, p, more):
                if more:
                    head.act(act, n + 1, 1 - p)
                    front(n + 1, 1 - p)

            pipelined(act, pro, body)

        @block.tensor
        def _(pe):
            def front(n, q):
                pe.wait_ge(head.xT_ready, n + 1)
                wait_reuse(pe, v_ready, n)
                for i, w in enumerate(("B_reT", "B_imT")):
                    mm = nc.tensor.matmul(u[i][:, 0:W], R.c64(w, 0, D), head.xT[q][0:D, :], start=True, stop=True)
                mm.then_inc(u_ready, 1)

            def pro():
                head.pe(pe, 0, 0)
                front(0, 0)

            def body(n, p, more):
                if more:
                    head.pe(pe, n + 1, 1 - p)
                products_bias(nc, y[p][0:HT, 0:PAIR], R, R.c1("lru_b", 0, 1))
                for t in range(NT):
                    add(nc, y[p][0:HT, t * D:(t + 1) * D], head.xT[p][0:D, t * HT:(t + 1) * HT],
                        R.c64("DT", 0, D), stop=False)
                if more:
                    front(n + 1, 1 - p)
                pe.wait_ge(states, n + 1)
                pe.wait_ge(pool_out, n + 1)
                C = [R.c128("C_reT"), R.negC[:, 0:D], R.negC[:, D:2 * D], R.negC[:, D:2 * D]]
                for t in range(NT):
                    for k in range(4):
                        mm = add(nc, y[p][0:HT, t * D:(t + 1) * D], out[p][k][:, t * HT:(t + 1) * HT], C[k],
                                 stop=k == 3)
                mm.then_inc(y_ready, 1)

            pipelined(pe, pro, body)


def top1(nc, R):
    with ExitStack() as ctx:
        st = Stage(nc, ctx, "top1")
        ln, head = Norm(nc, st, R), Head(nc, st, R)
        NC = 4
        lg, ohT, y = st.bank("logits"), st.bank("chosenT"), st.bank("y")
        hb = [st.bank(f"hidden{c}") for c in range(NC)]
        hid = [st.sb(f"hid{c}", [128, W]) for c in range(NC)]
        top = st.sb("top", [128, NT])
        eq, oh = st.sb("eq", [128, NT * E1]), st.sb("chosen", [128, NT * E1])
        lg_ready, oh_ready, ohT_ready, aug = st.sem("lg_ready"), st.sem("oh_ready"), st.sem("ohT_ready"), st.sem("aug")
        h_ready, relu_act, relu_dve = st.sem("h_ready"), st.sem("relu_act"), st.sem("relu_dve")
        y_ready = st.sem("y_ready")
        block = ctx.enter_context(nc.Block())
        desc = split(R.c128("desc32", 0, HT), t=NT)

        @block.vector
        def _(dve):
            def choose(n):
                dve.wait_ge(lg_ready, n + 1)
                l4, e4 = split(lg[0:HT, 0:NT * E1], t=NT), split(eq[0:HT, :], t=NT)
                nc.vector.reduce_max(top[0:HT, :], l4, axis=AX_X)
                dve.drain()
                nc.vector.tensor_tensor(e4, l4, spread(top[0:HT, :], E1), ALU.is_equal)
                dve.drain()
                nc.vector.tensor_tensor(e4, e4, desc, ALU.mult)
                dve.drain()
                nc.vector.reduce_max(top[0:HT, :], e4, axis=AX_X)
                dve.drain()
                nc.vector.tensor_tensor(split(oh[0:HT, :], t=NT), e4, spread(top[0:HT, :], E1), ALU.is_equal)\
                    .then_inc(oh_ready, 1)

            def pro():
                head.dve(dve, 0, 0)
                choose(0)

            def body(n, p, more):
                if more:
                    head.dve(dve, n + 1, 1 - p)
                for c in (1, 3):
                    dve.wait_ge(h_ready, n * NC + c + 1)
                    nc.vector.tensor_scalar(hid[c][:], hb[c][:, 0:W], 0.0, None, ALU.max).then_inc(relu_dve, 1)
                if more:
                    choose(n + 1)
                dve.wait_ge(y_ready, n + 1)
                nc.vector.scalar_tensor_tensor(out=hpair(R, n), in0=y[0:HT, 0:PAIR], scalar=0.0, in1=hpair(R, n),
                                               op0=ALU.max, op1=ALU.add)
                dve.drain()
                ln.stats(dve, n, p)

            pipelined(dve, pro, body)

        @block.gpsimd
        def _(pool):
            ln.finish(pool)

        @block.scalar
        def _(act):
            def put(n, q):
                act.wait_ge(ohT_ready, n + 1)
                nc.scalar.copy(head.xT[q][D:D + E1, :], ohT[0:E1, 0:W]).then_inc(aug, 1)

            def pro():
                head.act(act, 0, 0)
                put(0, 0)

            def body(n, p, more):
                if more:
                    head.act(act, n + 1, 1 - p)
                for c in (0, 2):
                    act.wait_ge(h_ready, n * NC + c + 1)
                    nc.scalar.activation(hid[c][:], hb[c][:, 0:W], ACT.Relu).then_inc(relu_act, 1)
                if more:
                    put(n + 1, 1 - p)

            pipelined(act, pro, body)

        @block.tensor
        def _(pe):
            def logits(n, q):
                pe.wait_ge(head.xT_ready, n + 1)
                products_bias(nc, lg[0:HT, 0:NT * E1], R, R.c1("router_b", 0, 1))
                for t in range(NT):
                    mm = add(nc, lg[0:HT, t * E1:(t + 1) * E1], head.xT[q][0:D, t * HT:(t + 1) * HT],
                             R.c64("routerT", 0, D), stop=True)
                mm.then_inc(lg_ready, 1)

            def turn_choice(n):
                pe.wait_ge(oh_ready, n + 1)
                for t in range(NT):
                    mm = nc.tensor.transpose(ohT[0:E1, t * HT:(t + 1) * HT], oh[0:HT, t * E1:(t + 1) * E1],
                                             R.c128("ident", 0, HT, 0, HT))
                mm.then_inc(ohT_ready, 1)

            def pro():
                head.pe(pe, 0, 0)
                logits(0, 0)
                turn_choice(0)

            def body(n, p, more):
                if more:
                    head.pe(pe, n + 1, 1 - p)
                pe.wait_ge(aug, n + 1)
                for c in range(NC):
                    nc.tensor.matmul(hb[c][:, 0:W], R.w96("L0W1", 0, 96, c * 128, 128), head.xT[p][0:96, :],
                                     start=True, stop=True).then_inc(h_ready, 1)
                if more:
                    logits(n + 1, 1 - p)
                pe.wait_ge(relu_act, 2 * n + 2)
                pe.wait_ge(relu_dve, 2 * n + 2)
                for t in range(NT):
                    o = y[0:HT, t * D:(t + 1) * D]
                    for c in range(NC):
                        nc.tensor.matmul(o, hid[c][:, t * HT:(t + 1) * HT], R.c128("L0W2", 0, 128, c * D, D),
                                         start=c == 0, stop=False, skip_group_check=True)
                    mm = add(nc, o, head.xT[p][D:D + E1, t * HT:(t + 1) * HT], R.b2[D:D + E1, :], stop=True)
                mm.then_inc(y_ready, 1)
                if more:
                    turn_choice(n + 1)

            pipelined(pe, pro, body)


def mqa(nc, R, v_dram, ctx_dram):
    with ExitStack() as ctx:
        st = Stage(nc, ctx, "mqa")
        head = Head(nc, st, R)
        s = [st.bank(f"s{i}") for i in range(3)]
        pt = [st.bank(f"pt{i}") for i in range(2)]
        cx = [st.bank(f"cx{i}") for i in range(2)]
        kT = [st.sb(f"kT{p}", [128, W]) for p in range(2)]
        q = [[st.sb(f"q{i}{p}", [128, W]) for i in range(4)] for p in range(2)]
        vT = st.sb("vT", [64, W])
        v = [st.sb(f"v{p}", [128, 2, 2, KD]) for p in range(2)]
        prob = [st.sb(f"prob{i}", [128, 2 * T]) for i in range(2)]
        probT = [st.sb(f"probT{i}", [128, 2 * T]) for i in range(2)]
        mx = [st.sb(f"mx{i}", [128, 2]) for i in range(3)]
        negm = [st.sb(f"negm{i}", [128, 2]) for i in range(3)]
        sums = [st.sb(f"sums{i}", [128, NH]) for i in range(2)]
        inv = st.sb("inv", [128, NH])
        cxs = [st.sb(f"cxs{i}", [128, NH * KD]) for i in range(2)]
        f_ready, f_act, f_dve = st.sem("front_ready"), st.sem("front_act"), st.sem("front_dve")
        v_out, v_in = st.sem("v_out"), st.sem("v_in")
        s_ready, m_ready, e_ready = st.sem("s_ready"), st.sem("m_ready"), st.sem("e_ready")
        pt_ready, pts_ready, av_done = st.sem("pt_ready"), st.sem("pts_ready"), st.sem("av_done")
        cx_ready, cx_stored = st.sem("cx_ready"), [st.sem(f"cx_stored{i}") for i in range(2)]
        block = ctx.enter_context(nc.Block())
        UNITS, SCALE = 16, 1.0 / float(np.sqrt(np.float32(KD // NH)))
        heads = lambda hp: [hp // 2 * 4 + hp % 2, hp // 2 * 4 + hp % 2 + 2]
        fbank = [cx[0], cx[1], s[0], s[1], s[2], pt[0]]

        @block.tensor
        def _(pe):
            def front(n, p):
                pe.wait_ge(head.xT_ready, n + 1)
                wait_reuse(pe, cx_ready, NT * n)
                wait_reuse(pe, pts_ready, UNITS * n)
                for i in range(6):
                    if i == 1:
                        w, rows = R.c64("WvT", 0, D), KD
                    else:
                        w = R.c64("WkT2", 0, D) if i == 0 else R.c64("WqT", 0, D, (i - 2) * 128, 128)
                        rows = 128
                    nc.tensor.matmul(fbank[i][0:rows, 0:W], w, head.xT[p][0:D, :], start=True, stop=True)\
                        .then_inc(f_ready, 1)

            def scores(n, p, u):
                t, hp = u // 4, u % 4
                smp = t // 2
                if u >= 3:
                    pe.wait_ge(e_ready, UNITS * n + u - 2)
                rows = slice(hp % 2 * KD, (hp % 2 + 1) * KD)
                for k in range(2):
                    mm = nc.tensor.matmul(s[u % 3][0:HT, k * T:(k + 1) * T],
                                          q[p][heads(hp)[k] // 2][rows, t * HT:(t + 1) * HT],
                                          kT[p][rows, smp * T:(smp + 1) * T], start=True, stop=True)
                mm.then_inc(s_ready, 1)

            def turn(n, u):
                pe.wait_ge(e_ready, UNITS * n + u + 1)
                if u >= 2:
                    pe.wait_ge(pts_ready, UNITS * n + u - 1)
                for j in range(4):
                    mm = nc.tensor.transpose(pt[u % 2][0:HT, j * HT:(j + 1) * HT],
                                             prob[u % 2][0:HT, j * HT:(j + 1) * HT], R.c128("ident", 0, HT, 0, HT))
                mm.then_inc(pt_ready, 1)

            def values(n, p, u):
                t, hp = u // 4, u % 4
                smp = t // 2
                pe.wait_ge(pts_ready, UNITS * n + u + 1)
                if u == 0:
                    pe.wait_ge(v_in, 32 * (n + 1))
                if hp == 0 and t >= 2:
                    pe.wait_ge(cx_ready, NT * n + t - 1)
                for k in range(2):
                    for c in range(2):
                        o = heads(hp)[k] * KD
                        mm = nc.tensor.matmul(cx[t % 2][0:HT, o:o + KD],
                                              probT[u % 2][0:HT, (2 * k + c) * HT:(2 * k + c + 1) * HT],
                                              v[p][0:HT, smp, c, :], start=c == 0, stop=c == 1, skip_group_check=True)
                mm.then_inc(av_done, 1)

            def pro():
                head.pe(pe, 0, 0)
                front(0, 0)

            def body(n, p, more):
                if more:
                    head.pe(pe, n + 1, 1 - p)
                pe.wait_ge(f_act, 3 * (n + 1))
                pe.wait_ge(f_dve, 3 * (n + 1))
                scores(n, p, 0)
                scores(n, p, 1)
                for u in range(UNITS):
                    if u + 2 < UNITS:
                        scores(n, p, u + 2)
                    turn(n, u)
                    if u >= 1:
                        values(n, p, u - 1)
                values(n, p, UNITS - 1)
                if more:
                    front(n + 1, 1 - p)

            pipelined(pe, pro, body)

        @block.scalar
        def _(act):
            def front(n, p):
                for i, dst in ((0, kT[p]), (2, q[p][0]), (4, q[p][2])):
                    act.wait_ge(f_ready, 6 * n + i + 1)
                    nc.scalar.copy(dst[:], fbank[i][:, 0:W]).then_inc(f_act, 1)

            def exps(n, u):
                t, hp = u // 4, u % 4
                act.wait_ge(m_ready, UNITS * n + u + 1)
                if u >= 2:
                    act.wait_ge(pt_ready, UNITS * n + u - 1)
                if hp == 0 and t >= 2:
                    act.wait_ge(cx_ready, NT * n + t - 1)
                for k in range(2):
                    e = nc.scalar.activation(prob[u % 2][0:HT, k * T:(k + 1) * T], s[u % 3][0:HT, k * T:(k + 1) * T],
                                             ACT.Exp, bias=negm[u % 3][0:HT, k:k + 1], scale=SCALE,
                                             accum_out=sums[t % 2][0:HT, heads(hp)[k]:heads(hp)[k] + 1])
                e.then_inc(e_ready, 1)

            def pro():
                head.act(act, 0, 0)
                front(0, 0)

            def body(n, p, more):
                if more:
                    head.act(act, n + 1, 1 - p)
                for u in range(UNITS):
                    exps(n, u)
                if more:
                    front(n + 1, 1 - p)

            pipelined(act, pro, body)

        @block.vector
        def _(dve):
            def front(n, p):
                for i, dst, rows in ((1, vT, KD), (3, q[p][1], 128), (5, q[p][3], 128)):
                    dve.wait_ge(f_ready, 6 * n + i + 1)
                    if i == 1:
                        wait_reuse(dve, v_out, 16 * n)
                    nc.vector.tensor_copy(dst[0:rows, :], fbank[i][0:rows, 0:W]).then_inc(f_dve, 1)

            def maxima(n, u):
                dve.wait_ge(s_ready, UNITS * n + u + 1)
                nc.vector.reduce_max(mx[u % 3][0:HT, :], split(s[u % 3][0:HT, 0:W], t=2), axis=AX_X)
                dve.drain()
                nc.vector.tensor_scalar(negm[u % 3][0:HT, :], mx[u % 3][0:HT, :], -SCALE, None, ALU.mult)\
                    .then_inc(m_ready, 1)

            def take(n, u):
                dve.wait_ge(pt_ready, UNITS * n + u + 1)
                if u >= 2:
                    dve.wait_ge(av_done, UNITS * n + u - 1)
                nc.vector.tensor_copy(probT[u % 2][0:HT, :], pt[u % 2][0:HT, 0:W]).then_inc(pts_ready, 1)

            def context(n, t):
                dve.wait_ge(av_done, UNITS * n + 4 * t + 4)
                dve.wait_ge(cx_stored[t % 2], 16 * (2 * n + t // 2 + 1))
                nc.vector.reciprocal(inv[0:HT, :], sums[t % 2][0:HT, :])
                dve.drain()
                nc.vector.tensor_tensor(cxs[t % 2][0:HT, :].rearrange("p (h d) -> p h d", h=NH),
                                        cx[t % 2][0:HT, :].rearrange("p (h d) -> p h d", h=NH),
                                        spread(inv[0:HT, :], KD), ALU.mult).then_inc(cx_ready, 1)

            def pro():
                for stored in cx_stored:
                    dve.sem_inc(stored, 16)
                head.dve(dve, 0, 0)
                front(0, 0)

            def body(n, p, more):
                if more:
                    head.dve(dve, n + 1, 1 - p)
                maxima(n, 0)
                maxima(n, 1)
                for u in range(UNITS):
                    if u + 2 < UNITS:
                        maxima(n, u + 2)
                    take(n, u)
                    if u % 4 == 1 and u > 4:
                        context(n, u // 4 - 1)
                context(n, NT - 1)
                if more:
                    front(n + 1, 1 - p)

            pipelined(dve, pro, body)

        @block.sync
        def _(sp):
            def v_round(n, p):
                sp.wait_ge(f_dve, 3 * n + 1)
                sp.dma_start(v_dram[bass.ds(2 * n, 2)].rearrange("s (c t) -> c s t", c=KD),
                             split(vT[:], t=2)).then_inc(v_out, 16)
                sp.wait_ge(v_out, 16 * (n + 1))
                for smp in range(2):
                    sp.dma_start(v[p][0:HT, smp], v_dram[bass.ds(2 * n + smp, 1)]
                                 .rearrange("s (c t d) -> t (s c) d", c=2, d=KD)).then_inc(v_in, 16)

            def pro():
                v_round(0, 0)

            def body(n, p, more):
                for t in range(NT):
                    sp.wait_ge(cx_ready, NT * n + t + 1)
                    sp.dma_start(ctx_dram[bass.ds(2 * n + t // 2, 1), t % 2].rearrange("s t c -> (s t) c"),
                                 cxs[t % 2][0:HT, :]).then_inc(cx_stored[t % 2], 16)
                if more:
                    v_round(n + 1, 1 - p)

            pipelined(sp, pro, body)
            for stored in cx_stored:
                sp.wait_ge(stored, 16 * (2 * PAIRS + 1))


def mqa_out(nc, R, ctx_dram):
    with ExitStack() as ctx:
        st = Stage(nc, ctx, "mqao")
        ln = Norm(nc, st, R)
        y = [st.bank(f"y{p}") for p in range(2)]
        c = [st.sb(f"c{p}", [128, 2, 4, T]) for p in range(2)]
        loaded = [st.sem(f"loaded{p}") for p in range(2)]
        y_ready, y_used = st.sem("y_ready"), st.sem("y_used")
        block = ctx.enter_context(nc.Block())

        @block.sync
        def _(sp):
            def load(n, p):
                sp.wait_ge(y_ready, n + 1)
                for smp in range(2):
                    sp.dma_start(c[p][:, smp], ctx_dram[bass.ds(2 * n + smp, 1)]
                                 .rearrange("s two t c -> s (two t c)")
                                 .rearrange("s (c p t) -> p (s c) t", p=128, t=T)).then_inc(loaded[p], 16)

            with sp.Fori(0, PAIRS // 2) as j:
                load(2 * j, 0)
                load(2 * j + 1, 1)

        @block.tensor
        def _(pe):
            def pair(n, p, turn):
                pe.wait_ge(loaded[p], 32 * turn)
                pe.wait_ge(y_used, n + 1)
                for t in range(NT):
                    for k in range(4):
                        mm = nc.tensor.matmul(y[p][0:HT, t * D:(t + 1) * D],
                                              c[p][:, t // 2, k, (t % 2) * HT:(t % 2 + 1) * HT],
                                              R.c128("WoT", 0, 128, k * D, D), start=k == 0, stop=k == 3,
                                              skip_group_check=True)
                mm.then_inc(y_ready, 1)

            with pe.Fori(0, PAIRS // 2) as j:
                pair(2 * j, 0, j + 1)
                pair(2 * j + 1, 1, j + 1)

        @block.vector
        def _(dve):
            dve.sem_inc(y_used, 2)
            dve.sem_inc(y_ready, 2)

            def pair(n, p):
                dve.wait_ge(y_ready, n + 3)
                nc.vector.tensor_tensor(hpair(R, n), hpair(R, n), y[p][0:HT, 0:PAIR], ALU.add).then_inc(y_used, 1)
                dve.drain()
                ln.stats(dve, n, p)

            with dve.Fori(0, PAIRS // 2) as j:
                pair(2 * j, 0)
                pair(2 * j + 1, 1)

        @block.gpsimd
        def _(pool):
            ln.finish(pool)


def top2_route(nc, R, name, gate, biases, own_norm):
    with ExitStack() as ctx:
        st = Stage(nc, ctx, name)
        xn = [st.sb(f"xn{p}", [128, PAIR]) for p in range(2)]
        xi = [st.sb(f"xi{p}", [128, PAIR]) for p in range(2)]
        turned = [st.bank(f"turned{p}") for p in range(2)]
        lg = [st.bank(f"logits{p}") for p in range(2)]
        xT = [st.sb(f"xT{p}", [64, W]) for p in range(2)]
        s4, sq, var, rs = (st.sb("s4", [128, NT]), st.sb("sq", [128, PAIR]), st.sb("var", [128, NT]),
                           st.sb("rs", [128, NT]))
        ALL = PAIRS * NT
        lga, eq, o1, o2 = (st.sb(k, [128, ALL * E2]) for k in ("all", "eq", "first", "second"))
        m1, m2, kk, dl, ex, w1, w2 = (st.sb(k, [128, ALL]) for k in ("m1", "m2", "kk", "dl", "ex", "w1", "w2"))
        x_ready, turned_ready, xT_ready = st.sem("x_ready"), st.sem("turned_ready"), st.sem("xT_ready")
        lg_ready, lg_used, var_ready, rs_ready = (st.sem(k) for k in ("lg_ready", "lg_used", "var_ready", "rs_ready"))
        diff_ready, exp_ready = st.sem("diff_ready"), st.sem("exp_ready")
        block = ctx.enter_context(nc.Block())
        src = xi if own_norm else xn

        @block.vector
        def _(dve):
            def make(n, p):
                wait_reuse(dve, turned_ready, n)
                ins = normalise(nc, R, n, xn[p][0:HT, :])
                if not own_norm:
                    ins.then_inc(x_ready, 1)
                    return
                x4 = split(xn[p][0:HT, :], t=NT)
                dve.drain()
                nc.vector.reduce_sum(s4[0:HT, :], x4, axis=AX_X)
                dve.drain()
                nc.vector.scalar_tensor_tensor(out=x4, in0=spread(s4[0:HT, :], D), scalar=-1.0 / D, in1=x4,
                                               op0=ALU.mult, op1=ALU.add)
                dve.drain()
                nc.vector.tensor_tensor(sq[0:HT, :], xn[p][0:HT, :], xn[p][0:HT, :], ALU.mult)
                dve.drain()
                nc.vector.reduce_sum(s4[0:HT, :], split(sq[0:HT, :], t=NT), axis=AX_X)
                dve.drain()
                nc.vector.tensor_scalar(var[0:HT, :], s4[0:HT, :], 1.0 / D, EPS, ALU.mult, ALU.add)\
                    .then_inc(var_ready, 1)
                dve.wait_ge(rs_ready, n + 1)
                nc.vector.tensor_tensor(split(xi[p][0:HT, :], t=NT), x4, spread(rs[0:HT, :], D), ALU.mult)\
                    .then_inc(x_ready, 1)

            def keep(n, p):
                dve.wait_ge(lg_ready, n + 1)
                nc.vector.tensor_copy(lga[0:HT, bass.ds(n * NT * E2, NT * E2)], lg[p][0:HT, 0:NT * E2])\
                    .then_inc(lg_used, 1)

            dve.sem_inc(lg_used, 2)

            def pro():
                make(0, 0)

            def body(n, p, more):
                if more:
                    make(n + 1, 1 - p)
                keep(n, p)

            pipelined(dve, pro, body)
            dve.drain()

            l3, e3 = (split(t[0:HT, :], e=E2) for t in (lga, eq))
            desc = split(R.c128("desc8", 0, HT), e=E2)

            def first_of_highest(src, top, out):
                nc.vector.reduce_max(top[0:HT, :], src, axis=AX_X)
                dve.drain()
                nc.vector.tensor_tensor(e3, src, spread(top[0:HT, :], E2), ALU.is_equal)
                dve.drain()
                nc.vector.tensor_tensor(e3, e3, desc, ALU.mult)
                dve.drain()
                nc.vector.reduce_max(kk[0:HT, :], e3, axis=AX_X)
                dve.drain()
                nc.vector.tensor_tensor(out, e3, spread(kk[0:HT, :], E2), ALU.is_equal)
                dve.drain()

            first, second = (split(t[0:HT, :], e=E2) for t in (o1, o2))
            first_of_highest(l3, m1, first)
            nc.vector.scalar_tensor_tensor(out=l3, in0=first, scalar=LOWEST, in1=l3, op0=ALU.mult, op1=ALU.add)
            dve.drain()
            first_of_highest(l3, m2, second)
            nc.vector.tensor_tensor(dl[0:HT, :], m2[0:HT, :], m1[0:HT, :], ALU.subtract).then_inc(diff_ready, 1)
            dve.wait_ge(exp_ready, 1)
            nc.vector.tensor_scalar(w2[0:HT, :], ex[0:HT, :], 1.0, None, ALU.add)
            dve.drain()
            nc.vector.reciprocal(w1[0:HT, :], w2[0:HT, :])
            dve.drain()
            nc.vector.tensor_tensor(w2[0:HT, :], ex[0:HT, :], w1[0:HT, :], ALU.mult)
            nc.vector.tensor_tensor(first, first, spread(w1[0:HT, :], E2), ALU.mult)
            dve.drain()
            nc.vector.tensor_tensor(second, second, spread(w2[0:HT, :], E2), ALU.mult)
            dve.drain()
            nc.vector.tensor_tensor(split(R.gates[0:HT, :], e=E2), first, second, ALU.add)

        @block.gpsimd
        def _(pool):
            if own_norm:
                with pool.Fori(0, PAIRS) as n:
                    pool.wait_ge(var_ready, n + 1)
                    nc.gpsimd.tensor_tensor(rs[0:HT, :], var[0:HT, :], R.neghalf[0:HT, 0:NT], ALU.pow)\
                        .then_inc(rs_ready, 1)

        @block.scalar
        def _(act):
            def put(n, p):
                act.wait_ge(turned_ready, n + 1)
                for half in range(2):
                    out, in_ = half_columns(xT[p][:], turned[p], half)
                    if own_norm:
                        nc.scalar.activation(out, in_, ACT.Identity, bias=R.c64("beta", 0, D),
                                             scale=R.c64("gamma", 0, D))
                    else:
                        nc.scalar.copy(out, in_)
                act.drain()
                nc.scalar.copy(R.xT[:, bass.ds(n * W, W)], xT[p][:]).then_inc(xT_ready, 1)

            with act.Fori(0, PAIRS // 2) as j:
                put(2 * j, 0)
                put(2 * j + 1, 1)
            act.wait_ge(diff_ready, 1)
            nc.scalar.activation(ex[0:HT, :], dl[0:HT, :], ACT.Exp).then_inc(exp_ready, 1)

        @block.tensor
        def _(pe):
            def turn(n, p):
                pe.wait_ge(x_ready, n + 1)
                turn_pair(nc, R, turned[p], src[p]).then_inc(turned_ready, 1)

            def logits(n, p):
                pe.wait_ge(xT_ready, n + 1)
                pe.wait_ge(lg_used, n + 1)
                products_bias(nc, lg[p][0:HT, 0:NT * E2], R, R.c1(biases[0], 0, 1))
                for b in biases[1:]:
                    add(nc, lg[p][0:HT, 0:NT * E2], R.ones[0:1, 0:HT], R.c1(b, 0, 1), stop=False)
                for t in range(NT):
                    mm = add(nc, lg[p][0:HT, t * E2:(t + 1) * E2], xT[p][:, t * HT:(t + 1) * HT],
                             R.c64(gate, 0, D), stop=True)
                mm.then_inc(lg_ready, 1)

            def pro():
                turn(0, 0)

            def body(n, p, more):
                if more:
                    turn(n + 1, 1 - p)
                logits(n, p)

            pipelined(pe, pro, body)


def top2(nc, R, name, w1, b1, w2, b2, func):
    with ExitStack() as ctx:
        st = Stage(nc, ctx, name)
        ln = Norm(nc, st, R)
        NB, NY = 4, 3
        hb = [st.bank(f"hidden{i}") for i in range(NB)]
        y = [st.bank(f"y{i}") for i in range(NY)]
        hid = [[st.sb(f"hid{e}{p}", [128, W]) for e in range(E2)] for p in range(2)]
        gated = [st.sb(f"gated{i}", [128, E2 * D]) for i in range(2)]
        acc = st.sb("acc", [128, PAIR])
        h_ready, h_used, y_ready, y_used = (st.sem(k) for k in ("h_ready", "h_used", "y_ready", "y_used"))
        block = ctx.enter_context(nc.Block())

        @block.tensor
        def _(pe):
            def front(n, p):
                for e in range(E2):
                    pe.wait_ge(h_used, n * E2 + e + 1)
                    pe.nop(nofuse=True)
                    nc.tensor.matmul(hb[e % NB][:, 0:W], R.c64(w1, 0, D, e * H2, H2), R.xT[:, bass.ds(n * W, W)],
                                     start=True, stop=True).then_inc(h_ready, 1)

            def body(n, p, more):
                pe.wait_ge(h_used, (n + 1) * E2 + NB)
                for t in range(NT):
                    pe.wait_ge(y_used, n * NT + (t - NY + 2 if t >= NY else 1))
                    products_bias(nc, y[t % NY][0:HT, :], R, R.c1(b2, 0, 1))
                    for e in range(E2):
                        mm = add(nc, y[t % NY][0:HT, e * D:(e + 1) * D], hid[p][e][:, t * HT:(t + 1) * HT],
                                 R.c128(w2, 0, 128, e * D, D), stop=True)
                    mm.then_inc(y_ready, 1)
                if more:
                    front(n + 1, 1 - p)

            pipelined(pe, lambda: front(0, 0), body)

        @block.scalar
        def _(act):
            act.sem_inc(h_used, NB)

            def front(n, p):
                for e in range(E2):
                    act.wait_ge(h_ready, n * E2 + e + 1)
                    nc.scalar.activation(hid[p][e][:], hb[e % NB][:, 0:W], func, bias=R.c128(b1, 0, 128, e, 1))\
                        .then_inc(h_used, 1)

            def body(n, p, more):
                if more:
                    front(n + 1, 1 - p)

            pipelined(act, lambda: front(0, 0), body)

        @block.vector
        def _(dve):
            def body(n, p, more):
                for t in range(NT):
                    dve.wait_ge(y_ready, n * NT + t + 1)
                    nc.vector.tensor_tensor(gated[t % 2][0:HT, :].rearrange("p (e d) -> p e d", e=E2),
                                            y[t % NY][0:HT, :].rearrange("p (e d) -> p e d", e=E2),
                                            spread(R.gates[0:HT, bass.ds(n * NT * E2 + t * E2, E2)], D), ALU.mult)\
                        .then_inc(y_used, 1)
                    dve.drain()
                    nc.vector.reduce_sum(acc[0:HT, t * D:(t + 1) * D],
                                         gated[t % 2][0:HT, :].rearrange("p (e d) -> p d e", e=E2), axis=AX_X)
                dve.drain()
                nc.vector.tensor_tensor(hpair(R, n), hpair(R, n), acc[0:HT, :], ALU.add)
                dve.drain()
                ln.stats(dve, n, p)

            pipelined(dve, lambda: dve.sem_inc(y_used, 1), body)

        @block.gpsimd
        def _(pool):
            ln.finish(pool)


def quadratic(nc, R):
    with ExitStack() as ctx:
        st = Stage(nc, ctx, "quad")
        ln, head = Norm(nc, st, R), Head(nc, st, R, dup=True)
        fb = [st.bank(f"f{i}") for i in range(2)]
        ob = [st.bank(f"o{i}") for i in range(4)]
        r = st.bank("r")
        q = [st.sb(f"q{i}", [128, W]) for i in range(4)]
        es = [st.sb(f"es{t}", [128, NH * D]) for t in range(NT)]
        om = [[st.sb(f"om{s}{i}", [128, W]) for i in range(6)] for s in range(2)]
        f_ready, f_done, o_ready, o_done, r_ready = (st.sem(k) for k in ("f_ready", "f_done", "o_ready", "o_done",
                                                                         "r_ready"))
        block = ctx.enter_context(nc.Block())
        F = 8
        U = 12

        @block.tensor
        def _(pe):
            def front(n, p):
                pe.wait_ge(head.xT_ready, n + 1)
                for i in range(F):
                    pe.wait_ge(f_done, n * F + i + 1)
                    if i < 4:
                        mm = nc.tensor.matmul(fb[i % 2][:, 0:W], R.c64("Q", 0, D, i * 128, 128), head.xT[p][0:D, :],
                                              start=True, stop=True)
                    else:
                        t = i - 4
                        mm = nc.tensor.matmul(fb[i % 2][0:HT, :], head.xT[p][0:D, t * HT:(t + 1) * HT],
                                              R.c64("ET", 0, D), start=True, stop=True)
                    mm.then_inc(f_ready, 1)

            def omega(n, p, smp):
                for i in range(6):
                    u = smp * 6 + i
                    pe.wait_ge(o_done, n * U + u + 1)
                    bank = ob[u % 4]
                    cols = T if i < 4 else HT
                    tile = 2 * smp if i < 4 else 2 * smp + 1
                    for k in range(2 if i < 4 else 4):
                        h = i // 2 * 4 + i % 2 + 2 * k if i < 4 else i - 4 + 2 * k
                        rows = slice((h % 2) * D, (h % 2 + 1) * D)
                        t0 = smp * T + (0 if i < 4 else HT)
                        mm = nc.tensor.matmul(bank[0:HT, k * cols:(k + 1) * cols],
                                              head.xT[p][rows, tile * HT:(tile + 1) * HT],
                                              q[h // 2][rows, t0:t0 + cols], start=True, stop=True)
                    mm.then_inc(o_ready, 1)

            def result(n, p, smp):
                pe.wait_ge(o_done, n * U + smp * 6 + 6 + 4)
                for half in range(2):
                    t = 2 * smp + half
                    terms = [(om[smp][h // 4 * 2 + h % 2], (h % 4 // 2) * T + half * HT, 2 * smp, h)
                             for h in range(NH)]
                    if half:
                        terms += [(om[smp][4 + h % 2], (h // 2) * HT, 2 * smp + 1, h) for h in range(NH)]
                    for i, (o, c, tile, h) in enumerate(terms):
                        mm = nc.tensor.matmul(r[0:HT, t * D:(t + 1) * D], o[0:HT, c:c + HT],
                                              es[tile][0:HT, h * D:(h + 1) * D], start=i == 0,
                                              stop=i == len(terms) - 1, skip_group_check=True)
                mm.then_inc(r_ready, 1)

            def pro():
                head.pe(pe, 0, 0)
                front(0, 0)

            def body(n, p, more):
                if more:
                    head.pe(pe, n + 1, 1 - p)
                pe.wait_ge(f_done, (n + 1) * F + 2)
                omega(n, p, 0)
                omega(n, p, 1)
                result(n, p, 0)
                result(n, p, 1)
                if more:
                    front(n + 1, 1 - p)

            pipelined(pe, pro, body)

        @block.scalar
        def _(act):
            act.sem_inc(f_done, 2)

            def front(n, p):
                for i in range(F):
                    act.wait_ge(f_ready, n * F + i + 1)
                    if i < 4:
                        nc.scalar.copy(q[i][:], fb[i % 2][:, 0:W]).then_inc(f_done, 1)
                    else:
                        nc.scalar.copy(es[i - 4][0:HT, :], fb[i % 2][0:HT, :]).then_inc(f_done, 1)

            def pro():
                head.act(act, 0, 0)
                front(0, 0)

            def body(n, p, more):
                if more:
                    head.act(act, n + 1, 1 - p)
                    front(n + 1, 1 - p)

            pipelined(act, pro, body)

        @block.vector
        def _(dve):
            dve.sem_inc(o_done, 4)
            causal = R.c128("causal", 0, HT)

            def body(n, p, more):
                if more:
                    head.dve(dve, n + 1, 1 - p)
                for smp in range(2):
                    for i in range(6):
                        u = smp * 6 + i
                        dve.wait_ge(o_ready, n * U + u + 1)
                        k, cols = (2, T) if i < 4 else (4, HT)
                        mask = causal[:, 0:cols].unsqueeze(1).to_broadcast([HT, k, cols])
                        nc.vector.tensor_tensor(split(om[smp][i][0:HT, :], t=k), split(ob[u % 4][0:HT, 0:W], t=k),
                                                mask, ALU.mult).then_inc(o_done, 1)
                dve.wait_ge(r_ready, 2 * n + 2)
                nc.vector.tensor_tensor(hpair(R, n), hpair(R, n), r[0:HT, 0:PAIR], ALU.add)
                dve.drain()
                ln.stats(dve, n, p)

            pipelined(dve, lambda: head.dve(dve, 0, 0), body)

        @block.gpsimd
        def _(pool):
            ln.finish(pool)


def sigmoid_attention(nc, R):
    with ExitStack() as ctx:
        st = Stage(nc, ctx, "sig")
        ln, head = Norm(nc, st, R), Head(nc, st, R)
        qb, y = st.bank("q"), st.bank("y")
        ab = [st.bank(f"a{i}") for i in range(2)]
        q = [st.sb(f"q{p}", [64, W]) for p in range(2)]
        att = [st.sb(f"att{i}", [128, W]) for i in range(2)]
        q_ready, q_done, a_ready, a_done, y_ready, y_used = (
            st.sem(k) for k in ("q_ready", "q_done", "a_ready", "a_done", "y_ready", "y_used"))
        block = ctx.enter_context(nc.Block())

        @block.tensor
        def _(pe):
            def front(n, p):
                pe.wait_ge(head.xT_ready, n + 1)
                wait_reuse(pe, q_done, n)
                nc.tensor.matmul(qb[:, 0:W], R.c64("qw2", 0, D), head.xT[p][0:D, :], start=True, stop=True)\
                    .then_inc(q_ready, 1)

            def scores(n, p, smp):
                for i in range(2):
                    tile = 2 * smp + i
                    mm = nc.tensor.matmul(ab[smp][0:HT, i * T:(i + 1) * T], head.xT[p][0:D, tile * HT:(tile + 1) * HT],
                                          q[p][:, smp * T:(smp + 1) * T], start=True, stop=True)
                mm.then_inc(a_ready, 1)

            def values(n, p, smp):
                pe.wait_ge(a_done, 2 * n + smp + 1)
                for half in range(2):
                    for i in range(2):
                        o = (2 * smp + half) * D
                        mm = nc.tensor.matmul(y[0:HT, o:o + D], att[smp][0:HT, i * T + half * HT:i * T + half * HT + HT],
                                              head.xn[p][0:HT, (2 * smp + i) * D:(2 * smp + i + 1) * D],
                                              start=i == 0, stop=i == 1, skip_group_check=True)
                if smp:
                    mm.then_inc(y_ready, 1)

            def pro():
                head.pe(pe, 0, 0)
                front(0, 0)

            def body(n, p, more):
                if more:
                    head.pe(pe, n + 1, 1 - p)
                pe.wait_ge(q_done, n + 1)
                scores(n, p, 0)
                scores(n, p, 1)
                if more:
                    front(n + 1, 1 - p)
                pe.wait_ge(y_used, n + 1)
                values(n, p, 0)
                values(n, p, 1)

            pipelined(pe, pro, body)

        @block.scalar
        def _(act):
            def front(n, p):
                act.wait_ge(q_ready, n + 1)
                nc.scalar.copy(q[p][:], qb[0:D, 0:W]).then_inc(q_done, 1)

            def pro():
                head.act(act, 0, 0)
                front(0, 0)

            def body(n, p, more):
                if more:
                    head.act(act, n + 1, 1 - p)
                for smp in range(2):
                    act.wait_ge(a_ready, 2 * n + smp + 1)
                    nc.scalar.activation(att[smp][0:HT, :], ab[smp][0:HT, 0:W], ACT.Sigmoid).then_inc(a_done, 1)
                if more:
                    front(n + 1, 1 - p)

            pipelined(act, pro, body)

        @block.vector
        def _(dve):
            def body(n, p, more):
                if more:
                    head.dve(dve, n + 1, 1 - p)
                dve.wait_ge(y_ready, n + 1)
                nc.vector.tensor_tensor(hpair(R, n), hpair(R, n), y[0:HT, 0:PAIR], ALU.add).then_inc(y_used, 1)
                dve.drain()
                ln.stats(dve, n, p)

            dve.sem_inc(y_used, 1)
            pipelined(dve, lambda: head.dve(dve, 0, 0), body)

        @block.gpsimd
        def _(pool):
            ln.finish(pool)


def depths(nc, R, out):
    with ExitStack() as ctx:
        st = Stage(nc, ctx, "mod")
        head = Head(nc, st, R)
        wb = st.bank("weights")
        hb = [st.bank(f"hidden{i}") for i in range(2)]
        y = [st.bank(f"y{p}") for p in range(2)]
        hid = [st.sb(f"hid{i}", [128, W]) for i in range(2)]
        wrow, diag = st.sb("wrow", [128, W]), st.sb("diag", [128, W])
        scr = [st.sb(f"scr{i}", [128, T]) for i in range(2)]
        wcol, hi, ties, rank, f = (st.sb(k, [128, NT]) for k in ("wcol", "higher", "ties", "rank", "factor"))
        o = [st.sb(f"o{p}", [128, PAIR]) for p in range(2)]
        w_ready, w_used, h_ready, h_done, y_ready, o_ready = (
            st.sem(k) for k in ("w_ready", "w_used", "h_ready", "h_done", "y_ready", "o_ready"))
        stored = [st.sem(f"stored{p}") for p in range(2)]
        block = ctx.enter_context(nc.Block())

        @block.tensor
        def _(pe):
            def front(n, p):
                pe.wait_ge(head.xT_ready, n + 1)
                wait_reuse(pe, w_used, n)
                nc.tensor.matmul(wb[0:HT, 0:W], R.c64("wr_rep", 0, D), head.xT[p][0:D, :], start=True, stop=False)
                nc.tensor.matmul(wb[0:HT, 0:W], R.c1("L3br", 0, 1, 0, HT), R.ones[0:1, 0:W], start=False, stop=True)\
                    .then_inc(w_ready, 1)
                wait_reuse(pe, h_done, 2 * n)
                for i in range(2):
                    nc.tensor.matmul(hb[i][:, 0:W], R.c64("L3w1", 0, D, i * 128, 128), head.xT[p][0:D, :],
                                     start=True, stop=True).then_inc(h_ready, 1)

            def pro():
                head.pe(pe, 0, 0)
                front(0, 0)

            def body(n, p, more):
                if more:
                    head.pe(pe, n + 1, 1 - p)
                pe.wait_ge(h_done, 2 * n + 2)
                products_bias(nc, y[p][0:HT, 0:PAIR], R, R.c1("L3b2", 0, 1))
                for t in range(NT):
                    for i in range(2):
                        mm = add(nc, y[p][0:HT, t * D:(t + 1) * D], hid[i][:, t * HT:(t + 1) * HT],
                                 R.c128("L3w2", 0, 128, i * D, D), stop=i == 1)
                mm.then_inc(y_ready, 1)
                if more:
                    front(n + 1, 1 - p)

            pipelined(pe, pro, body)

        @block.scalar
        def _(act):
            def front(n, p):
                act.wait_ge(w_ready, n + 1)
                if not isinstance(n, int) or n > 0:
                    act.wait_ge(o_ready, n)
                nc.scalar.copy(wrow[0:HT, :], wb[0:HT, 0:W]).then_inc(w_used, 1)
                for i in range(2):
                    act.wait_ge(h_ready, 2 * n + i + 1)
                    nc.scalar.activation(hid[i][:], hb[i][:, 0:W], ACT.Gelu_apprx_tanh,
                                         bias=R.c128("L3b1", 0, 128, i, 1)).then_inc(h_done, 1)

            def pro():
                head.act(act, 0, 0)
                front(0, 0)

            def body(n, p, more):
                if more:
                    head.act(act, n + 1, 1 - p)
                    front(n + 1, 1 - p)

            pipelined(act, pro, body)

        @block.vector
        def _(dve):
            def body(n, p, more):
                if more:
                    head.dve(dve, n + 1, 1 - p)
                dve.wait_ge(w_used, n + 1)
                ident = R.c128("ident", 0, HT, 0, HT).unsqueeze(1).to_broadcast([HT, NT, HT])
                nc.vector.tensor_tensor(split(diag[0:HT, :], t=NT), split(wrow[0:HT, :], t=NT), ident, ALU.mult)
                dve.drain()
                nc.vector.reduce_sum(wcol[0:HT, :], split(diag[0:HT, :], t=NT), axis=AX_X)
                dve.drain()
                for t in range(NT):
                    row = wrow[0:HT, (t // 2) * T:(t // 2 + 1) * T]
                    nc.vector.tensor_scalar(scr[0][0:HT, :], row, wcol[0:HT, t:t + 1], None, ALU.is_gt, ALU.add,
                                            accum_out=hi[0:HT, t:t + 1])
                    nc.vector.scalar_tensor_tensor(out=scr[1][0:HT, :], in0=row, scalar=wcol[0:HT, t:t + 1],
                                                   in1=R.c128("earlier", 0, HT, (t % 2) * T, T), op0=ALU.is_equal,
                                                   op1=ALU.mult, accum_out=ties[0:HT, t:t + 1])
                    dve.drain()
                nc.vector.tensor_tensor(rank[0:HT, :], hi[0:HT, :], ties[0:HT, :], ALU.add)
                dve.drain()
                nc.vector.scalar_tensor_tensor(out=f[0:HT, :], in0=rank[0:HT, :], scalar=float(KEEP),
                                               in1=wcol[0:HT, :], op0=ALU.is_lt, op1=ALU.mult)
                dve.drain()
                dve.wait_ge(stored[p], 8 * (n - p) + 16)
                dve.wait_ge(y_ready, n + 1)
                nc.vector.tensor_tensor(split(o[p][0:HT, :], t=NT), split(y[p][0:HT, 0:PAIR], t=NT),
                                        spread(f[0:HT, :], D), ALU.mult)
                dve.drain()
                nc.vector.tensor_tensor(o[p][0:HT, :], o[p][0:HT, :], head.xn[p][0:HT, :], ALU.add)
                dve.drain()
                nc.vector.tensor_tensor(o[p][0:HT, :], o[p][0:HT, :], hpair(R, n), ALU.add).then_inc(o_ready, 1)

            for s in stored:
                dve.sem_inc(s, 16)
            pipelined(dve, lambda: head.dve(dve, 0, 0), body)

        @block.sync
        def _(sp):
            def store(n, p):
                sp.wait_ge(o_ready, n + 1)
                sp.dma_start(out[bass.ds(2 * n, 2)].rearrange("s (two t) d -> t (s two) d", two=2),
                             split(o[p][0:HT, :], t=NT)).then_inc(stored[p], 16)

            with sp.Fori(0, PAIRS // 2) as j:
                store(2 * j, 0)
                store(2 * j + 1, 1)
            for s in stored:
                sp.wait_ge(s, 16 * (PAIRS // 2) + 16)


class Resident:
    pass


def fusion_kernel(nc, x, txt, p64, p128, p1, p96, b2, out):
    with ExitStack() as ctx:
        st = Stage(nc, ctx, "all")
        R = Resident()
        R.h, R.hc = st.sb("h", [128, PAIRS * PAIR]), st.sb("centred", [128, PAIRS * PAIR])
        R.rstd = st.sb("rstd", [128, PAIRS * NT])
        R.neghalf, R.half, R.euler = st.sb("neghalf", [128, NT]), st.sb("half", [128, 1]), st.sb("euler", [128, 1])
        R.ones = st.sb("ones", [1, W])
        R.lru = st.sb("lru_consts", [128, 4])
        R.cos, R.sin, R.decay = st.sb("cos", [128, T]), st.sb("sin", [128, T]), st.sb("decay", [128, W])
        R.negC = st.sb("negC", [128, 2 * D])
        R.gates = st.sb("gates", [128, PAIRS * NT * E2])
        R.xT = st.sb("xT", [64, PAIRS * W])
        t64, t128 = st.sb("p64", [64, offsets(PACK64)[1]]), st.sb("p128", [128, offsets(PACK128)[1]])
        t1, t96 = st.sb("p1", [1, offsets(PACK1)[1]]), st.sb("p96", [96, offsets(PACK96)[1]])
        R.b2 = st.sb("top1_b2", [96, D])
        R.c64, R.c128, R.c1, R.w96 = Named(t64, PACK64), Named(t128, PACK128), Named(t1, PACK1), Named(t96, PACK96)
        v_dram = nc.dram_tensor("v_scratch", [B, KD * T], F32).ap()
        ctx_dram = nc.dram_tensor("ctx_scratch", [B, 2, HT, NH * KD], F32).ap()

        loads = [(t128[:], p128), (t1[:], p1), (t64[:], p64), (t96[:], p96), (R.b2[D:D + E1, :], b2)]
        tokenizer(nc, R, x, txt, loads)
        lru(nc, R)
        top1(nc, R)
        mqa(nc, R, v_dram, ctx_dram)
        mqa_out(nc, R, ctx_dram)
        top2_route(nc, R, "rg", "L1WrT", ["L1br"], own_norm=True)
        top2(nc, R, "gelu2", "L1W1", "L1b1", "L1W2", "L1b2", ACT.Gelu)
        quadratic(nc, R)
        top2_route(nc, R, "rr", "L2WgT", ["L2bg", "L2bias"], own_norm=False)
        top2(nc, R, "relu2", "L2W1", "L2b1", "L2W2", "L2b2", ACT.Relu)
        sigmoid_attention(nc, R)
        depths(nc, R, out)


def pack(spec, parts, rows):
    for name, n in spec:
        assert parts[name].shape == (rows, n), (name, parts[name].shape, n)
    return np.ascontiguousarray(np.concatenate([parts[name] for name, _ in spec], axis=1))


def laid_out(i):
    f = np.float32
    rep = lambda v, n: np.tile(v.reshape(1, -1), (1, n))
    experts_in = lambda w: w.transpose(1, 0, 2).reshape(w.shape[1], -1)
    x = i["x"].reshape(PAIRS, 2, D, XM, 2).transpose(0, 4, 2, 1, 3).reshape(PAIRS, 128, 2, XM)
    w = i["L0_tok_weight"].reshape(D, 25, D)
    w = np.concatenate([w, np.zeros((D, 1, D), f)], axis=1).reshape(D, KPAR, 2, D)
    tokw = w.transpose(2, 0, 1, 3).reshape(128, KPAR * D)
    p64 = {"B_reT": i["L0_attn_B_re"].T, "B_imT": i["L0_attn_B_im"].T, "DT": i["L0_attn_D"].T,
           "routerT": i["L0_ffn_router_w"].T, "WqT": i["L1_attn_Wq"].T,
           "WkT2": np.concatenate([i["L1_attn_Wk"].T] * 2, axis=1), "WvT": i["L1_attn_Wv"].T,
           "L1WrT": i["L1_ffn_Wr"], "L1W1": experts_in(i["L1_ffn_W1"]), "gamma": i["L1_ffn_gamma"][:, None],
           "beta": i["L1_ffn_beta"][:, None], "Q": experts_in(i["L2_attn_Q"]),
           "ET": i["L2_attn_E"].transpose(2, 0, 1).reshape(D, -1), "L2WgT": i["L2_ffn_Wg"],
           "L2W1": experts_in(i["L2_ffn_W1"]), "qw2": np.tile(i["L3_attn_q_weight"], (1, 2)),
           "wr_rep": np.tile(i["L3_ffn_wr"], (1, HT)), "L3w1": i["L3_ffn_w1"]}
    chunks = lambda w: w.reshape(-1, 128, D).transpose(1, 0, 2).reshape(128, -1)
    part = np.arange(128)[:, None]
    cols = np.arange(T)[None, :]
    p128 = {"tokw": tokw, "C_reT": i["L0_attn_C_re"].T, "C_imT": i["L0_attn_C_im"].T,
            "nu_log": i["L0_attn_nu_log"][:, None], "theta_log": i["L0_attn_theta_log"][:, None],
            "bh_re": i["L0_attn_bh_re"][:, None], "bh_im": i["L0_attn_bh_im"][:, None],
            "L0W2": chunks(i["L0_ffn_W2"].reshape(E1 * H1, D)), "WoT": chunks(np.ascontiguousarray(i["L1_attn_Wo"].T)),
            "L1W2": chunks(i["L1_ffn_W2"].reshape(-1, D)), "L1b1": i["L1_ffn_b1"].T,
            "L2W2": chunks(i["L2_ffn_W2"].reshape(-1, D)), "L2b1": i["L2_ffn_b1"].T,
            "L3w2": chunks(i["L3_ffn_w2"]), "L3b1": i["L3_ffn_b1"].reshape(2, 128).T,
            "ident": np.eye(128, dtype=f),
            "desc8": np.tile(np.arange(E2, 0, -1, dtype=f), (128, PAIRS * NT)),
            "desc32": np.tile(np.arange(E1, 0, -1, dtype=f), (128, NT)),
            "causal": (part <= cols).astype(f),
            "earlier": np.concatenate([(cols < part + k * HT).astype(f) for k in range(2)], axis=1)}
    p1 = {"tok_b": rep(i["L0_tok_bias"], 2), "router_b": rep(i["L0_ffn_router_b"], NT),
          "lru_b": rep(i["L0_attn_bias_output"], NT), "L1br": rep(i["L1_ffn_br"], NT),
          "L1b2": i["L1_ffn_b2"].reshape(1, -1), "L2bg": rep(i["L2_ffn_bg"], NT), "L2bias": rep(i["L2_ffn_bias"], NT),
          "L2b2": i["L2_ffn_b2"].reshape(1, -1), "L3br": rep(i["L3_ffn_br"], T), "L3b2": rep(i["L3_ffn_b2"], NT)}
    mine = np.kron(np.eye(E1, dtype=f), np.ones((1, H1), f))
    b1 = np.zeros((E1, E1, H1), f)
    b1[np.arange(E1), np.arange(E1)] = i["L0_ffn_b1"]
    top = i["L0_ffn_W1"].transpose(1, 0, 2).reshape(D, -1)
    p96 = {"L0W1": np.concatenate([top, b1.reshape(E1, -1)]),
           "L0notmine": np.concatenate([np.zeros((D, E1 * H1), f), (mine - 1) * f(BIG)])}
    return {"x": np.ascontiguousarray(x), "txt": i["txt"], "p64": pack(PACK64, p64, 64),
            "p128": pack(PACK128, p128, 128), "p1": pack(PACK1, p1, 1), "p96": pack(PACK96, p96, 96),
            "b2": i["L0_ffn_b2"]}


def kernel(**inputs):
    import numpy as _np
    import concourse.bacc as _bacc
    from concourse.bass_utils import run_bass_kernel_spmd as _run

    arrays = laid_out({k: _np.asarray(v) for k, v in inputs.items()})
    nc = _bacc.Bacc("TRN2", target_bir_lowering=False, num_devices=1)
    args = [nc.dram_tensor(f"in_{k}", a.shape, F32, kind="ExternalInput").ap() for k, a in arrays.items()]
    out = nc.dram_tensor("out", (B, T, D), F32, kind="ExternalOutput").ap()
    fusion_kernel(nc, *args, out)
    r = _run(nc, [{f"in_{k}": a for k, a in arrays.items()}], core_ids=[0])
    return r.results[0]["out"]
```

```python
from contextlib import ExitStack

import numpy as np
import concourse.bass as bass
from concourse import mybir

ALU = mybir.AluOpType
ACT = mybir.ActivationFunctionType
F32 = mybir.dt.float32
F32R = mybir.dt.float32r
AX_X = mybir.AxisListType.X

B, T, D = 16, 210, 64
HT = T // 2
PAIRS = B // 2
NT = 4
W = 2 * T
PAIR = NT * D
PATCHES, KPAR, XM = 82, 13, 500
PSTEP = 6
HL = 128
E1, H1 = 32, 16
NH, KD = 8, 64
E2, H2 = 8, 128
H3 = 256
KEEP = T // 2 - 1
EPS = 1e-5
BIG = 1e30
LOWEST = -3e38

PACK64 = [("L0W1", E1 * H1), ("B_reT", HL), ("B_imT", HL), ("DT2", 2 * D), ("routerT", E1), ("WqT", NH * KD), ("WkT2", 2 * KD),
          ("WvT2", 2 * KD), ("L1WrT", E2), ("L1W1", E2 * H2), ("L2WgT", E2), ("L2W1", E2 * H2), ("qw2", 2 * D),
          ("wr_rep", 128), ("L3w1", H3)]
PACKQE = [("Q", NH * D), ("ET", NH * D)]
PACKC = [("L0b1", E1 * H1), ("L0b2_2", 2 * D)]
PACK128 = [("nu_log", 1), ("theta_log", 1), ("bh_re", 1), ("bh_im", 1), ("C_re2", 2 * D), ("C_im2", 2 * D),
           ("L0W2", 4 * D), ("WoT", 4 * D), ("L1W2", E2 * D), ("L1b1", E2), ("L2W2", E2 * D), ("L2b1", E2),
           ("L3w2", 2 * D), ("L3b1", 2), ("ident", 128), ("desc8", PAIRS * NT * E2), ("desc32", NT * E1),
           ("causal", T + 1), ("earlier", 2 * T), ("same_tile", W), ("pick_expert", E2 * 128), ("L1b2", D), ("L2b2", D),
           ("router_b", NT * E1), ("L1br", E2), ("L2bg", E2), ("L2bias", E2), ("L3br", 1),
           ("lru_b", 1), ("L3b2", 1), ("gamma", 1), ("beta", 1)]
PACK1 = [("tok_b", 2 * D)]


def offsets(pack):
    at, o = {}, 0
    for name, n in pack:
        at[name] = (o, n)
        o += n
    return at, o


class Named:

    def __init__(self, tensor, pack):
        self.t, (self.at, _) = tensor, offsets(pack)

    def __call__(self, name, p0=0, p1=128, a=0, n=None):
        o, size = self.at[name]
        return self.t[p0:p1, o + a:o + a + (size - a if n is None else n)]


def split(ap, **kw):
    return ap.rearrange("p (t e) -> p t e", **kw)


def spread(ap, n):
    return ap.unsqueeze(2).to_broadcast([ap.shape[0], ap.shape[1], n])


def wait_reuse(eng, sem, value):
    if not isinstance(value, int) or value > 0:
        eng.wait_ge(sem, value)


def pipelined(eng, prologue, body):
    prologue()
    with eng.Fori(0, PAIRS // 2 - 1) as j:
        body(2 * j, 0, 2)
        body(2 * j + 1, 1, 2)
    body(PAIRS - 2, 0, 1)
    body(PAIRS - 1, 1, 0)


class Stage:

    def __init__(self, nc, ctx, name):
        self.nc, self.ctx, self.name, self.sems = nc, ctx, name, []

    def sb(self, name, shape, dt=F32):
        return self.ctx.enter_context(self.nc.sbuf_tensor(f"{self.name}_{name}", shape, dt))

    def bank(self, name):
        return self.ctx.enter_context(self.nc.psum_tensor(f"{self.name}_{name}", [128, 512], F32))

    def sem(self, name):
        sem = self.ctx.enter_context(self.nc.semaphore(f"{self.name}_{name}"))
        self.sems.append(sem)
        return sem

    def clear_semaphores(self):
        with self.nc.Block() as block:
            @block.gpsimd
            def _(pool):
                for sem in self.sems:
                    pool.sem_clear(sem)


class Norm:

    def __init__(self, nc, st, res, keep_var=False):
        self.nc, self.res, self.keep_var = nc, res, keep_var
        self.sum = st.sb("ln_sum", [128, 4, NT])
        self.sq = st.sb("ln_sq", [128, PAIR])
        self.var = st.sb("ln_var", [128, 2, NT])
        self.var_ready = st.sem("ln_var_ready")
        self.rstd_done = st.sem("ln_rstd_done")

    def stats(self, dve, n, p):
        nc, R = self.nc, self.res
        h = R.h[0:HT, bass.ds(n * PAIR, PAIR)]
        hc = R.hc[0:HT, bass.ds(n * PAIR, PAIR)]
        nc.vector.reduce_sum(self.sum[0:HT, p, :], split(h, t=NT), axis=AX_X)
        dve.drain()
        nc.vector.scalar_tensor_tensor(out=split(hc, t=NT), in0=spread(self.sum[0:HT, p, :], D), scalar=-1.0 / D,
                                       in1=split(h, t=NT), op0=ALU.mult, op1=ALU.add)
        dve.drain()
        nc.vector.tensor_tensor(self.sq[0:HT, :], hc, hc, ALU.mult)
        dve.drain()
        nc.vector.reduce_sum(self.sum[0:HT, 2 + p, :], split(self.sq[0:HT, :], t=NT), axis=AX_X)
        dve.drain()
        dve.wait_ge(self.rstd_done, n + 1)
        nc.vector.tensor_scalar(self.var[0:HT, p, :], self.sum[0:HT, 2 + p, :], 1.0 / D, EPS, ALU.mult, ALU.add)\
            .then_inc(self.var_ready, 1)
        if self.keep_var:
            nc.vector.tensor_scalar(R.var[0:HT, bass.ds(n * NT, NT)], self.sum[0:HT, 2 + p, :], 1.0 / D, None,
                                    ALU.mult)

    def rstd(self, pool, n, p):
        pool.wait_ge(self.var_ready, n + 1)
        self.nc.gpsimd.tensor_tensor(self.res.rstd[0:HT, bass.ds(n * NT, NT)], self.var[0:HT, p, :],
                                     self.res.neghalf[0:HT, 0:NT], ALU.pow).then_inc(self.rstd_done, 1)

    def finish(self, pool):
        pool.sem_inc(self.rstd_done, 1)
        with pool.Fori(0, PAIRS // 2) as j:
            self.rstd(pool, 2 * j, 0)
            self.rstd(pool, 2 * j + 1, 1)


def normalise(nc, R, n, out):
    return nc.vector.tensor_tensor(split(out, t=NT), split(R.hc[0:HT, bass.ds(n * PAIR, PAIR)], t=NT),
                                   spread(R.rstd[0:HT, bass.ds(n * NT, NT)], D), ALU.mult)


def turn_pair(nc, R, bank, x):
    for smp in range(2):
        mm = nc.tensor.transpose(bank[0:2 * D, smp * HT:(smp + 1) * HT], x[0:HT, smp * 2 * D:(smp + 1) * 2 * D],
                                 R.c128("ident", 0, HT, 0, HT))
    return mm


def half_columns(xT, bank, half):
    return (xT.rearrange("p (s two c) -> p s two c", s=2, two=2)[:, :, half, :],
            bank[half * D:(half + 1) * D, 0:2 * HT].rearrange("p (s c) -> p s c", s=2))


class Head:

    def __init__(self, nc, st, res, twice=False):
        self.nc, self.res, self.twice = nc, res, twice
        self.xn = [st.sb(f"xn{p}", [128, PAIR]) for p in range(2)]
        if twice:
            self.xh = [st.sb(f"xh{p}", [128, W], F32R) for p in range(2)]
            self.xl = [st.sb(f"xl{p}", [128, W], F32R) for p in range(2)]
        else:
            self.x2 = [st.sb(f"x2{p}", [128, W], F32R) for p in range(2)]
        self.turned = st.bank("turned")
        self.xn_ready = st.sem("xn_ready")
        self.turned_ready = st.sem("turned_ready")
        self.high_ready = st.sem("high_ready")
        self.x_ready = st.sem("x_ready")

    def xn_dve(self, dve, n, q):
        normalise(self.nc, self.res, n, self.xn[q][0:HT, :]).then_inc(self.xn_ready, 1)

    def pe(self, pe, n, q):
        pe.wait_ge(self.xn_ready, n + 1)
        wait_reuse(pe, self.x_ready, n)
        turn_pair(self.nc, self.res, self.turned, self.xn[q]).then_inc(self.turned_ready, 1)

    def high_act(self, act, n, q):
        act.wait_ge(self.turned_ready, n + 1)
        x = self.xh[q] if self.twice else self.x2[q]
        for rows in range(2 if self.twice else 1):
            for half in range(2):
                out, in_ = half_columns(x[rows * D:(rows + 1) * D, :], self.turned, half)
                done = self.nc.scalar.copy(out, in_)
        done.then_inc(self.high_ready, 1)

    def low_dve(self, dve, n, q):
        dve.wait_ge(self.high_ready, n + 1)
        high = (self.xh if self.twice else self.x2)[q][0:D, :].bitcast(F32)
        for rows in range(2 if self.twice else 1):
            low = self.xl[q][rows * D:(rows + 1) * D, :] if self.twice else self.x2[q][D:2 * D, :]
            for half in range(2):
                out, in_ = half_columns(low, self.turned, half)
                hi, _ = half_columns(high, self.turned, half)
                done = self.nc.vector.tensor_tensor(out, in_, hi, ALU.subtract)
        done.then_inc(self.x_ready, 1)


def product64(nc, out, R, name, x, start=True, stop=True, a=0, n=128):
    o = R.at64[name][0] + a
    nc.tensor.matmul(out, R.wh[:, o:o + n], x, start=start, stop=False, skip_group_check=True)
    return nc.tensor.matmul(out, R.wl[:, o:o + n], x, start=False, stop=stop, skip_group_check=True)


def product64T(nc, out, R, name, x, a=0, n=None):
    o, size = R.at64[name]
    o, n = o + a, size if n is None else n
    nc.tensor.matmul(out, x, R.wh[:, o:o + n], start=True, stop=False, skip_group_check=True)
    return nc.tensor.matmul(out, x, R.wl[:, o:o + n], start=False, stop=True, skip_group_check=True)


class Tail:

    def __init__(self, nc, st, res, bias=None):
        self.nc, self.res, self.bias = nc, res, bias
        self.yT, self.y = st.bank("yT"), st.bank("y")
        self.flat = st.sb("yT_halves", [128, 2 * HT])
        self.yT_ready, self.flat_ready, self.y_ready, self.y_used = (
            st.sem(k) for k in ("yT_ready", "flat_ready", "y_ready", "y_used"))

    def act(self, act, n):
        act.wait_ge(self.yT_ready, n + 1)
        for half in range(2):
            in_, _ = half_columns(self.yT[0:D, 0:W], self.yT, half)
            out = self.flat[half * D:(half + 1) * D, :].rearrange("p (s c) -> p s c", s=2)
            if self.bias is None:
                done = self.nc.scalar.copy(out, in_)
            else:
                done = self.nc.scalar.activation(out, in_, ACT.Identity, bias=self.res.c128(self.bias, 0, D))
        done.then_inc(self.flat_ready, 1)

    def pe(self, pe, n):
        pe.wait_ge(self.y_used, n + 1)
        pe.wait_ge(self.flat_ready, n + 1)
        for smp in range(2):
            mm = self.nc.tensor.transpose(self.y[0:HT, smp * 2 * D:(smp + 1) * 2 * D],
                                          self.flat[:, smp * HT:(smp + 1) * HT], self.res.c128("ident"))
        mm.then_inc(self.y_ready, 1)

    def first(self, dve):
        dve.sem_inc(self.y_used, 1)

    def residual(self, dve, n, p, ln, relu=False):
        dve.wait_ge(self.y_ready, n + 1)
        y, h = self.y[0:HT, 0:PAIR], hpair(self.res, n)
        if relu:
            self.nc.vector.scalar_tensor_tensor(out=h, in0=y, scalar=0.0, in1=h, op0=ALU.max, op1=ALU.add)\
                .then_inc(self.y_used, 1)
        else:
            self.nc.vector.tensor_tensor(h, h, y, ALU.add).then_inc(self.y_used, 1)
        dve.drain()
        ln.stats(dve, n, p)


def products_bias(nc, out, R, row):
    return nc.tensor.matmul(out, R.ones[0:1, 0:HT], row, start=True, stop=False, skip_group_check=True)


def add(nc, out, lhsT, rhs, stop):
    return nc.tensor.matmul(out, lhsT, rhs, start=False, stop=stop, skip_group_check=True)


def hpair(R, n):
    return R.h[0:HT, bass.ds(n * PAIR, PAIR)]


def tokenizer(nc, R, x, txt, loads, tokw_dram, p64, pqe, pc, notmine):
    with ExitStack() as ctx:
        st = Stage(nc, ctx, "tok")
        ln = Norm(nc, st, R)
        xs = [st.sb(f"x{p}", [128, 2, XM]) for p in range(2)]
        y = [st.bank(f"y{p}") for p in range(2)]
        tokw = st.sb("tokw", [128, KPAR * D])
        raw64, rawqe = st.sb("raw64", [128, offsets(PACK64)[1]]), st.sb("rawqe", [128, offsets(PACKQE)[1]])
        rawc, others = st.sb("rawc", [2 * E1, offsets(PACKC)[1]]), st.sb("others", [2 * E1, E1 * H1])
        qeh, pickh = st.sb("qeh", [128, offsets(PACKQE)[1]], F32R), st.sb("pickh", [2 * E1, offsets(PACKC)[1]], F32R)
        pw = st.sb("pw", [128, 9, 2])
        tmp = st.sb("tmp", [128, T])
        ang = st.sb("ang", [128, 8])
        first_loaded, rest_loaded = st.sem("first_loaded"), st.sem("rest_loaded")
        x_loaded = [st.sem(f"x_loaded{p}") for p in range(2)]
        y_ready, y_used = st.sem("y_ready"), st.sem("y_used")
        consts, angle, turn, unit = st.sem("consts"), st.sem("angle"), st.sem("turn"), st.sem("unit")
        decay_sq, gamma_done = st.sem("decay_sq"), st.sem("gamma_done")
        ctx.callback(st.clear_semaphores)
        block = ctx.enter_context(nc.Block())
        c128 = R.c128
        loads = loads[:2] + [(tokw[:], tokw_dram)] + loads[2:]
        for dst, src in ((raw64, p64), (rawqe, pqe)):
            loads += [(dst[0:D, :], src), (dst[D:2 * D, :], src)]
        for rows in (slice(0, E1), slice(E1, 2 * E1)):
            loads += [(rawc[rows, :], pc), (others[rows, :], notmine)]

        @block.sync
        def _(sp):
            for dst, src in loads[:2]:
                sp.dma_start(dst, src).then_inc(first_loaded, 16)

            def load(n, p):
                sp.wait_ge(y_ready, n - 1)
                sp.dma_start(xs[p][:], x[bass.ds(n, 1)].rearrange("a p s m -> (a p) s m")).then_inc(x_loaded[p], 16)

            for p in range(2):
                sp.dma_start(xs[p][:], x[p]).then_inc(x_loaded[p], 16)
            with sp.Fori(1, PAIRS // 2) as j:
                load(2 * j, 0)
                load(2 * j + 1, 1)

        @block.scalar
        def _(act):
            for dst, src in loads[2:]:
                act.dma_start(dst, src).then_inc(rest_loaded, 16)
            tokens = R.h[:].rearrange("p (b two d) -> p b two d", two=2, d=D)
            act.dma_start(tokens[PATCHES:HT, 0:B, 0, :], txt[:, 0:HT - PATCHES, :].rearrange("b t d -> t b d"))\
                .then_inc(rest_loaded, 16)
            act.dma_start(tokens[0:HT, 0:B, 1, :], txt[:, HT - PATCHES:, :].rearrange("b t d -> t b d"))\
                .then_inc(rest_loaded, 16)
            act.wait_ge(first_loaded, 32)
            nc.scalar.activation(ang[:, 0:1], c128("nu_log"), ACT.Exp)
            nc.scalar.activation(ang[:, 1:2], c128("theta_log"), ACT.Exp)
            act.drain()
            nc.scalar.activation(R.lru[:, 0:1], ang[:, 0:1], ACT.Exp, scale=-1.0).then_inc(angle, 1)
            act.wait_ge(turn, 1)
            nc.scalar.activation(ang[:, 4:5], ang[:, 2:3], ACT.Sin)
            nc.scalar.activation(ang[:, 5:6], ang[:, 2:3], ACT.Sin, scale=0.5).then_inc(unit, 1)
            act.wait_ge(rest_loaded, 16 * (len(loads)))

            def gelu(n, p):
                act.wait_ge(y_ready, n + 1)
                out = R.h[0:PATCHES, bass.ds(n * PAIR, PAIR)].rearrange("p (s two d) -> p s two d", two=2, d=D)
                act.nop(nofuse=True)
                nc.scalar.activation(out[:, :, 0, :], split(y[p][0:PATCHES, 0:2 * D], t=2), ACT.Gelu)\
                    .then_inc(y_used, 1)

            with act.Fori(0, PAIRS // 2) as j:
                gelu(2 * j, 0)
                gelu(2 * j + 1, 1)

        @block.tensor
        def _(pe):
            pe.wait_ge(consts, 1)
            pe.wait_ge(first_loaded, 32)
            pe.wait_ge(rest_loaded, 16 * (len(loads)))

            def patches(n, p, turn_no):
                pe.wait_ge(x_loaded[p], 16 * turn_no)
                pe.wait_ge(y_used, n + 1)
                nc.tensor.matmul(y[p][0:PATCHES, 0:2 * D], R.ones[0:1, 0:PATCHES], R.c1("tok_b", 0, 1),
                                 start=True, stop=False, skip_group_check=True)
                for s in range(2):
                    for c in range(KPAR):
                        k = 128 if c < KPAR - 1 else D
                        mm = add(nc, y[p][0:PATCHES, s * D:(s + 1) * D],
                                 xs[p][0:k, s, c:c + PSTEP * (PATCHES - 1) + 1:PSTEP],
                                 tokw[0:k, c * D:(c + 1) * D], stop=c == KPAR - 1)
                mm.then_inc(y_ready, 1)

            with pe.Fori(0, PAIRS // 2) as j:
                patches(2 * j, 0, j + 1)
                patches(2 * j + 1, 1, j + 1)

        @block.vector
        def _(dve):
            nc.vector.memset(R.neghalf[:], -0.5)
            nc.vector.memset(R.gates[:, PAIRS], 0.0)
            nc.vector.memset(R.half[:], 0.5)
            nc.vector.memset(R.ones[:], 1.0).then_inc(consts, 1)
            dve.sem_inc(y_used, 2)
            dve.wait_ge(angle, 1)
            nc.vector.tensor_tensor(ang[:, 6:7], R.lru[:, 0:1], R.lru[:, 0:1], ALU.mult)
            nc.vector.tensor_scalar(ang[:, 3:4], ang[:, 1:2], 1.0 / (2 * np.pi), None, ALU.mult)
            dve.drain()
            nc.vector.tensor_scalar(ang[:, 7:8], ang[:, 6:7], -1.0, 1.0, ALU.mult, ALU.add).then_inc(decay_sq, 1)
            nc.vector.tensor_scalar(ang[:, 3:4], ang[:, 3:4], 12582912.0, None, ALU.add)
            dve.drain()
            nc.vector.tensor_scalar(ang[:, 3:4], ang[:, 3:4], -12582912.0, None, ALU.add)
            dve.drain()
            nc.vector.scalar_tensor_tensor(out=ang[:, 2:3], in0=ang[:, 3:4], scalar=-6.28125, in1=ang[:, 1:2],
                                           op0=ALU.mult, op1=ALU.add)
            dve.drain()
            nc.vector.scalar_tensor_tensor(out=ang[:, 2:3], in0=ang[:, 3:4], scalar=-(2 * np.pi - 6.28125),
                                           in1=ang[:, 2:3], op0=ALU.mult, op1=ALU.add).then_inc(turn, 1)
            nc.vector.memset(R.decay[:], 1.0)
            dve.drain()
            nc.vector.tensor_scalar(R.decay[:], R.decay[:], R.lru[:, 0:1], None, ALU.mult)
            dve.drain()
            nc.vector.memset(R.decay[:, 0:W:T], 0.0)
            nc.vector.tensor_scalar(R.negC[:, 0:2 * D], c128("C_re2"), -1.0, None, ALU.mult)
            nc.vector.tensor_scalar(R.negC[:, 2 * D:4 * D], c128("C_im2"), -1.0, None, ALU.mult)
            nc.vector.memset(R.cos[:, 0:1], 1.0)
            nc.vector.memset(R.sin[:, 0:1], 0.0)
            dve.wait_ge(unit, 1)
            nc.vector.tensor_copy(pw[:, 0, 1:2], ang[:, 4:5])
            nc.vector.tensor_tensor(ang[:, 3:4], ang[:, 5:6], ang[:, 5:6], ALU.mult)
            dve.drain()
            nc.vector.tensor_scalar(pw[:, 0, 0:1], ang[:, 3:4], -2.0, 1.0, ALU.mult, ALU.add)
            m, k = 1, 0
            while m < T:
                n = min(m, T - m)
                dve.drain()
                c, s = pw[:, k, 0:1], pw[:, k, 1:2]
                nc.vector.tensor_tensor(ang[:, 3:4], c, c, ALU.mult)
                dve.drain()
                nc.vector.scalar_tensor_tensor(out=ang[:, 3:4], in0=s, scalar=s, in1=ang[:, 3:4],
                                               op0=ALU.mult, op1=ALU.add)
                dve.drain()
                nc.vector.tensor_scalar(ang[:, 3:4], ang[:, 3:4], -0.5, 1.5, ALU.mult, ALU.add)
                dve.drain()
                nc.vector.tensor_scalar(pw[:, k, 0:2], pw[:, k, 0:2], ang[:, 3:4], None, ALU.mult)
                dve.drain()
                nc.vector.tensor_scalar(tmp[:, 0:n], R.sin[:, 0:n], s, None, ALU.mult)
                nc.vector.tensor_scalar(R.sin[:, m:m + n], R.sin[:, 0:n], c, None, ALU.mult)
                nc.vector.tensor_tensor(pw[:, k + 1, 0:1], s, s, ALU.mult)
                nc.vector.tensor_scalar(pw[:, k + 1, 1:2], c, s, 2.0, ALU.mult, ALU.mult)
                dve.drain()
                nc.vector.scalar_tensor_tensor(out=R.cos[:, m:m + n], in0=R.cos[:, 0:n], scalar=c, in1=tmp[:, 0:n],
                                               op0=ALU.mult, op1=ALU.subtract)
                nc.vector.scalar_tensor_tensor(out=R.sin[:, m:m + n], in0=R.cos[:, 0:n], scalar=s,
                                               in1=R.sin[:, m:m + n], op0=ALU.mult, op1=ALU.add)
                nc.vector.scalar_tensor_tensor(out=pw[:, k + 1, 0:1], in0=c, scalar=c, in1=pw[:, k + 1, 0:1],
                                               op0=ALU.mult, op1=ALU.subtract)
                m, k = m + n, k + 1
            dve.wait_ge(gamma_done, 1)
            nc.vector.tensor_scalar(R.lru[:, 2:3], R.lru[:, 1:2], 1.0, c128("bh_re"), ALU.add, ALU.mult)
            nc.vector.tensor_scalar(R.lru[:, 3:4], R.lru[:, 1:2], 1.0, c128("bh_im"), ALU.add, ALU.mult)
            dve.wait_ge(rest_loaded, 16 * (len(loads)))
            nc.vector.tensor_copy(R.wh[:], raw64[:])
            nc.vector.tensor_tensor(rawc[:, 0:E1 * H1], rawc[:, 0:E1 * H1], others[:], ALU.add)
            dve.drain()
            nc.vector.tensor_copy(R.qe[0:D, :], rawqe[0:D, :])
            nc.vector.tensor_copy(qeh[D:2 * D, :], rawqe[D:2 * D, :])
            nc.vector.tensor_copy(R.pick[0:E1, :], rawc[0:E1, :])
            nc.vector.tensor_copy(pickh[E1:2 * E1, :], rawc[E1:2 * E1, :])
            nc.vector.memset(R.pick[2 * E1:128, :].bitcast(F32), 0.0)
            nc.vector.tensor_copy(R.pick_expert[:], c128("pick_expert"))
            for i, b in enumerate(("L1b2", "L2b2", "L2b2")):
                nc.vector.tensor_copy(R.b2h[:, i * D:(i + 1) * D], c128(b))
            dve.drain()
            nc.vector.tensor_tensor(R.wl[:], raw64[:], R.wh[:].bitcast(F32), ALU.subtract)
            nc.vector.tensor_tensor(R.qe[D:2 * D, :], rawqe[D:2 * D, :], qeh[D:2 * D, :].bitcast(F32), ALU.subtract)
            nc.vector.tensor_tensor(R.pick[E1:2 * E1, :], rawc[E1:2 * E1, :], pickh[E1:2 * E1, :].bitcast(F32),
                                    ALU.subtract)
            for i, b in enumerate(("L1b2", "L2b2", "L2b2")):
                nc.vector.tensor_tensor(R.b2l[:, i * D:(i + 1) * D], c128(b),
                                        R.b2h[:, i * D:(i + 1) * D].bitcast(F32), ALU.subtract)

            def stats(n, p):
                dve.wait_ge(y_used, n + 3)
                ln.stats(dve, n, p)

            with dve.Fori(0, PAIRS // 2) as j:
                stats(2 * j, 0)
                stats(2 * j + 1, 1)

        @block.gpsimd
        def _(pool):
            pool.wait_ge(consts, 1)
            pool.wait_ge(decay_sq, 1)
            nc.gpsimd.tensor_tensor(R.lru[:, 1:2], ang[:, 7:8], R.half[:, 0:1], ALU.pow).then_inc(gamma_done, 1)
            ln.finish(pool)


def lru(nc, R):
    with ExitStack() as ctx:
        st = Stage(nc, ctx, "lru")
        ln, head, tail = Norm(nc, st, R), Head(nc, st, R), Tail(nc, st, R, bias="lru_b")
        u = [st.bank("u_re"), st.bank("u_im")]
        v = [[st.sb(f"v{i}{p}", [128, W]) for i in range(2)] for p in range(2)]
        a = [st.sb(f"a{i}", [128, W]) for i in range(2)]
        m = [st.sb(f"m{i}", [128, W]) for i in range(4)]
        g = [st.sb(f"g{i}", [128, W]) for i in range(2)]
        out = [[st.sb(f"out{k}{p}", [128, W]) for k in range(4)] for p in range(2)]
        u_ready, v_ready = st.sem("u_ready"), st.sem("v_ready")
        pool_in, scanned, pool_out = st.sem("pool_in"), st.sem("scanned"), st.sem("pool_out")
        states = st.sem("states")
        block = ctx.enter_context(nc.Block())
        two = lambda ap: split(ap[:, 0:W], t=2)
        table = lambda t: t[:, 0:T].unsqueeze(1).to_broadcast([128, 2, T])
        COS, SIN = table(R.cos), table(R.sin)

        @block.vector
        def _(dve):
            def front(n, q):
                head.low_dve(dve, n, q)
                dve.wait_ge(v_ready, n + 1)
                nc.vector.tensor_tensor(two(m[0]), two(v[q][0]), COS, ALU.mult)
                nc.vector.tensor_tensor(two(m[1]), two(v[q][1]), SIN, ALU.mult)
                nc.vector.tensor_tensor(two(m[2]), two(v[q][1]), COS, ALU.mult)
                dve.drain()
                nc.vector.tensor_tensor(a[0][:], m[0][:], m[1][:], ALU.add)
                dve.wait_ge(pool_in, n + 1)
                nc.vector.tensor_tensor(a[1][:], m[2][:], m[3][:], ALU.subtract)
                dve.drain()
                nc.vector.tensor_tensor_scan(g[0][:], R.decay[:], a[0][:], 0.0, ALU.mult, ALU.add)
                nc.vector.tensor_tensor_scan(g[1][:], R.decay[:], a[1][:], 0.0, ALU.mult, ALU.add).then_inc(scanned, 1)
                dve.drain()
                nc.vector.tensor_tensor(two(out[q][0]), two(g[0]), COS, ALU.mult)
                nc.vector.tensor_tensor(two(out[q][1]), two(g[1]), SIN, ALU.mult)
                nc.vector.tensor_tensor(two(out[q][2]), two(g[0]), SIN, ALU.mult).then_inc(states, 1)

            def pro():
                tail.first(dve)
                head.xn_dve(dve, 0, 0)
                head.xn_dve(dve, 1, 1)
                front(0, 0)

            def body(n, p, more):
                if more:
                    front(n + 1, 1 - p)
                tail.residual(dve, n, p, ln)
                if more > 1:
                    head.xn_dve(dve, n + 2, p)

            pipelined(dve, pro, body)

        @block.gpsimd
        def _(pool):
            def front(n, q):
                pool.wait_ge(v_ready, n + 1)
                nc.gpsimd.tensor_tensor(two(m[3]), two(v[q][0]), SIN, ALU.mult).then_inc(pool_in, 1)
                pool.wait_ge(scanned, n + 1)
                nc.gpsimd.tensor_tensor(two(out[q][3]), two(g[1]), COS, ALU.mult).then_inc(pool_out, 1)

            def body(n, p, more):
                if more:
                    front(n + 1, 1 - p)
                ln.rstd(pool, n, p)

            pool.sem_inc(ln.rstd_done, 1)
            pipelined(pool, lambda: front(0, 0), body)

        @block.scalar
        def _(act):
            def front(n, q):
                head.high_act(act, n, q)
                act.wait_ge(u_ready, n + 1)
                nc.scalar.activation(v[q][0][:], u[0][:, 0:W], ACT.Identity, bias=R.lru[:, 2:3], scale=R.lru[:, 1:2])
                nc.scalar.activation(v[q][1][:], u[1][:, 0:W], ACT.Identity, bias=R.lru[:, 3:4], scale=R.lru[:, 1:2])\
                    .then_inc(v_ready, 1)

            def body(n, p, more):
                if more:
                    front(n + 1, 1 - p)
                tail.act(act, n)

            pipelined(act, lambda: front(0, 0), body)

        @block.tensor
        def _(pe):
            def front(n, q):
                head.pe(pe, n, q)
                pe.wait_ge(head.x_ready, n + 1)
                wait_reuse(pe, v_ready, n)
                for i, w in enumerate(("B_reT", "B_imT")):
                    mm = product64(nc, u[i][:, 0:W], R, w, head.x2[q][:])
                mm.then_inc(u_ready, 1)

            def body(n, p, more):
                if more:
                    front(n + 1, 1 - p)
                product64(nc, tail.yT[:, 0:W], R, "DT2", head.x2[p][:], stop=False)
                pe.wait_ge(states, n + 1)
                pe.wait_ge(pool_out, n + 1)
                C = [R.c128("C_re2"), R.negC[:, 0:2 * D], R.negC[:, 2 * D:4 * D], R.negC[:, 2 * D:4 * D]]
                for k in range(4):
                    mm = add(nc, tail.yT[:, 0:W], C[k], out[p][k][:], stop=k == 3)
                mm.then_inc(tail.yT_ready, 1)
                tail.pe(pe, n)

            pipelined(pe, lambda: front(0, 0), body)


def top1(nc, R):
    with ExitStack() as ctx:
        st = Stage(nc, ctx, "top1")
        ln, head, tail = Norm(nc, st, R), Head(nc, st, R), Tail(nc, st, R)
        NC, NB = 4, 3
        lg, ohT = st.bank("logits"), st.bank("chosenT")
        hb = [st.bank(f"hidden{c}") for c in range(NB)]
        hid = [st.sb(f"hid{c}", [128, W]) for c in range(NC)]
        picked = [st.sb(f"picked{p}", [128, W], F32R) for p in range(2)]
        lgs, eq, top = st.sb("lgs", [128, NT * E1]), st.sb("eq", [128, NT * E1]), st.sb("top", [128, 2, NT])
        oh = st.sb("chosen", [128, NT, 128])
        lg_ready, oh_ready, ohT_ready, picked_ready = (st.sem(k) for k in ("lg_ready", "oh_ready", "ohT_ready",
                                                                           "picked_ready"))
        h_ready, relu_act, relu_dve = st.sem("h_ready"), st.sem("relu_act"), st.sem("relu_dve")
        block = ctx.enter_context(nc.Block())
        desc = split(R.c128("desc32", 0, HT), t=NT)
        o_pick = lambda a, n: R.pick[:, a:a + n]

        @block.vector
        def _(dve):
            def choose(n):
                dve.wait_ge(lg_ready, n + 1)
                l4, e4 = split(lgs[0:HT, :], t=NT), split(eq[0:HT, :], t=NT)
                nc.vector.tensor_tensor(lgs[0:HT, :], lg[0:HT, 0:NT * E1], R.c128("router_b", 0, HT), ALU.add)
                dve.drain()
                nc.vector.reduce_max(top[0:HT, 0, :], l4, axis=AX_X)
                dve.drain()
                nc.vector.tensor_tensor(e4, l4, spread(top[0:HT, 0, :], E1), ALU.is_equal)
                dve.drain()
                nc.vector.tensor_tensor(e4, e4, desc, ALU.mult)
                dve.drain()
                nc.vector.reduce_max(top[0:HT, 1, :], e4, axis=AX_X)
                dve.drain()
                for copy in range(2):
                    done = nc.vector.tensor_tensor(oh[0:HT, :, copy * E1:(copy + 1) * E1], e4,
                                                   spread(top[0:HT, 1, :], E1), ALU.is_equal)
                done.then_inc(oh_ready, 1)

            def pro():
                tail.first(dve)
                nc.vector.memset(oh[:], 0.0)
                head.xn_dve(dve, 0, 0)
                head.xn_dve(dve, 1, 1)
                head.low_dve(dve, 0, 0)
                choose(0)

            def body(n, p, more):
                if more:
                    head.low_dve(dve, n + 1, 1 - p)
                for c in (1, 3):
                    dve.wait_ge(h_ready, n * NC + c + 1)
                    nc.vector.tensor_scalar(hid[c][:], hb[c % NB][:, 0:W], 0.0, None, ALU.max).then_inc(relu_dve, 1)
                if more:
                    choose(n + 1)
                tail.residual(dve, n, p, ln, relu=True)
                if more > 1:
                    head.xn_dve(dve, n + 2, p)

            pipelined(dve, pro, body)

        @block.gpsimd
        def _(pool):
            ln.finish(pool)

        @block.scalar
        def _(act):
            def put(n, q):
                act.wait_ge(ohT_ready, n + 1)
                nc.scalar.copy(picked[q][:], ohT[:, 0:W]).then_inc(picked_ready, 1)

            def pro():
                head.high_act(act, 0, 0)
                put(0, 0)

            def body(n, p, more):
                if more:
                    head.high_act(act, n + 1, 1 - p)
                for c in (0, 2):
                    act.wait_ge(h_ready, n * NC + c + 1)
                    nc.scalar.activation(hid[c][:], hb[c % NB][:, 0:W], ACT.Relu).then_inc(relu_act, 1)
                tail.act(act, n)
                if more:
                    put(n + 1, 1 - p)

            pipelined(act, pro, body)

        @block.tensor
        def _(pe):
            def logits(n, q):
                pe.wait_ge(head.x_ready, n + 1)
                for t in range(NT):
                    mm = product64T(nc, lg[0:HT, t * E1:(t + 1) * E1], R, "routerT",
                                    head.x2[q][:, t * HT:(t + 1) * HT])
                mm.then_inc(lg_ready, 1)

            def turn_choice(n):
                pe.wait_ge(oh_ready, n + 1)
                for t in range(NT):
                    mm = nc.tensor.transpose(ohT[:, t * HT:(t + 1) * HT], oh[0:HT, t, :], R.c128("ident", 0, HT, 0, HT))
                mm.then_inc(ohT_ready, 1)

            def pro():
                head.pe(pe, 0, 0)
                logits(0, 0)
                turn_choice(0)

            def body(n, p, more):
                if more:
                    head.pe(pe, n + 1, 1 - p)
                pe.wait_ge(picked_ready, n + 1)
                for c in range(NC):
                    if c == NB:
                        pe.wait_ge(relu_act, 2 * n + 1)
                    product64(nc, hb[c % NB][:, 0:W], R, "L0W1", head.x2[p][:], stop=False, a=c * 128)
                    add(nc, hb[c % NB][:, 0:W], o_pick(c * 128, 128), picked[p][:], stop=True).then_inc(h_ready, 1)
                if more:
                    logits(n + 1, 1 - p)
                nc.tensor.matmul(tail.yT[:, 0:W], o_pick(E1 * H1, 128), picked[p][:], start=True, stop=False,
                                 skip_group_check=True)
                pe.wait_ge(relu_act, 2 * n + 2)
                pe.wait_ge(relu_dve, 2 * n + 2)
                for c in range(NC):
                    mm = add(nc, tail.yT[0:D, 0:W], R.c128("L0W2", 0, 128, c * D, D), hid[c][:], stop=c == NC - 1)
                mm.then_inc(tail.yT_ready, 1)
                if more:
                    turn_choice(n + 1)
                tail.pe(pe, n)

            pipelined(pe, pro, body)


def mqa(nc, R, v_dram, ctx_dram):
    with ExitStack() as ctx:
        st = Stage(nc, ctx, "mqa")
        head = Head(nc, st, R)
        s = [st.bank(f"s{i}") for i in range(3)]
        pt = [st.bank(f"pt{i}") for i in range(2)]
        cxT, cx = st.bank("cxT"), st.bank("cx")
        kh = [st.sb(f"kh{p}", [128, W], F32R) for p in range(2)]
        kl = [st.sb(f"kl{p}", [128, W], F32R) for p in range(2)]
        q2 = [[st.sb(f"q{h}{p}", [128, W], F32R) for h in range(NH)] for p in range(2)]
        vT = st.sb("vT", [64, W])
        v = [st.sb(f"v{p}", [128, 2, 2, KD]) for p in range(2)]
        prob = [st.sb(f"prob{i}", [128, 2 * T]) for i in range(2)]
        probT = [st.sb(f"probT{i}", [128, 2 * T]) for i in range(2)]
        mx = [st.sb(f"mx{i}", [128, 2]) for i in range(3)]
        negm = [st.sb(f"negm{i}", [128, 2]) for i in range(3)]
        sums = [st.sb(f"sums{i}", [128, NH]) for i in range(2)]
        inv = st.sb("inv", [128, NH])
        cxTs = [st.sb(f"cxTs{i}", [128, T]) for i in range(2)]
        cxs = [st.sb(f"cxs{i}", [128, NH * KD]) for i in range(2)]
        f_ready, f_act, f_dve = st.sem("front_ready"), st.sem("front_act"), st.sem("front_dve")
        v_out, v_in = st.sem("v_out"), st.sem("v_in")
        s_ready, m_ready, e_ready = st.sem("s_ready"), st.sem("m_ready"), st.sem("e_ready")
        pt_ready, pts_ready, av_done = st.sem("pt_ready"), st.sem("pts_ready"), st.sem("av_done")
        cxT_done, cx_turned = st.sem("cxT_done"), st.sem("cx_turned")
        cx_ready, cx_stored = st.sem("cx_ready"), [st.sem(f"cx_stored{i}") for i in range(2)]
        block = ctx.enter_context(nc.Block())
        UNITS, SCALE = 16, 1.0 / float(np.sqrt(np.float32(KD // NH)))
        heads = lambda hp: [hp // 2 * 4 + hp % 2, hp // 2 * 4 + hp % 2 + 2]
        fbank = [cxT, cx, s[0], s[1], s[2], pt[0]]
        FA, FD = 10, 9

        @block.tensor
        def _(pe):
            def front(n, p):
                pe.wait_ge(head.x_ready, n + 1)
                wait_reuse(pe, cx_ready, NT * n)
                wait_reuse(pe, pts_ready, UNITS * n)
                for i in range(6):
                    name, a = (("WkT2", 0), ("WvT2", 0))[i] if i < 2 else ("WqT", (i - 2) * 128)
                    product64(nc, fbank[i][:, 0:W], R, name, head.x2[p][:], a=a).then_inc(f_ready, 1)

            def scores(n, p, u):
                t, hp = u // 4, u % 4
                smp = t // 2
                if u >= 3:
                    pe.wait_ge(e_ready, UNITS * n + u - 2)
                for k in range(2):
                    o, q = s[u % 3][0:HT, k * T:(k + 1) * T], q2[p][heads(hp)[k]][:, t * HT:(t + 1) * HT]
                    nc.tensor.matmul(o, q, kh[p][:, smp * T:(smp + 1) * T], start=True, stop=False,
                                     skip_group_check=True)
                    mm = add(nc, o, q, kl[p][:, smp * T:(smp + 1) * T], stop=True)
                mm.then_inc(s_ready, 1)

            def turn(n, u):
                pe.wait_ge(e_ready, UNITS * n + u + 1)
                if u >= 2:
                    pe.wait_ge(pts_ready, UNITS * n + u - 1)
                for k in range(2):
                    for c in range(2):
                        mm = nc.tensor.transpose(pt[u % 2][0:HT, (2 * c + k) * HT:(2 * c + k + 1) * HT],
                                                 prob[u % 2][0:HT, (2 * k + c) * HT:(2 * k + c + 1) * HT],
                                                 R.c128("ident", 0, HT, 0, HT))
                mm.then_inc(pt_ready, 1)

            def values(n, p, u):
                smp = u // 8
                pe.wait_ge(pts_ready, UNITS * n + u + 1)
                if u == 0:
                    pe.wait_ge(v_in, 32 * (n + 1))
                if u >= 2 and u % 2 == 0:
                    pe.wait_ge(cxT_done, UNITS // 2 * n + u // 2)
                for c in range(2):
                    mm = nc.tensor.matmul(cxT[u % 2 * KD:(u % 2 + 1) * KD, 0:T], v[p][0:HT, smp, c, :],
                                          probT[u % 2][0:HT, c * T:(c + 1) * T], start=c == 0, stop=c == 1,
                                          skip_group_check=True)
                mm.then_inc(av_done, 1)

            def turn_back(n, u):
                t, m = u // 4, u % 4 // 2
                pe.wait_ge(cxT_done, UNITS // 2 * n + (u + 1) // 2)
                if m == 0 and t > 0:
                    pe.wait_ge(cx_ready, NT * n + t)
                for k in range(2):
                    mm = nc.tensor.transpose(cx[0:HT, (2 * m + k) * 2 * KD:(2 * m + k + 1) * 2 * KD],
                                             cxTs[u // 2 % 2][:, k * HT:(k + 1) * HT], R.c128("ident"))
                mm.then_inc(cx_turned, 1)

            def pro():
                head.pe(pe, 0, 0)
                front(0, 0)

            def body(n, p, more):
                if more:
                    head.pe(pe, n + 1, 1 - p)
                pe.wait_ge(f_act, FA * (n + 1))
                pe.wait_ge(f_dve, FD * (n + 1))
                scores(n, p, 0)
                scores(n, p, 1)
                for u in range(UNITS + 2):
                    if u + 2 < UNITS:
                        scores(n, p, u + 2)
                    if u < UNITS:
                        turn(n, u)
                    if 1 <= u <= UNITS:
                        values(n, p, u - 1)
                    if u >= 3 and u % 2:
                        turn_back(n, u - 2)
                if more:
                    front(n + 1, 1 - p)

            pipelined(pe, pro, body)

        @block.scalar
        def _(act):
            def front(n, p):
                act.wait_ge(f_ready, 6 * n + 1)
                nc.scalar.copy(kh[p][:], fbank[0][:, 0:W]).then_inc(f_act, 1)
                act.wait_ge(f_ready, 6 * n + 2)
                wait_reuse(act, v_out, 16 * n)
                nc.scalar.copy(vT[:], fbank[1][0:KD, 0:W]).then_inc(f_act, 1)
                for i in range(4):
                    act.wait_ge(f_ready, 6 * n + i + 3)
                    for k in range(2):
                        nc.scalar.copy(q2[p][2 * i + k][0:KD, :], fbank[i + 2][k * KD:(k + 1) * KD, 0:W])\
                            .then_inc(f_act, 1)

            def exps(n, u):
                t, hp = u // 4, u % 4
                act.wait_ge(m_ready, UNITS * n + u + 1)
                if u >= 2:
                    act.wait_ge(pt_ready, UNITS * n + u - 1)
                if hp == 0 and t >= 2:
                    act.wait_ge(cx_ready, NT * n + t - 1)
                for k in range(2):
                    h = heads(hp)[k]
                    e = nc.scalar.activation(prob[u % 2][0:HT, k * T:(k + 1) * T], s[u % 3][0:HT, k * T:(k + 1) * T],
                                             ACT.Exp, bias=negm[u % 3][0:HT, k:k + 1], scale=SCALE,
                                             accum_out=sums[t % 2][0:HT, h:h + 1])
                e.then_inc(e_ready, 1)

            def take_context(n, u):
                act.wait_ge(av_done, UNITS * n + u + 1)
                if u >= 4:
                    act.wait_ge(cx_turned, UNITS // 2 * n + u // 2 - 1)
                nc.scalar.copy(cxTs[u // 2 % 2][:], cxT[:, 0:T]).then_inc(cxT_done, 1)

            def pro():
                head.high_act(act, 0, 0)
                front(0, 0)

            def body(n, p, more):
                if more:
                    head.high_act(act, n + 1, 1 - p)
                for u in range(UNITS + 2):
                    if u >= 3 and u % 2:
                        take_context(n, u - 2)
                    if u < UNITS:
                        exps(n, u)
                if more:
                    front(n + 1, 1 - p)

            pipelined(act, pro, body)

        @block.vector
        def _(dve):
            def front(n, p):
                dve.wait_ge(f_act, FA * n + 1)
                nc.vector.tensor_tensor(kl[p][:], fbank[0][:, 0:W], kh[p][:].bitcast(F32), ALU.subtract)\
                    .then_inc(f_dve, 1)
                for i in range(4):
                    for k in range(2):
                        q = q2[p][2 * i + k]
                        dve.wait_ge(f_act, FA * n + 3 + 2 * i + k)
                        nc.vector.tensor_tensor(q[KD:2 * KD, :], fbank[i + 2][k * KD:(k + 1) * KD, 0:W],
                                                q[0:KD, :].bitcast(F32), ALU.subtract).then_inc(f_dve, 1)

            def maxima(n, u):
                dve.wait_ge(s_ready, UNITS * n + u + 1)
                nc.vector.reduce_max(mx[u % 3][0:HT, :], split(s[u % 3][0:HT, 0:W], t=2), axis=AX_X)
                dve.drain()
                nc.vector.tensor_scalar(negm[u % 3][0:HT, :], mx[u % 3][0:HT, :], -SCALE, None, ALU.mult)\
                    .then_inc(m_ready, 1)

            def take(n, u):
                dve.wait_ge(pt_ready, UNITS * n + u + 1)
                if u >= 2:
                    dve.wait_ge(av_done, UNITS * n + u - 1)
                nc.vector.tensor_copy(probT[u % 2][0:HT, :], pt[u % 2][0:HT, 0:W]).then_inc(pts_ready, 1)

            def context(n, t):
                dve.wait_ge(cx_turned, UNITS // 2 * n + 2 * t + 2)
                dve.wait_ge(cx_stored[t % 2], 16 * (2 * n + t // 2 + 1))
                nc.vector.reciprocal(inv[0:HT, :], sums[t % 2][0:HT, :])
                dve.drain()
                nc.vector.tensor_tensor(cxs[t % 2][0:HT, :].rearrange("p (h d) -> p h d", h=NH),
                                        cx[0:HT, :].rearrange("p (h d) -> p h d", h=NH),
                                        spread(inv[0:HT, :], KD), ALU.mult).then_inc(cx_ready, 1)

            def pro():
                for stored in cx_stored:
                    dve.sem_inc(stored, 16)
                head.xn_dve(dve, 0, 0)
                head.xn_dve(dve, 1, 1)
                head.low_dve(dve, 0, 0)
                front(0, 0)

            def body(n, p, more):
                maxima(n, 0)
                maxima(n, 1)
                if more:
                    head.low_dve(dve, n + 1, 1 - p)
                for u in range(UNITS):
                    if u + 2 < UNITS:
                        maxima(n, u + 2)
                    take(n, u)
                    if u % 4 == 3 and u > 4:
                        context(n, u // 4 - 1)
                context(n, NT - 1)
                if more:
                    front(n + 1, 1 - p)
                if more > 1:
                    head.xn_dve(dve, n + 2, p)

            pipelined(dve, pro, body)

        @block.sync
        def _(sp):
            def v_round(n, p):
                sp.wait_ge(f_act, FA * n + 2)
                sp.dma_start(v_dram[bass.ds(2 * n, 2)].rearrange("s (c t) -> c s t", c=KD),
                             split(vT[:], t=2)).then_inc(v_out, 16)
                sp.wait_ge(v_out, 16 * (n + 1))
                for smp in range(2):
                    sp.dma_start(v[p][0:HT, smp], v_dram[bass.ds(2 * n + smp, 1)]
                                 .rearrange("s (c t d) -> t (s c) d", c=2, d=KD)).then_inc(v_in, 16)

            def body(n, p, more):
                for t in range(NT):
                    sp.wait_ge(cx_ready, NT * n + t + 1)
                    sp.dma_start(ctx_dram[bass.ds(2 * n + t // 2, 1), t % 2].rearrange("s t c -> (s t) c"),
                                 cxs[t % 2][0:HT, :]).then_inc(cx_stored[t % 2], 16)
                if more:
                    v_round(n + 1, 1 - p)

            pipelined(sp, lambda: v_round(0, 0), body)
            for stored in cx_stored:
                sp.wait_ge(stored, 16 * (2 * PAIRS + 1))


def mqa_out(nc, R, ctx_dram):
    with ExitStack() as ctx:
        st = Stage(nc, ctx, "mqao")
        ln, tail = Norm(nc, st, R, keep_var=True), Tail(nc, st, R)
        c = [st.sb(f"c{p}", [128, 2, 4, T]) for p in range(2)]
        loaded = [st.sem(f"loaded{p}") for p in range(2)]
        block = ctx.enter_context(nc.Block())

        @block.sync
        def _(sp):
            sp.sem_inc(tail.yT_ready, 1)

            def load(n, p):
                if not isinstance(n, int):
                    sp.wait_ge(tail.yT_ready, n)
                for smp in range(2):
                    sp.dma_start(c[p][:, smp], ctx_dram[bass.ds(2 * n + smp, 1)]
                                 .rearrange("s two t c -> s (two t c)")
                                 .rearrange("s (c p t) -> p (s c) t", p=128, t=T)).then_inc(loaded[p], 16)

            load(0, 0)
            load(1, 1)
            with sp.Fori(1, PAIRS // 2) as j:
                load(2 * j, 0)
                load(2 * j + 1, 1)

        @block.tensor
        def _(pe):
            def products(n, p, turn):
                pe.wait_ge(loaded[p], 32 * turn)
                wait_reuse(pe, tail.flat_ready, n)
                for k in range(4):
                    mm = nc.tensor.matmul(tail.yT[0:D, 0:W], R.c128("WoT", 0, 128, k * D, D), c[p][:, :, k, :],
                                          start=k == 0, stop=k == 3, skip_group_check=True)
                mm.then_inc(tail.yT_ready, 1)

            products(0, 0, 1)
            with pe.Fori(0, PAIRS // 2 - 1) as j:
                products(2 * j + 1, 1, j + 1)
                tail.pe(pe, 2 * j)
                products(2 * j + 2, 0, j + 2)
                tail.pe(pe, 2 * j + 1)
            products(PAIRS - 1, 1, PAIRS // 2)
            tail.pe(pe, PAIRS - 2)
            tail.pe(pe, PAIRS - 1)

        @block.scalar
        def _(act):
            tail.act(act, 1)
            with act.Fori(1, PAIRS) as n:
                act.wait_ge(tail.y_ready, n)
                tail.act(act, n + 1)

        @block.vector
        def _(dve):
            tail.first(dve)

            with dve.Fori(0, PAIRS // 2) as j:
                tail.residual(dve, 2 * j, 0, ln)
                tail.residual(dve, 2 * j + 1, 1, ln)

        @block.gpsimd
        def _(pool):
            ln.finish(pool)


def top2_route(nc, R, name, gate, biases, own_norm):
    with ExitStack() as ctx:
        st = Stage(nc, ctx, name)
        xn = [st.sb(f"xn{p}", [128, PAIR]) for p in range(2)]
        turned = [st.bank(f"turned{p}") for p in range(2)]
        lg = [st.bank(f"logits{p}") for p in range(2)]
        xT = [st.sb(f"xT{p}", [64, W]) for p in range(2)]
        x2 = [st.sb(f"x2{p}", [128, W], F32R) for p in range(2)]
        ALL = PAIRS * NT
        factor, var = st.sb("factor", [128, ALL]), st.sb("var", [128, ALL])
        lga, eq, o1, o2 = (st.sb(k, [128, ALL * E2]) for k in ("all", "eq", "first", "second"))
        m1, m2, kk, dl, ex, w1, w2 = (st.sb(k, [128, ALL]) for k in ("m1", "m2", "kk", "dl", "ex", "w1", "w2"))
        high = st.sb("gates_high", [128, ALL * E2], F32R)
        xn_ready, turned_ready, high_ready, x_ready = (st.sem(k) for k in ("xn_ready", "turned_ready", "high_ready",
                                                                           "x_ready"))
        lg_ready, var_ready, rs_ready = st.sem("lg_ready"), st.sem("var_ready"), st.sem("rs_ready")
        diff_ready, exp_ready = st.sem("diff_ready"), st.sem("exp_ready")
        block = ctx.enter_context(nc.Block())

        @block.vector
        def _(dve):
            def make(n, p):
                scale = factor if own_norm else R.rstd
                nc.vector.tensor_tensor(split(xn[p][0:HT, :], t=NT), split(R.hc[0:HT, bass.ds(n * PAIR, PAIR)], t=NT),
                                        spread(scale[0:HT, bass.ds(n * NT, NT)], D), ALU.mult).then_inc(xn_ready, 1)

            def low(n, p):
                dve.wait_ge(high_ready, n + 1)
                if own_norm:
                    nc.vector.tensor_tensor(x2[p][D:2 * D, :], xT[p][:], x2[p][0:D, :].bitcast(F32), ALU.subtract)\
                        .then_inc(x_ready, 1)
                    return
                for half in range(2):
                    out, in_ = half_columns(x2[p][D:2 * D, :], turned[p], half)
                    hi, _ = half_columns(x2[p][0:D, :].bitcast(F32), turned[p], half)
                    done = nc.vector.tensor_tensor(out, in_, hi, ALU.subtract)
                done.then_inc(x_ready, 1)

            def keep(n, p):
                dve.wait_ge(lg_ready, n + 1)
                out = lga[0:HT, bass.ds(n * NT * E2, NT * E2)]
                bias = [R.c128(b, 0, HT).unsqueeze(1).to_broadcast([HT, NT, E2]) for b in biases]
                dve.nop(nofuse=True)
                nc.vector.tensor_tensor(split(out, t=NT), split(lg[p][0:HT, 0:NT * E2], t=NT), bias[0], ALU.add)
                for b in bias[1:]:
                    dve.drain()
                    nc.vector.tensor_tensor(split(out, t=NT), split(out, t=NT), b, ALU.add)

            def pro():
                if own_norm:
                    nc.vector.tensor_tensor(factor[0:HT, :], R.rstd[0:HT, :], R.rstd[0:HT, :], ALU.mult)
                    dve.drain()
                    nc.vector.tensor_tensor(factor[0:HT, :], R.var[0:HT, :], factor[0:HT, :], ALU.mult)
                    dve.drain()
                    nc.vector.tensor_scalar(var[0:HT, :], factor[0:HT, :], EPS, None, ALU.add).then_inc(var_ready, 1)
                    dve.wait_ge(rs_ready, 1)
                    nc.vector.tensor_tensor(factor[0:HT, :], var[0:HT, :], R.rstd[0:HT, :], ALU.mult)
                    dve.drain()
                make(0, 0)
                make(1, 1)
                low(0, 0)

            def body(n, p, more):
                if more:
                    low(n + 1, 1 - p)
                if more > 1:
                    make(n + 2, p)
                keep(n, p)

            pipelined(dve, pro, body)
            dve.drain()

            l3, e3 = (split(t[0:HT, :], e=E2) for t in (lga, eq))
            desc = split(R.c128("desc8", 0, HT), e=E2)

            def first_of_highest(src, top, out):
                nc.vector.reduce_max(top[0:HT, :], src, axis=AX_X)
                dve.drain()
                nc.vector.tensor_tensor(e3, src, spread(top[0:HT, :], E2), ALU.is_equal)
                dve.drain()
                nc.vector.tensor_tensor(e3, e3, desc, ALU.mult)
                dve.drain()
                nc.vector.reduce_max(kk[0:HT, :], e3, axis=AX_X)
                dve.drain()
                nc.vector.tensor_tensor(out, e3, spread(kk[0:HT, :], E2), ALU.is_equal)
                dve.drain()

            first, second = (split(t[0:HT, :], e=E2) for t in (o1, o2))
            first_of_highest(l3, m1, first)
            nc.vector.scalar_tensor_tensor(out=l3, in0=first, scalar=LOWEST, in1=l3, op0=ALU.mult, op1=ALU.add)
            dve.drain()
            first_of_highest(l3, m2, second)
            nc.vector.tensor_tensor(dl[0:HT, :], m2[0:HT, :], m1[0:HT, :], ALU.subtract).then_inc(diff_ready, 1)
            dve.wait_ge(exp_ready, 1)
            nc.vector.tensor_scalar(w2[0:HT, :], ex[0:HT, :], 1.0, None, ALU.add)
            dve.drain()
            nc.vector.reciprocal(w1[0:HT, :], w2[0:HT, :])
            dve.drain()
            nc.vector.tensor_tensor(w2[0:HT, :], ex[0:HT, :], w1[0:HT, :], ALU.mult)
            nc.vector.tensor_tensor(first, first, spread(w1[0:HT, :], E2), ALU.mult)
            dve.drain()
            nc.vector.tensor_tensor(second, second, spread(w2[0:HT, :], E2), ALU.mult)
            dve.drain()
            nc.vector.tensor_tensor(first, first, second, ALU.add)
            dve.drain()
            nc.vector.tensor_copy(high[0:HT, :], o1[0:HT, :])
            dve.drain()
            by_pair = lambda ap: ap.rearrange("p (n g) -> p n g", n=PAIRS)
            nc.vector.tensor_copy(R.gates[0:HT, 0:PAIRS, 0, :], by_pair(high[0:HT, :].bitcast(F32)))
            nc.vector.tensor_tensor(R.gates[0:HT, 0:PAIRS, 1, :], by_pair(o1[0:HT, :]),
                                    by_pair(high[0:HT, :].bitcast(F32)), ALU.subtract)

        @block.gpsimd
        def _(pool):
            if own_norm:
                pool.wait_ge(var_ready, 1)
                nc.gpsimd.tensor_tensor(var[0:HT, :], var[0:HT, :],
                                        R.neghalf[0:HT, 0:1].to_broadcast([HT, ALL]), ALU.pow).then_inc(rs_ready, 1)

        @block.scalar
        def _(act):
            def put(n, p):
                act.wait_ge(turned_ready, n + 1)
                for half in range(2):
                    if own_norm:
                        out, in_ = half_columns(xT[p][:], turned[p], half)
                        nc.scalar.activation(out, in_, ACT.Identity, bias=R.c128("beta", 0, D),
                                             scale=R.c128("gamma", 0, D))
                    else:
                        out, in_ = half_columns(x2[p][0:D, :], turned[p], half)
                        done = nc.scalar.copy(out, in_)
                if own_norm:
                    act.drain()
                    done = nc.scalar.copy(x2[p][0:D, :], xT[p][:])
                done.then_inc(high_ready, 1)

            def store(n, p):
                act.wait_ge(x_ready, n + 1)
                act.nop(nofuse=True)
                nc.scalar.copy(R.x2[:, bass.ds(n * W, W)], x2[p][:].bitcast(F32))
                act.drain()

            def body(n, p, more):
                if more:
                    put(n + 1, 1 - p)
                store(n, p)

            pipelined(act, lambda: put(0, 0), body)
            act.wait_ge(diff_ready, 1)
            nc.scalar.activation(ex[0:HT, :], dl[0:HT, :], ACT.Exp).then_inc(exp_ready, 1)

        @block.tensor
        def _(pe):
            def turn(n, p):
                pe.wait_ge(xn_ready, n + 1)
                turn_pair(nc, R, turned[p], xn[p]).then_inc(turned_ready, 1)

            def logits(n, p):
                pe.wait_ge(x_ready, n + 1)
                for t in range(NT):
                    mm = product64T(nc, lg[p][0:HT, t * E2:(t + 1) * E2], R, gate, x2[p][:, t * HT:(t + 1) * HT])
                mm.then_inc(lg_ready, 1)

            def pro():
                turn(0, 0)
                turn(1, 1)

            def body(n, p, more):
                logits(n, p)
                if more > 1:
                    turn(n + 2, p)

            pipelined(pe, pro, body)


def top2(nc, R, name, w1, b1, w2, b2, func):
    with ExitStack() as ctx:
        st = Stage(nc, ctx, name)
        ln, tail = Norm(nc, st, R), Tail(nc, st, R)
        hb, gb = ([st.bank(f"{k}{i}") for i in range(2)] for k in ("hidden", "gates"))
        gT = st.bank("gatesT")
        G = [st.sb(f"G{p}", [128, W], F32R) for p in range(2)]
        hid = [st.sb(f"hid{i}", [128, W]) for i in range(2)]
        gs = st.sb("gates", [128, 128])
        NG = 4
        gated = [st.sb(f"gated{i}", [128, W]) for i in range(NG)]
        gs_ready, gT_ready, G_ready, h_ready, gb_ready, hid_ready, gated_ready = (
            st.sem(k) for k in ("gs_ready", "gT_ready", "G_ready", "h_ready", "gb_ready", "hid_ready", "gated_ready"))
        block = ctx.enter_context(nc.Block())
        AHEAD = 3
        b2_at = {"L1b2": 0, "L2b2": D}[b2]

        @block.tensor
        def _(pe):
            def turn_gates(n):
                pe.wait_ge(gs_ready, n + 1)
                nc.tensor.transpose(gT[:, 0:HT], gs[0:HT, :],
                                    R.c128("ident", 0, HT, 0, HT)).then_inc(gT_ready, 1)

            def hidden(n, p, e):
                pe.wait_ge(gated_ready, n * E2 + e + 1)
                pe.nop(nofuse=True)
                product64(nc, hb[e % 2][:, 0:W], R, w1, R.x2[:, bass.ds(n * W, W)], a=e * H2).then_inc(h_ready, 1)
                if e == 0:
                    pe.wait_ge(G_ready, n + 1)
                nc.tensor.matmul(gb[e % 2][:, 0:W], R.pick_expert[:, e * 128:(e + 1) * 128], G[p][:],
                                 start=True, stop=True).then_inc(gb_ready, 1)

            def pro():
                turn_gates(0)
                for e in range(AHEAD):
                    hidden(0, 0, e)

            def body(n, p, more):
                for k, b in enumerate((R.b2h, R.b2l)):
                    nc.tensor.matmul(tail.yT[:, 0:W], b[:, b2_at:b2_at + 128], G[p][:], start=k == 0, stop=False,
                                     skip_group_check=True)
                for e in range(E2):
                    pe.wait_ge(gated_ready, n * E2 + e + 3)
                    mm = add(nc, tail.yT[0:D, 0:W], R.c128(w2, 0, 128, e * D, D), gated[e % NG][:], stop=e == E2 - 1)
                    if e == 1 and more:
                        turn_gates(n + 1)
                    if e == E2 - 1:
                        mm.then_inc(tail.yT_ready, 1)
                    if e + AHEAD < E2:
                        hidden(n, p, e + AHEAD)
                    elif more:
                        hidden(n + 1, 1 - p, e + AHEAD - E2)
                tail.pe(pe, n)

            pipelined(pe, pro, body)

        @block.scalar
        def _(act):
            def unit(n, e):
                act.wait_ge(h_ready, n * E2 + e + 1)
                nc.scalar.activation(hid[e % 2][:], hb[e % 2][:, 0:W], func, bias=R.c128(b1, 0, 128, e, 1))\
                    .then_inc(hid_ready, 1)

            def take_gates(n):
                nc.scalar.copy(gs[0:HT, :], R.gates[0:HT, bass.ds(n, 2)].rearrange("p n two g -> p (n two g)"))\
                    .then_inc(gs_ready, 1)

            def pro():
                take_gates(0)
                unit(0, 0)
                unit(0, 1)

            def body(n, p, more):
                if more:
                    act.wait_ge(gT_ready, n + 1)
                    act.nop(nofuse=True)
                    take_gates(n + 1)
                for e in range(E2):
                    if e + 2 < E2:
                        unit(n, e + 2)
                    elif more:
                        unit(n + 1, e + 2 - E2)
                tail.act(act, n)

            pipelined(act, pro, body)

        @block.vector
        def _(dve):
            def own_tiles(n, p):
                dve.wait_ge(gT_ready, n + 1)
                nc.vector.tensor_tensor(split(G[p][:], t=NT), gT[:, 0:HT].unsqueeze(1).to_broadcast([128, NT, HT]),
                                        split(R.c128("same_tile"), t=NT), ALU.mult).then_inc(G_ready, 1)

            def weight(n, e):
                dve.wait_ge(hid_ready, n * E2 + e + 1)
                dve.wait_ge(gb_ready, n * E2 + e + 1)
                nc.vector.tensor_tensor(gated[e % NG][:], hid[e % 2][:], gb[e % 2][:, 0:W], ALU.mult)\
                    .then_inc(gated_ready, 1)

            def pro():
                dve.sem_inc(gated_ready, 2)
                tail.first(dve)
                own_tiles(0, 0)
                for e in range(AHEAD):
                    weight(0, e)

            def body(n, p, more):
                for e in range(E2):
                    if e == 2 and more:
                        own_tiles(n + 1, 1 - p)
                    if e + AHEAD < E2:
                        weight(n, e + AHEAD)
                    elif more and e < E2 - 1:
                        weight(n + 1, e + AHEAD - E2)
                tail.residual(dve, n, p, ln)
                if more:
                    weight(n + 1, AHEAD - 1)

            pipelined(dve, pro, body)

        @block.gpsimd
        def _(pool):
            ln.finish(pool)


def quadratic(nc, R):
    with ExitStack() as ctx:
        st = Stage(nc, ctx, "quad")
        ln, head, tail = Norm(nc, st, R), Head(nc, st, R, twice=True), Tail(nc, st, R)
        fb = [st.bank(f"f{i}") for i in range(2)]
        ob = [st.bank(f"o{i}") for i in range(3)]
        q2 = st.sb("q2", [128, NH, W], F32R)
        es = [[st.sb(f"es{t}{p}", [128, NH * D]) for t in range(NT)] for p in range(2)]
        LATE = HT + 1
        om = [[st.sb(f"om{s}{i}", [128, 2 * T if i < 4 else 4 * LATE]) for i in range(6)] for s in range(2)]
        f_ready, f_act, f_dve, o_ready, o_done = (st.sem(k) for k in ("f_ready", "f_act", "f_dve", "o_ready", "o_done"))
        block = ctx.enter_context(nc.Block())
        F, U, FD = 8, 12, 4

        @block.tensor
        def _(pe):
            def front(n, p, i):
                if 2 <= i < 6:
                    pe.wait_ge(f_act, F * n + i - 1)
                elif i >= 6:
                    pe.wait_ge(f_dve, FD * n + i - 5)
                if i < 4:
                    o, tile, (e, _) = fb[i % 2][0:HT, :], slice(i * HT, (i + 1) * HT), R.atqe["ET"]
                    args = [(x[p][:, tile], R.qe[:, e:e + NH * D]) for x in (head.xh, head.xl)]
                else:
                    o, c = fb[i % 2][:, 0:W], R.atqe["Q"][0] + (i - 4) * 128
                    args = [(R.qe[:, c:c + 128], x[p][:]) for x in (head.xh, head.xl)]
                nc.tensor.matmul(o, *args[0], start=True, stop=False)
                nc.tensor.matmul(o, *args[1], start=False, stop=True).then_inc(f_ready, 1)

            def omega(n, p, smp, i):
                u = smp * 6 + i
                pe.wait_ge(o_done, n * U + u + 1)
                if i < 4:
                    tile, q = 2 * smp, q2[:, 2 * i:2 * i + 2, smp * T:(smp + 1) * T]
                else:
                    tile, q = 2 * smp + 1, q2[:, 4 * (i - 4):4 * (i - 3), (smp + 1) * T - LATE:(smp + 1) * T]
                o = split(ob[u % 3][0:HT, 0:q.shape[1] * q.shape[2]], t=q.shape[1])
                tile = slice(tile * HT, (tile + 1) * HT)
                nc.tensor.matmul(o, head.xh[p][:, tile], q, start=True, stop=False)
                nc.tensor.matmul(o, head.xl[p][:, tile], q, start=False, stop=True).then_inc(o_ready, 1)

            def result(p, smp, h):
                first, late = om[smp][h // 2], om[smp][4 + h // 4]
                nc.tensor.matmul(tail.yT[0:D, smp * T:(smp + 1) * T], es[p][2 * smp][0:HT, h * D:(h + 1) * D],
                                 first[0:HT, h % 2 * T:(h % 2 + 1) * T], start=h == 0, stop=False,
                                 skip_group_check=True)
                return add(nc, tail.yT[0:D, (smp + 1) * T - LATE:(smp + 1) * T],
                           es[p][2 * smp + 1][0:HT, h * D:(h + 1) * D],
                           late[0:HT, h % 4 * LATE:(h % 4 + 1) * LATE], stop=h == NH - 1)

            def first_sample(n, p):
                pe.wait_ge(f_dve, FD * (n + 1))
                for i in range(6):
                    omega(n, p, 0, i)

            def pro():
                head.pe(pe, 0, 0)
                pe.wait_ge(head.x_ready, 1)
                for i in range(F):
                    front(0, 0, i)
                first_sample(0, 0)

            def body(n, p, more):
                if more:
                    head.pe(pe, n + 1, 1 - p)
                for i in range(6):
                    omega(n, p, 1, i)
                    if i == 1:
                        pe.wait_ge(o_done, n * U + 6 + 3)
                    for h in ((), (0,), (1, 2), (3, 4), (5, 6), (7,))[i]:
                        result(p, 0, h)
                    if i >= 2 and more:
                        if i == 2:
                            pe.wait_ge(head.x_ready, n + 2)
                        front(n + 1, 1 - p, i - 2)
                for i in range(4):
                    if more:
                        front(n + 1, 1 - p, 4 + i)
                    if i == 0:
                        pe.wait_ge(o_done, n * U + 12 + 3)
                    for h in (2 * i, 2 * i + 1):
                        mm = result(p, 1, h)
                mm.then_inc(tail.yT_ready, 1)
                if more:
                    first_sample(n + 1, 1 - p)
                tail.pe(pe, n)

            pipelined(pe, pro, body)

        @block.scalar
        def _(act):
            def front(n, p):
                for i in range(F):
                    act.wait_ge(f_ready, n * F + i + 1)
                    if i < 4:
                        nc.scalar.copy(es[p][i][0:HT, :], fb[i % 2][0:HT, :]).then_inc(f_act, 1)
                    else:
                        nc.scalar.copy(q2[0:D, 2 * (i - 4), :], fb[i % 2][0:D, 0:W])
                        nc.scalar.copy(q2[0:D, 2 * (i - 4) + 1, :], fb[i % 2][D:2 * D, 0:W]).then_inc(f_act, 1)

            def pro():
                head.high_act(act, 0, 0)
                front(0, 0)

            def body(n, p, more):
                if more:
                    head.high_act(act, n + 1, 1 - p)
                    front(n + 1, 1 - p)
                tail.act(act, n)

            pipelined(act, pro, body)

        @block.vector
        def _(dve):
            causal = R.c128("causal", 0, HT)

            def q_low(n):
                for i in range(4):
                    dve.wait_ge(f_act, n * F + 4 + i + 1)
                    for k in range(2):
                        done = nc.vector.tensor_tensor(q2[D:2 * D, 2 * i + k, :], fb[i % 2][k * D:(k + 1) * D, 0:W],
                                                       q2[0:D, 2 * i + k, :].bitcast(F32), ALU.subtract)
                    done.then_inc(f_dve, 1)

            def masks(n, smp):
                for i in range(6):
                    u = smp * 6 + i
                    dve.wait_ge(o_ready, n * U + u + 1)
                    k, mask = (2, causal[:, 1:T + 1]) if i < 4 else (4, causal[:, 0:LATE])
                    cols = mask.shape[1]
                    nc.vector.tensor_tensor(split(om[smp][i][0:HT, :], t=k), split(ob[u % 3][0:HT, 0:k * cols], t=k),
                                            mask.unsqueeze(1).to_broadcast([HT, k, cols]), ALU.mult).then_inc(o_done, 1)

            def pro():
                dve.sem_inc(o_done, 3)
                tail.first(dve)
                head.xn_dve(dve, 0, 0)
                head.xn_dve(dve, 1, 1)
                head.low_dve(dve, 0, 0)
                q_low(0)
                masks(0, 0)

            def body(n, p, more):
                if more:
                    head.low_dve(dve, n + 1, 1 - p)
                masks(n, 1)
                if more:
                    q_low(n + 1)
                    masks(n + 1, 0)
                tail.residual(dve, n, p, ln)
                if more > 1:
                    head.xn_dve(dve, n + 2, p)

            pipelined(dve, pro, body)

        @block.gpsimd
        def _(pool):
            ln.finish(pool)


def sigmoid_attention(nc, R):
    with ExitStack() as ctx:
        st = Stage(nc, ctx, "sig")
        ln, head, tail = Norm(nc, st, R), Head(nc, st, R), Tail(nc, st, R)
        qb = st.bank("q")
        ab = [[st.bank(f"a{s}{p}") for s in range(2)] for p in range(2)]
        qh, ql = ([st.sb(f"{k}{p}", [128, W], F32R) for p in range(2)] for k in ("qh", "ql"))
        att = [[st.sb(f"att{s}{p}", [128, W]) for s in range(2)] for p in range(2)]
        q_ready, qh_ready, ql_ready, a_ready, a_done = (
            st.sem(k) for k in ("q_ready", "qh_ready", "ql_ready", "a_ready", "a_done"))
        block = ctx.enter_context(nc.Block())

        @block.tensor
        def _(pe):
            def query(n, p):
                pe.wait_ge(head.x_ready, n + 1)
                product64(nc, qb[:, 0:W], R, "qw2", head.x2[p][:]).then_inc(q_ready, 1)

            def scores(n, p):
                pe.wait_ge(ql_ready, n + 1)
                for smp in range(2):
                    for i in range(2):
                        tile = 2 * smp + i
                        o, x = ab[p][smp][0:HT, i * T:(i + 1) * T], head.x2[p][:, tile * HT:(tile + 1) * HT]
                        nc.tensor.matmul(o, x, qh[p][:, smp * T:(smp + 1) * T], start=True, stop=False,
                                         skip_group_check=True)
                        mm = add(nc, o, x, ql[p][:, smp * T:(smp + 1) * T], stop=True)
                    mm.then_inc(a_ready, 1)

            def values(n, p):
                for smp in range(2):
                    pe.wait_ge(a_done, 2 * n + smp + 1)
                    for i in range(2):
                        tile = 2 * smp + i
                        mm = nc.tensor.matmul(tail.yT[0:D, smp * T:(smp + 1) * T],
                                              head.xn[p][0:HT, tile * D:(tile + 1) * D],
                                              att[p][smp][0:HT, i * T:(i + 1) * T], start=i == 0, stop=i == 1,
                                              skip_group_check=True)
                mm.then_inc(tail.yT_ready, 1)

            def pro():
                head.pe(pe, 0, 0)
                query(0, 0)
                head.pe(pe, 1, 1)
                scores(0, 0)
                query(1, 1)

            def body(n, p, more):
                values(n, p)
                if more:
                    scores(n + 1, 1 - p)
                tail.pe(pe, n)
                if more > 1:
                    head.pe(pe, n + 2, p)
                    query(n + 2, p)

            pipelined(pe, pro, body)

        @block.scalar
        def _(act):
            def query(n, p):
                act.wait_ge(q_ready, n + 1)
                nc.scalar.copy(qh[p][:], qb[:, 0:W]).then_inc(qh_ready, 1)

            def sigmoid(n, p):
                for smp in range(2):
                    act.wait_ge(a_ready, 2 * n + smp + 1)
                    nc.scalar.activation(att[p][smp][0:HT, :], ab[p][smp][0:HT, 0:W], ACT.Sigmoid).then_inc(a_done, 1)

            def pro():
                head.high_act(act, 0, 0)
                query(0, 0)
                head.high_act(act, 1, 1)
                sigmoid(0, 0)
                query(1, 1)

            def body(n, p, more):
                tail.act(act, n)
                if more:
                    sigmoid(n + 1, 1 - p)
                if more > 1:
                    head.high_act(act, n + 2, p)
                    query(n + 2, p)

            pipelined(act, pro, body)

        @block.vector
        def _(dve):
            def query_low(n, p):
                dve.wait_ge(qh_ready, n + 1)
                nc.vector.tensor_tensor(ql[p][:], qb[:, 0:W], qh[p][:].bitcast(F32), ALU.subtract).then_inc(ql_ready, 1)

            def pro():
                tail.first(dve)
                head.xn_dve(dve, 0, 0)
                head.xn_dve(dve, 1, 1)
                for n in range(2):
                    head.low_dve(dve, n, n)
                    query_low(n, n)

            def body(n, p, more):
                tail.residual(dve, n, p, ln)
                if more > 1:
                    head.xn_dve(dve, n + 2, p)
                    head.low_dve(dve, n + 2, p)
                    query_low(n + 2, p)

            pipelined(dve, pro, body)

        @block.gpsimd
        def _(pool):
            ln.finish(pool)


def depths(nc, R, out):
    with ExitStack() as ctx:
        st = Stage(nc, ctx, "mod")
        head, tail = Head(nc, st, R), Tail(nc, st, R, bias="L3b2")
        wb, wcolumn = st.bank("weights"), st.bank("wcolumn")
        hb = [st.bank(f"hidden{i}") for i in range(2)]
        hid = [st.sb(f"hid{i}", [128, W]) for i in range(2)]
        wrow = [st.sb(f"wrow{p}", [128, W]) for p in range(2)]
        scr = [st.sb(f"scr{i}", [128, T]) for i in range(2)]
        wcol, hi, ties, rank, f = (st.sb(k, [128, NT]) for k in ("wcol", "higher", "ties", "rank", "factor"))
        x_and_h = [st.sb(f"x_and_h{p}", [128, PAIR]) for p in range(2)]
        o = [st.sb(f"o{p}", [128, PAIR]) for p in range(2)]
        w_ready, wrow_ready, wcol_ready, h_ready, h_done, sum_ready, o_ready = (
            st.sem(k) for k in ("w_ready", "wrow_ready", "wcol_ready", "h_ready", "h_done", "sum_ready", "o_ready"))
        stored = [st.sem(f"stored{p}") for p in range(2)]
        block = ctx.enter_context(nc.Block())

        @block.tensor
        def _(pe):
            def front(n, p):
                pe.wait_ge(head.x_ready, n + 1)
                product64(nc, wb[:, 0:W], R, "wr_rep", head.x2[p][:]).then_inc(w_ready, 1)
                for i in range(2):
                    product64(nc, hb[i][:, 0:W], R, "L3w1", head.x2[p][:], a=i * 128).then_inc(h_ready, 1)

            def columns(n, p):
                pe.wait_ge(wrow_ready, n + 1)
                pe.wait_ge(tail.y_used, n + 1)
                for t in range(NT):
                    mm = nc.tensor.transpose(wcolumn[0:HT, t * HT:(t + 1) * HT],
                                             wrow[p][0:HT, t * HT:(t + 1) * HT], R.c128("ident", 0, HT, 0, HT))
                mm.then_inc(wcol_ready, 1)

            def pro():
                head.pe(pe, 0, 0)
                front(0, 0)
                head.pe(pe, 1, 1)

            def body(n, p, more):
                columns(n, p)
                pe.wait_ge(h_done, 2 * n + 2)
                for i in range(2):
                    mm = nc.tensor.matmul(tail.yT[0:D, 0:W], R.c128("L3w2", 0, 128, i * D, D), hid[i][:],
                                          start=i == 0, stop=i == 1, skip_group_check=True)
                mm.then_inc(tail.yT_ready, 1)
                if more:
                    front(n + 1, 1 - p)
                tail.pe(pe, n)
                if more > 1:
                    head.pe(pe, n + 2, p)

            pipelined(pe, pro, body)

        @block.scalar
        def _(act):
            def front(n, p):
                act.wait_ge(w_ready, n + 1)
                nc.scalar.activation(wrow[p][0:HT, :], wb[0:HT, 0:W], ACT.Identity, bias=R.c128("L3br", 0, HT))\
                    .then_inc(wrow_ready, 1)
                for i in range(2):
                    act.wait_ge(h_ready, 2 * n + i + 1)
                    nc.scalar.activation(hid[i][:], hb[i][:, 0:W], ACT.Gelu_apprx_tanh,
                                         bias=R.c128("L3b1", 0, 128, i, 1)).then_inc(h_done, 1)

            def pro():
                head.high_act(act, 0, 0)
                front(0, 0)
                head.high_act(act, 1, 1)

            def body(n, p, more):
                tail.act(act, n)
                if more:
                    front(n + 1, 1 - p)
                if more > 1:
                    head.high_act(act, n + 2, p)

            pipelined(act, pro, body)

        @block.vector
        def _(dve):
            def pro():
                tail.first(dve)
                for s in stored:
                    dve.sem_inc(s, 16)
                head.xn_dve(dve, 0, 0)
                head.xn_dve(dve, 1, 1)
                head.low_dve(dve, 0, 0)

            def body(n, p, more):
                dve.wait_ge(wcol_ready, n + 1)
                nc.vector.tensor_copy(wcol[0:HT, :], wcolumn[0:HT, 0:W:HT])
                dve.drain()
                for t in range(NT):
                    row = wrow[p][0:HT, (t // 2) * T:(t // 2 + 1) * T]
                    nc.vector.tensor_scalar(scr[0][0:HT, :], row, wcol[0:HT, t:t + 1], None, ALU.is_gt, ALU.add,
                                            accum_out=hi[0:HT, t:t + 1])
                    nc.vector.scalar_tensor_tensor(out=scr[1][0:HT, :], in0=row, scalar=wcol[0:HT, t:t + 1],
                                                   in1=R.c128("earlier", 0, HT, (t % 2) * T, T), op0=ALU.is_equal,
                                                   op1=ALU.mult, accum_out=ties[0:HT, t:t + 1])
                    dve.drain()
                    if t == 1 and more:
                        head.low_dve(dve, n + 1, 1 - p)
                nc.vector.tensor_tensor(rank[0:HT, :], hi[0:HT, :], ties[0:HT, :], ALU.add)
                dve.drain()
                nc.vector.scalar_tensor_tensor(out=f[0:HT, :], in0=rank[0:HT, :], scalar=float(KEEP),
                                               in1=wcol[0:HT, :], op0=ALU.is_lt, op1=ALU.mult)
                dve.drain()
                dve.wait_ge(stored[p], 8 * (n - p) + 16)
                dve.wait_ge(tail.y_ready, n + 1)
                nc.vector.tensor_tensor(split(o[p][0:HT, :], t=NT), split(tail.y[0:HT, 0:PAIR], t=NT),
                                        spread(f[0:HT, :], D), ALU.mult).then_inc(tail.y_used, 1)
                dve.drain()
                dve.wait_ge(sum_ready, n + 1)
                nc.vector.tensor_tensor(o[p][0:HT, :], o[p][0:HT, :], x_and_h[p][0:HT, :], ALU.add).then_inc(o_ready, 1)
                if more > 1:
                    head.xn_dve(dve, n + 2, p)

            pipelined(dve, pro, body)

        @block.gpsimd
        def _(pool):
            def body(n, p, more):
                pool.wait_ge(head.xn_ready, n + 1)
                pool.nop(nofuse=True)
                nc.gpsimd.tensor_tensor(x_and_h[p][0:HT, :], head.xn[p][0:HT, :], hpair(R, n), ALU.add)\
                    .then_inc(sum_ready, 1)

            pipelined(pool, lambda: None, body)

        @block.sync
        def _(sp):
            def store(n, p):
                sp.wait_ge(o_ready, n + 1)
                sp.dma_start(out[bass.ds(2 * n, 2)].rearrange("s (two t) d -> t (s two) d", two=2),
                             split(o[p][0:HT, :], t=NT)).then_inc(stored[p], 16)

            with sp.Fori(0, PAIRS // 2) as j:
                store(2 * j, 0)
                store(2 * j + 1, 1)
            for s in stored:
                sp.wait_ge(s, 16 * (PAIRS // 2) + 16)


class Resident:
    pass


def fusion_kernel(nc, x, txt, p128, p1, tokw, p64, pqe, pc, others, out):
    with ExitStack() as ctx:
        st = Stage(nc, ctx, "all")
        R = Resident()
        R.h, R.hc = st.sb("h", [128, PAIRS * PAIR]), st.sb("centred", [128, PAIRS * PAIR])
        R.rstd = st.sb("rstd", [128, PAIRS * NT])
        R.neghalf, R.half = st.sb("neghalf", [128, NT]), st.sb("half", [128, 1])
        R.ones = st.sb("ones", [1, 128])
        R.lru = st.sb("lru_consts", [128, 4])
        R.cos, R.sin, R.decay = st.sb("cos", [128, T]), st.sb("sin", [128, T]), st.sb("decay", [128, W])
        R.negC = st.sb("negC", [128, 4 * D])
        R.var = st.sb("var", [128, PAIRS * NT])
        R.gates = st.sb("gates", [128, PAIRS + 1, 2, NT * E2])
        R.x2 = st.sb("x2", [128, PAIRS * W], F32R)
        R.wh, R.wl = (st.sb(k, [128, offsets(PACK64)[1]], F32R) for k in ("w_high", "w_low"))
        R.qe = st.sb("quadratic_w", [128, offsets(PACKQE)[1]], F32R)
        R.pick = st.sb("top1_pick", [128, offsets(PACKC)[1]], F32R)
        R.pick_expert = st.sb("picks", [128, E2 * 128], F32R)
        R.b2h, R.b2l = (st.sb(k, [128, 3 * D], F32R) for k in ("b2_high", "b2_low"))
        R.at64, R.atqe = offsets(PACK64)[0], offsets(PACKQE)[0]
        t128, t1 = st.sb("p128", [128, offsets(PACK128)[1]]), st.sb("p1", [1, offsets(PACK1)[1]])
        R.c128, R.c1 = Named(t128, PACK128), Named(t1, PACK1)
        v_dram = nc.dram_tensor("v_scratch", [B, KD * T], F32).ap()
        ctx_dram = nc.dram_tensor("ctx_scratch", [B, 2, HT, NH * KD], F32).ap()

        tokenizer(nc, R, x, txt, [(t128[:], p128), (t1[:], p1)], tokw, p64, pqe, pc, others)
        lru(nc, R)
        top1(nc, R)
        mqa(nc, R, v_dram, ctx_dram)
        mqa_out(nc, R, ctx_dram)
        top2_route(nc, R, "rg", "L1WrT", ["L1br"], own_norm=True)
        top2(nc, R, "gelu2", "L1W1", "L1b1", "L1W2", "L1b2", ACT.Gelu)
        quadratic(nc, R)
        top2_route(nc, R, "rr", "L2WgT", ["L2bg", "L2bias"], own_norm=False)
        top2(nc, R, "relu2", "L2W1", "L2b1", "L2W2", "L2b2", ACT.Relu)
        sigmoid_attention(nc, R)
        depths(nc, R, out)


def pack(spec, parts, rows):
    for name, n in spec:
        assert parts[name].shape == (rows, n), (name, parts[name].shape, n)
    return np.ascontiguousarray(np.concatenate([parts[name] for name, _ in spec], axis=1))


def laid_out(i):
    f = np.float32
    rep = lambda v, n: np.tile(v.reshape(1, -1), (1, n))
    experts_in = lambda w: w.transpose(1, 0, 2).reshape(w.shape[1], -1)
    x = i["x"].reshape(PAIRS, 2, D, XM, 2).transpose(0, 4, 2, 1, 3).reshape(PAIRS, 128, 2, XM)
    w = i["L0_tok_weight"].reshape(D, 25, D)
    w = np.concatenate([w, np.zeros((D, 1, D), f)], axis=1).reshape(D, KPAR, 2, D)
    tokw = w.transpose(2, 0, 1, 3).reshape(128, KPAR * D)
    twice = lambda w: np.tile(w, (1, 2))
    p64 = {"L0W1": experts_in(i["L0_ffn_W1"]), "B_reT": i["L0_attn_B_re"].T, "B_imT": i["L0_attn_B_im"].T,
           "DT2": twice(i["L0_attn_D"].T), "routerT": i["L0_ffn_router_w"].T, "WqT": i["L1_attn_Wq"].T,
           "WkT2": twice(i["L1_attn_Wk"].T), "WvT2": twice(i["L1_attn_Wv"].T), "L1WrT": i["L1_ffn_Wr"],
           "L1W1": experts_in(i["L1_ffn_W1"]), "L2WgT": i["L2_ffn_Wg"], "L2W1": experts_in(i["L2_ffn_W1"]),
           "qw2": twice(i["L3_attn_q_weight"]), "wr_rep": np.tile(i["L3_ffn_wr"], (1, 128)), "L3w1": i["L3_ffn_w1"]}
    pqe = {"Q": experts_in(i["L2_attn_Q"]), "ET": i["L2_attn_E"].transpose(2, 0, 1).reshape(D, -1)}
    chunks = lambda w: w.reshape(-1, 128, D).transpose(1, 0, 2).reshape(128, -1)
    column = lambda v: np.concatenate([v.reshape(-1, 1), np.zeros((128 - v.size, 1), f)])
    rows = lambda v: np.tile(v.reshape(1, -1), (128, 1))
    part = np.arange(128)[:, None]
    cols = np.arange(T)[None, :]
    gate_row = (part < 2 * NT * E2)
    by_gate = lambda b2: np.concatenate([np.tile(b2, (2 * NT, 1)), np.zeros((128 - 2 * NT * E2, D), f)])
    p128 = {"nu_log": i["L0_attn_nu_log"][:, None], "theta_log": i["L0_attn_theta_log"][:, None],
            "bh_re": i["L0_attn_bh_re"][:, None], "bh_im": i["L0_attn_bh_im"][:, None],
            "C_re2": twice(i["L0_attn_C_re"].T), "C_im2": twice(i["L0_attn_C_im"].T),
            "L0W2": chunks(i["L0_ffn_W2"].reshape(E1 * H1, D)), "WoT": chunks(np.ascontiguousarray(i["L1_attn_Wo"].T)),
            "L1W2": chunks(i["L1_ffn_W2"].reshape(-1, D)), "L1b1": i["L1_ffn_b1"].T,
            "L2W2": chunks(i["L2_ffn_W2"].reshape(-1, D)), "L2b1": i["L2_ffn_b1"].T,
            "L3w2": chunks(i["L3_ffn_w2"]), "L3b1": i["L3_ffn_b1"].reshape(2, 128).T,
            "ident": np.eye(128, dtype=f),
            "desc8": np.tile(np.arange(E2, 0, -1, dtype=f), (128, PAIRS * NT)),
            "desc32": np.tile(np.arange(E1, 0, -1, dtype=f), (128, NT)),
            "causal": (part < np.arange(T + 1)[None, :]).astype(f),
            "earlier": np.concatenate([(cols < part + k * HT).astype(f) for k in range(2)], axis=1),
            "same_tile": (gate_row & (part // E2 % NT == np.arange(W)[None, :] // HT)).astype(f),
            "pick_expert": (gate_row & (part % E2 == np.arange(E2 * 128)[None, :] // 128)).astype(f),
            "L1b2": by_gate(i["L1_ffn_b2"]), "L2b2": by_gate(i["L2_ffn_b2"]),
            "router_b": rows(np.tile(i["L0_ffn_router_b"], NT)), "L1br": rows(i["L1_ffn_br"]),
            "L2bg": rows(i["L2_ffn_bg"]), "L2bias": rows(i["L2_ffn_bias"]), "L3br": rows(i["L3_ffn_br"]),
            "lru_b": column(i["L0_attn_bias_output"]), "L3b2": column(i["L3_ffn_b2"]),
            "gamma": column(i["L1_ffn_gamma"]), "beta": column(i["L1_ffn_beta"])}
    p1 = {"tok_b": rep(i["L0_tok_bias"], 2)}
    mine = np.kron(np.eye(E1, dtype=f), np.ones((1, H1), f))
    b1 = np.zeros((E1, E1, H1), f)
    b1[np.arange(E1), np.arange(E1)] = i["L0_ffn_b1"]
    pc = {"L0b1": b1.reshape(E1, -1), "L0b2_2": twice(i["L0_ffn_b2"])}
    return {"x": np.ascontiguousarray(x), "txt": i["txt"], "p128": pack(PACK128, p128, 128), "p1": pack(PACK1, p1, 1),
            "tokw": np.ascontiguousarray(tokw), "p64": pack(PACK64, p64, 64), "pqe": pack(PACKQE, pqe, 64),
            "pc": pack(PACKC, pc, E1), "others": (mine - 1) * f(BIG)}


def kernel(**inputs):
    import numpy as _np
    import concourse.bacc as _bacc
    from concourse.bass_utils import run_bass_kernel_spmd as _run

    arrays = laid_out({k: _np.asarray(v) for k, v in inputs.items()})
    nc = _bacc.Bacc("TRN2", target_bir_lowering=False, num_devices=1)
    args = [nc.dram_tensor(f"in_{k}", a.shape, F32, kind="ExternalInput").ap() for k, a in arrays.items()]
    out = nc.dram_tensor("out", (B, T, D), F32, kind="ExternalOutput").ap()
    fusion_kernel(nc, *args, out)
    r = _run(nc, [{f"in_{k}": a for k, a in arrays.items()}], core_ids=[0])
    return r.results[0]["out"]
```

```python
from contextlib import ExitStack

import numpy as np
import concourse.bass as bass
from concourse import mybir

ALU = mybir.AluOpType
ACT = mybir.ActivationFunctionType
F32 = mybir.dt.float32
F32R = mybir.dt.float32r
AX_X = mybir.AxisListType.X

B, T, D = 16, 210, 64
HT = T // 2
PAIRS = B // 2
NT = 4
W = 2 * T
PAIR = NT * D
PATCHES, KPAR, XM = 82, 13, 500
PSTEP = 6
HL = 128
E1, H1 = 32, 16
NH, KD = 8, 64
E2, H2 = 8, 128
H3 = 256
KEEP = T // 2 - 1
EPS = 1e-5
BIG = 1e30
LOWEST = -3e38

PACK64 = [("L0W1", E1 * H1), ("B_reT", HL), ("B_imT", HL), ("DT2", 2 * D), ("routerT", E1), ("WqT", NH * KD), ("WkT2", 2 * KD),
          ("WvT2", 2 * KD), ("L1WrT", E2), ("L1W1", E2 * H2), ("L2WgT", E2), ("L2W1", E2 * H2), ("qw2", 2 * D),
          ("wr_rep", 128), ("L3w1", H3)]
PACKQE = [("Q", NH * D), ("ET", NH * D)]
PACKC = [("L0b1", E1 * H1), ("L0b2_2", 2 * D)]
PACK128 = [("nu_log", 1), ("theta_log", 1), ("bh_re", 1), ("bh_im", 1), ("C_re2", 2 * D), ("C_im2", 2 * D),
           ("L0W2", 4 * D), ("WoT", 4 * D), ("L1W2", E2 * D), ("L1b1", E2), ("L2W2", E2 * D), ("L2b1", E2),
           ("L3w2", 2 * D), ("L3b1", 2), ("ident", 128), ("desc8", PAIRS * NT * E2), ("desc32", NT * E1),
           ("causal", T + 1), ("earlier", 2 * T), ("same_tile", W), ("pick_expert", E2 * 128), ("L1b2", D), ("L2b2", D),
           ("router_b", NT * E1), ("L1br", E2), ("L2bg", E2), ("L2bias", E2), ("L3br", 1),
           ("lru_b", 1), ("L3b2", 1), ("gamma", 1), ("beta", 1)]
PACK1 = [("tok_b", 2 * D)]


def offsets(pack):
    at, o = {}, 0
    for name, n in pack:
        at[name] = (o, n)
        o += n
    return at, o


class Named:

    def __init__(self, tensor, pack):
        self.t, (self.at, _) = tensor, offsets(pack)

    def __call__(self, name, p0=0, p1=128, a=0, n=None):
        o, size = self.at[name]
        return self.t[p0:p1, o + a:o + a + (size - a if n is None else n)]


def split(ap, **kw):
    return ap.rearrange("p (t e) -> p t e", **kw)


def spread(ap, n):
    return ap.unsqueeze(2).to_broadcast([ap.shape[0], ap.shape[1], n])


def wait_reuse(eng, sem, value):
    if not isinstance(value, int) or value > 0:
        eng.wait_ge(sem, value)


def pipelined(eng, prologue, body, last=2):
    prologue()
    with eng.Fori(0, (PAIRS - last) // 2) as j:
        body(2 * j, 0, last)
        body(2 * j + 1, 1, last)
    for n in range(PAIRS - last, PAIRS):
        body(n, n % 2, PAIRS - 1 - n)


class Stage:

    def __init__(self, nc, ctx, name):
        self.nc, self.ctx, self.name, self.sems = nc, ctx, name, []

    def sb(self, name, shape, dt=F32):
        return self.ctx.enter_context(self.nc.sbuf_tensor(f"{self.name}_{name}", shape, dt))

    def bank(self, name):
        return self.ctx.enter_context(self.nc.psum_tensor(f"{self.name}_{name}", [128, 512], F32))

    def sem(self, name):
        sem = self.ctx.enter_context(self.nc.semaphore(f"{self.name}_{name}"))
        self.sems.append(sem)
        return sem

    def clear_semaphores(self):
        with self.nc.Block() as block:
            @block.gpsimd
            def _(pool):
                for sem in self.sems:
                    pool.sem_clear(sem)


class Norm:

    def __init__(self, nc, st, res, by_pool=False, by_act=False, keep_var=False):
        self.nc, self.res, self.by_pool, self.by_act, self.keep_var = nc, res, by_pool, by_act, keep_var
        self.sum, self.sum_sq = st.sb("ln_sum", [128, 2, NT]), st.sb("ln_sum_sq", [128, 2, NT])
        self.sq, self.var = st.sb("ln_sq", [128, PAIR]), st.sb("ln_var", [128, 2, NT])
        self.handed_over = st.sem("ln_handed_over")
        if by_pool:
            self.last_sq = st.sb("ln_last_sq", [128, PAIR])
        if by_act:
            self.squares_done = st.sem("ln_squares_done")
        self.rstd_done = st.sem("ln_rstd_done")

    def on_pool(self, n):
        return self.by_pool and not (isinstance(n, int) and n == PAIRS - 1)

    def stats(self, dve, n, p):
        nc, R = self.nc, self.res
        h = R.h[0:HT, bass.ds(n * PAIR, PAIR)]
        hc = R.hc[0:HT, bass.ds(n * PAIR, PAIR)]
        nc.vector.reduce_sum(self.sum[0:HT, p, :], split(h, t=NT), axis=AX_X)
        dve.drain()
        centred = nc.vector.scalar_tensor_tensor(out=split(hc, t=NT), in0=spread(self.sum[0:HT, p, :], D),
                                                 scalar=-1.0 / D, in1=split(h, t=NT), op0=ALU.mult, op1=ALU.add)
        if self.by_act or self.on_pool(n):
            centred.then_inc(self.handed_over, 1)
            return
        sq = self.last_sq if self.by_pool else self.sq
        dve.drain()
        nc.vector.tensor_tensor(sq[0:HT, :], hc, hc, ALU.mult)
        dve.drain()
        nc.vector.reduce_sum(self.sum_sq[0:HT, p, :], split(sq[0:HT, :], t=NT), axis=AX_X)
        dve.drain()
        dve.wait_ge(self.rstd_done, n + 1)
        nc.vector.tensor_scalar(self.var[0:HT, p, :], self.sum_sq[0:HT, p, :], 1.0 / D, EPS, ALU.mult, ALU.add)\
            .then_inc(self.handed_over, 1)
        if self.keep_var:
            nc.vector.tensor_scalar(R.var[0:HT, bass.ds(n * NT, NT)], self.sum_sq[0:HT, p, :], 1.0 / D, None,
                                    ALU.mult)

    def squares(self, act, n, p):
        act.wait_ge(self.handed_over, n + 1)
        act.wait_ge(self.rstd_done, n + 1)
        act.nop(nofuse=True)
        for t in range(NT):
            done = self.nc.scalar.activation(self.sq[0:HT, t * D:(t + 1) * D],
                                             self.res.hc[0:HT, bass.ds(n * PAIR + t * D, D)], ACT.Square,
                                             accum_out=self.sum_sq[0:HT, p, t:t + 1])
        done.then_inc(self.squares_done, 1)
        act.drain()

    def rstd(self, pool, n, p):
        nc, R = self.nc, self.res
        pool.wait_ge(self.squares_done if self.by_act else self.handed_over, n + 1)
        if self.by_act:
            pool.nop(nofuse=True)
            nc.gpsimd.tensor_scalar(self.var[0:HT, p, :], self.sum_sq[0:HT, p, :], 1.0 / D, EPS, ALU.mult, ALU.add)
            pool.drain()
        if self.on_pool(n):
            hc = R.hc[0:HT, bass.ds(n * PAIR, PAIR)]
            pool.nop(nofuse=True)
            nc.gpsimd.tensor_tensor(self.sq[0:HT, :], hc, hc, ALU.mult)
            pool.drain()
            sq, k = split(self.sq[0:HT, :], t=NT), D
            while k > 1:
                k //= 2
                out = sq[:, :, 0:k] if k > 1 else self.sum_sq[0:HT, 0, :].unsqueeze(2)
                nc.gpsimd.tensor_tensor(out, sq[:, :, 0:k], sq[:, :, k:2 * k], ALU.add)
                pool.drain()
            nc.gpsimd.tensor_scalar(self.var[0:HT, p, :], self.sum_sq[0:HT, 0, :], 1.0 / D, EPS, ALU.mult, ALU.add)
            pool.drain()
        nc.gpsimd.tensor_tensor(R.rstd[0:HT, bass.ds(n * NT, NT)], self.var[0:HT, p, :], R.neghalf[0:HT, 0:NT],
                                ALU.pow).then_inc(self.rstd_done, 1)

    def finish(self, pool):
        pool.sem_inc(self.rstd_done, 2)
        with pool.Fori(0, PAIRS // 2 - 1) as j:
            self.rstd(pool, 2 * j, 0)
            self.rstd(pool, 2 * j + 1, 1)
        self.rstd(pool, PAIRS - 2, 0)
        self.rstd(pool, PAIRS - 1, 1)


def normalise(nc, R, n, out):
    return nc.vector.tensor_tensor(split(out, t=NT), split(R.hc[0:HT, bass.ds(n * PAIR, PAIR)], t=NT),
                                   spread(R.rstd[0:HT, bass.ds(n * NT, NT)], D), ALU.mult)


def turn_pair(nc, R, bank, x):
    for smp in range(2):
        mm = nc.tensor.transpose(bank[0:2 * D, smp * HT:(smp + 1) * HT], x[0:HT, smp * 2 * D:(smp + 1) * 2 * D],
                                 R.c128("ident", 0, HT, 0, HT))
    return mm


def half_columns(xT, bank, half):
    return (xT.rearrange("p (s two c) -> p s two c", s=2, two=2)[:, :, half, :],
            bank[half * D:(half + 1) * D, 0:2 * HT].rearrange("p (s c) -> p s c", s=2))


class Head:

    def __init__(self, nc, st, res, twice=False):
        self.nc, self.res, self.twice = nc, res, twice
        self.xn = [st.sb(f"xn{p}", [128, PAIR]) for p in range(2)]
        if twice:
            self.xh = [st.sb(f"xh{p}", [128, W], F32R) for p in range(2)]
            self.xl = [st.sb(f"xl{p}", [128, W], F32R) for p in range(2)]
        else:
            self.x2 = [st.sb(f"x2{p}", [128, W], F32R) for p in range(2)]
        self.turned = st.bank("turned")
        self.xn_ready = st.sem("xn_ready")
        self.turned_ready = st.sem("turned_ready")
        self.high_ready = st.sem("high_ready")
        self.x_ready = st.sem("x_ready")

    def xn_dve(self, dve, n, q):
        normalise(self.nc, self.res, n, self.xn[q][0:HT, :]).then_inc(self.xn_ready, 1)

    def pe(self, pe, n, q):
        pe.wait_ge(self.xn_ready, n + 1)
        wait_reuse(pe, self.x_ready, n)
        turn_pair(self.nc, self.res, self.turned, self.xn[q]).then_inc(self.turned_ready, 1)

    def high_act(self, act, n, q):
        act.wait_ge(self.turned_ready, n + 1)
        x = self.xh[q] if self.twice else self.x2[q]
        for rows in range(2 if self.twice else 1):
            for half in range(2):
                out, in_ = half_columns(x[rows * D:(rows + 1) * D, :], self.turned, half)
                done = self.nc.scalar.copy(out, in_)
        done.then_inc(self.high_ready, 1)

    def low_dve(self, dve, n, q):
        dve.wait_ge(self.high_ready, n + 1)
        high = (self.xh if self.twice else self.x2)[q][0:D, :].bitcast(F32)
        for rows in range(2 if self.twice else 1):
            low = self.xl[q][rows * D:(rows + 1) * D, :] if self.twice else self.x2[q][D:2 * D, :]
            for half in range(2):
                out, in_ = half_columns(low, self.turned, half)
                hi, _ = half_columns(high, self.turned, half)
                done = self.nc.vector.tensor_tensor(out, in_, hi, ALU.subtract)
        done.then_inc(self.x_ready, 1)


def product64(nc, out, R, name, x, start=True, stop=True, a=0, n=128):
    o = R.at64[name][0] + a
    nc.tensor.matmul(out, R.wh[:, o:o + n], x, start=start, stop=False, skip_group_check=True)
    return nc.tensor.matmul(out, R.wl[:, o:o + n], x, start=False, stop=stop, skip_group_check=True)


def product64T(nc, out, R, name, x, a=0, n=None):
    o, size = R.at64[name]
    o, n = o + a, size if n is None else n
    nc.tensor.matmul(out, x, R.wh[:, o:o + n], start=True, stop=False, skip_group_check=True)
    return nc.tensor.matmul(out, x, R.wl[:, o:o + n], start=False, stop=True, skip_group_check=True)


class Tail:

    def __init__(self, nc, st, res, bias=None):
        self.nc, self.res, self.bias = nc, res, bias
        self.yT, self.y = st.bank("yT"), st.bank("y")
        self.flat = st.sb("yT_halves", [128, 2 * HT])
        self.yT_ready, self.flat_ready, self.y_ready, self.y_used = (
            st.sem(k) for k in ("yT_ready", "flat_ready", "y_ready", "y_used"))

    def act(self, act, n):
        act.wait_ge(self.yT_ready, n + 1)
        for half in range(2):
            in_, _ = half_columns(self.yT[0:D, 0:W], self.yT, half)
            out = self.flat[half * D:(half + 1) * D, :].rearrange("p (s c) -> p s c", s=2)
            if self.bias is None:
                done = self.nc.scalar.copy(out, in_)
            else:
                done = self.nc.scalar.activation(out, in_, ACT.Identity, bias=self.res.c128(self.bias, 0, D))
        done.then_inc(self.flat_ready, 1)

    def pe(self, pe, n):
        pe.wait_ge(self.y_used, n + 1)
        pe.wait_ge(self.flat_ready, n + 1)
        for smp in range(2):
            mm = self.nc.tensor.transpose(self.y[0:HT, smp * 2 * D:(smp + 1) * 2 * D],
                                          self.flat[:, smp * HT:(smp + 1) * HT], self.res.c128("ident"))
        mm.then_inc(self.y_ready, 1)

    def first(self, dve):
        dve.sem_inc(self.y_used, 1)

    def residual(self, dve, n, p, ln, relu=False):
        dve.wait_ge(self.y_ready, n + 1)
        y, h = self.y[0:HT, 0:PAIR], hpair(self.res, n)
        if relu:
            self.nc.vector.scalar_tensor_tensor(out=h, in0=y, scalar=0.0, in1=h, op0=ALU.max, op1=ALU.add)\
                .then_inc(self.y_used, 1)
        else:
            self.nc.vector.tensor_tensor(h, h, y, ALU.add).then_inc(self.y_used, 1)
        dve.drain()
        ln.stats(dve, n, p)


def add(nc, out, lhsT, rhs, stop):
    return nc.tensor.matmul(out, lhsT, rhs, start=False, stop=stop, skip_group_check=True)


def hpair(R, n):
    return R.h[0:HT, bass.ds(n * PAIR, PAIR)]


def tokenizer(nc, R, x, txt, loads, tokw_dram, p64, pqe, pc, notmine):
    with ExitStack() as ctx:
        st = Stage(nc, ctx, "tok")
        ln = Norm(nc, st, R, by_act=True)
        xs = [st.sb(f"x{p}", [128, 2, XM]) for p in range(2)]
        y = [st.bank(f"y{p}") for p in range(2)]
        tokw = st.sb("tokw", [128, KPAR * D])
        raw64, rawqe = st.sb("raw64", [128, offsets(PACK64)[1]]), st.sb("rawqe", [128, offsets(PACKQE)[1]])
        rawc, others = st.sb("rawc", [2 * E1, offsets(PACKC)[1]]), st.sb("others", [2 * E1, E1 * H1])
        qeh, pickh = st.sb("qeh", [128, offsets(PACKQE)[1]], F32R), st.sb("pickh", [2 * E1, offsets(PACKC)[1]], F32R)
        pw = st.sb("pw", [128, 9, 2])
        tmp = st.sb("tmp", [128, T])
        ang = st.sb("ang", [128, 8])
        first_loaded, rest_loaded, tok_loaded = st.sem("first_loaded"), st.sem("rest_loaded"), st.sem("tok_loaded")
        high_ready = st.sem("high_ready")
        x_loaded = [st.sem(f"x_loaded{p}") for p in range(2)]
        y_ready, y_used = st.sem("y_ready"), st.sem("y_used")
        consts, angle, turn, unit = st.sem("consts"), st.sem("angle"), st.sem("turn"), st.sem("unit")
        decay_sq, gamma_done = st.sem("decay_sq"), st.sem("gamma_done")
        ctx.callback(st.clear_semaphores)
        block = ctx.enter_context(nc.Block())
        c128 = R.c128
        (consts_load, bias_load), loads = loads, []
        for dst, src in ((raw64, p64), (rawqe, pqe)):
            loads += [(dst[0:D, :], src), (dst[D:2 * D, :], src)]
        for rows in (slice(0, E1), slice(E1, 2 * E1)):
            loads += [(rawc[rows, :], pc), (others[rows, :], notmine)]

        @block.sync
        def _(sp):
            for dst, src in (bias_load, (tokw[:], tokw_dram)):
                sp.dma_start(dst, src).then_inc(tok_loaded, 16)

            def load(n, p):
                sp.wait_ge(y_ready, n - 1)
                sp.dma_start(xs[p][:], x[bass.ds(n, 1)].rearrange("a p s m -> (a p) s m")).then_inc(x_loaded[p], 16)

            for p in range(2):
                sp.dma_start(xs[p][:], x[p]).then_inc(x_loaded[p], 16)
            with sp.Fori(1, PAIRS // 2) as j:
                load(2 * j, 0)
                load(2 * j + 1, 1)

        @block.scalar
        def _(act):
            act.dma_start(*consts_load).then_inc(first_loaded, 16)
            act.wait_ge(first_loaded, 16)
            nc.scalar.activation(ang[:, 0:1], c128("nu_log"), ACT.Exp)
            nc.scalar.activation(ang[:, 1:2], c128("theta_log"), ACT.Exp)
            act.drain()
            nc.scalar.activation(R.lru[:, 0:1], ang[:, 0:1], ACT.Exp, scale=-1.0).then_inc(angle, 1)
            act.wait_ge(turn, 1)
            nc.scalar.activation(ang[:, 4:5], ang[:, 2:3], ACT.Sin)
            nc.scalar.activation(ang[:, 5:6], ang[:, 2:3], ACT.Sin, scale=0.5).then_inc(unit, 1)
            for dst, src in loads:
                act.dma_start(dst, src).then_inc(rest_loaded, 16)
            tokens = R.h[:].rearrange("p (b two d) -> p b two d", two=2, d=D)
            act.dma_start(tokens[PATCHES:HT, 0:B, 0, :], txt[:, 0:HT - PATCHES, :].rearrange("b t d -> t b d"))\
                .then_inc(rest_loaded, 16)
            act.dma_start(tokens[0:HT, 0:B, 1, :], txt[:, HT - PATCHES:, :].rearrange("b t d -> t b d"))\
                .then_inc(rest_loaded, 16)

            def gelu(n, p):
                act.wait_ge(y_ready, n + 1)
                out = R.h[0:PATCHES, bass.ds(n * PAIR, PAIR)].rearrange("p (s two d) -> p s two d", two=2, d=D)
                act.nop(nofuse=True)
                nc.scalar.activation(out[:, :, 0, :], split(y[p][0:PATCHES, 0:2 * D], t=2), ACT.Gelu)\
                    .then_inc(y_used, 1)

            def pro():
                for n in range(4):
                    gelu(n, n % 2)

            def body(n, p, more):
                if more == 4:
                    gelu(n + 4, p)
                ln.squares(act, n, p)

            pipelined(act, pro, body, last=4)

        @block.tensor
        def _(pe):
            pe.wait_ge(consts, 1)
            pe.wait_ge(tok_loaded, 32)

            def patches(n, p, turn_no):
                pe.wait_ge(x_loaded[p], 16 * turn_no)
                pe.wait_ge(y_used, n + 1)
                nc.tensor.matmul(y[p][0:PATCHES, 0:2 * D], R.ones[0:1, 0:PATCHES], R.c1("tok_b", 0, 1),
                                 start=True, stop=False, skip_group_check=True)
                for s in range(2):
                    for c in range(KPAR):
                        k = 128 if c < KPAR - 1 else D
                        mm = add(nc, y[p][0:PATCHES, s * D:(s + 1) * D],
                                 xs[p][0:k, s, c:c + PSTEP * (PATCHES - 1) + 1:PSTEP],
                                 tokw[0:k, c * D:(c + 1) * D], stop=c == KPAR - 1)
                mm.then_inc(y_ready, 1)

            with pe.Fori(0, PAIRS // 2) as j:
                patches(2 * j, 0, j + 1)
                patches(2 * j + 1, 1, j + 1)

        @block.vector
        def _(dve):
            nc.vector.memset(R.neghalf[:], -0.5)
            nc.vector.memset(R.gates[:, PAIRS], 0.0)
            nc.vector.memset(R.half[:], 0.5)
            nc.vector.memset(R.ones[:], 1.0).then_inc(consts, 1)
            dve.sem_inc(y_used, 2)
            dve.wait_ge(angle, 1)
            nc.vector.tensor_tensor(ang[:, 6:7], R.lru[:, 0:1], R.lru[:, 0:1], ALU.mult)
            nc.vector.tensor_scalar(ang[:, 3:4], ang[:, 1:2], 1.0 / (2 * np.pi), None, ALU.mult)
            dve.drain()
            nc.vector.tensor_scalar(ang[:, 7:8], ang[:, 6:7], -1.0, 1.0, ALU.mult, ALU.add).then_inc(decay_sq, 1)
            nc.vector.tensor_scalar(ang[:, 3:4], ang[:, 3:4], 12582912.0, None, ALU.add)
            dve.drain()
            nc.vector.tensor_scalar(ang[:, 3:4], ang[:, 3:4], -12582912.0, None, ALU.add)
            dve.drain()
            nc.vector.scalar_tensor_tensor(out=ang[:, 2:3], in0=ang[:, 3:4], scalar=-6.28125, in1=ang[:, 1:2],
                                           op0=ALU.mult, op1=ALU.add)
            dve.drain()
            nc.vector.scalar_tensor_tensor(out=ang[:, 2:3], in0=ang[:, 3:4], scalar=-(2 * np.pi - 6.28125),
                                           in1=ang[:, 2:3], op0=ALU.mult, op1=ALU.add).then_inc(turn, 1)
            nc.vector.memset(R.decay[:], 1.0)
            dve.drain()
            nc.vector.tensor_scalar(R.decay[:], R.decay[:], R.lru[:, 0:1], None, ALU.mult)
            dve.drain()
            nc.vector.memset(R.decay[:, 0:W:T], 0.0)
            nc.vector.tensor_scalar(R.negC[:, 0:2 * D], c128("C_re2"), -1.0, None, ALU.mult)
            nc.vector.tensor_scalar(R.negC[:, 2 * D:4 * D], c128("C_im2"), -1.0, None, ALU.mult)
            nc.vector.memset(R.cos[:, 0:1], 1.0)
            nc.vector.memset(R.sin[:, 0:1], 0.0)
            dve.wait_ge(unit, 1)
            nc.vector.tensor_copy(pw[:, 0, 1:2], ang[:, 4:5])
            nc.vector.tensor_tensor(ang[:, 3:4], ang[:, 5:6], ang[:, 5:6], ALU.mult)
            dve.drain()
            nc.vector.tensor_scalar(pw[:, 0, 0:1], ang[:, 3:4], -2.0, 1.0, ALU.mult, ALU.add)
            m, k = 1, 0
            while m < T:
                n = min(m, T - m)
                dve.drain()
                c, s = pw[:, k, 0:1], pw[:, k, 1:2]
                nc.vector.tensor_tensor(ang[:, 3:4], c, c, ALU.mult)
                dve.drain()
                nc.vector.scalar_tensor_tensor(out=ang[:, 3:4], in0=s, scalar=s, in1=ang[:, 3:4],
                                               op0=ALU.mult, op1=ALU.add)
                dve.drain()
                nc.vector.tensor_scalar(ang[:, 3:4], ang[:, 3:4], -0.5, 1.5, ALU.mult, ALU.add)
                dve.drain()
                nc.vector.tensor_scalar(pw[:, k, 0:2], pw[:, k, 0:2], ang[:, 3:4], None, ALU.mult)
                dve.drain()
                nc.vector.tensor_scalar(tmp[:, 0:n], R.sin[:, 0:n], s, None, ALU.mult)
                nc.vector.tensor_scalar(R.sin[:, m:m + n], R.sin[:, 0:n], c, None, ALU.mult)
                nc.vector.tensor_tensor(pw[:, k + 1, 0:1], s, s, ALU.mult)
                nc.vector.tensor_scalar(pw[:, k + 1, 1:2], c, s, 2.0, ALU.mult, ALU.mult)
                dve.drain()
                nc.vector.scalar_tensor_tensor(out=R.cos[:, m:m + n], in0=R.cos[:, 0:n], scalar=c, in1=tmp[:, 0:n],
                                               op0=ALU.mult, op1=ALU.subtract)
                nc.vector.scalar_tensor_tensor(out=R.sin[:, m:m + n], in0=R.cos[:, 0:n], scalar=s,
                                               in1=R.sin[:, m:m + n], op0=ALU.mult, op1=ALU.add)
                nc.vector.scalar_tensor_tensor(out=pw[:, k + 1, 0:1], in0=c, scalar=c, in1=pw[:, k + 1, 0:1],
                                               op0=ALU.mult, op1=ALU.subtract)
                m, k = m + n, k + 1
            dve.wait_ge(gamma_done, 1)
            nc.vector.tensor_scalar(R.lru[:, 2:3], R.lru[:, 1:2], 1.0, c128("bh_re"), ALU.add, ALU.mult)
            nc.vector.tensor_scalar(R.lru[:, 3:4], R.lru[:, 1:2], 1.0, c128("bh_im"), ALU.add, ALU.mult)
            dve.wait_ge(rest_loaded, 16 * (len(loads) + 2))
            nc.vector.tensor_copy(R.wh[:], raw64[:]).then_inc(high_ready, 1)
            nc.vector.tensor_tensor(rawc[:, 0:E1 * H1], rawc[:, 0:E1 * H1], others[:], ALU.add)
            dve.drain()
            nc.vector.tensor_copy(R.qe[0:D, :], rawqe[0:D, :])
            nc.vector.tensor_copy(qeh[D:2 * D, :], rawqe[D:2 * D, :])
            nc.vector.tensor_copy(R.pick[0:E1, :], rawc[0:E1, :])
            nc.vector.tensor_copy(pickh[E1:2 * E1, :], rawc[E1:2 * E1, :])
            nc.vector.memset(R.pick[2 * E1:128, :].bitcast(F32), 0.0)
            nc.vector.tensor_copy(R.pick_expert[:], c128("pick_expert"))
            for i, b in enumerate(("L1b2", "L2b2", "L2b2")):
                nc.vector.tensor_copy(R.b2h[:, i * D:(i + 1) * D], c128(b))
            dve.drain()
            nc.vector.tensor_tensor(R.qe[D:2 * D, :], rawqe[D:2 * D, :], qeh[D:2 * D, :].bitcast(F32), ALU.subtract)
            nc.vector.tensor_tensor(R.pick[E1:2 * E1, :], rawc[E1:2 * E1, :], pickh[E1:2 * E1, :].bitcast(F32),
                                    ALU.subtract)
            for i, b in enumerate(("L1b2", "L2b2", "L2b2")):
                nc.vector.tensor_tensor(R.b2l[:, i * D:(i + 1) * D], c128(b),
                                        R.b2h[:, i * D:(i + 1) * D].bitcast(F32), ALU.subtract)

            def stats(n, p):
                dve.wait_ge(y_used, n + 3)
                ln.stats(dve, n, p)

            with dve.Fori(0, PAIRS // 2) as j:
                stats(2 * j, 0)
                stats(2 * j + 1, 1)

        @block.gpsimd
        def _(pool):
            pool.wait_ge(consts, 1)
            pool.wait_ge(decay_sq, 1)
            nc.gpsimd.tensor_tensor(R.lru[:, 1:2], ang[:, 7:8], R.half[:, 0:1], ALU.pow).then_inc(gamma_done, 1)
            pool.wait_ge(high_ready, 1)
            nc.gpsimd.tensor_tensor(R.wl[:], raw64[:], R.wh[:].bitcast(F32), ALU.subtract)
            ln.finish(pool)


def lru(nc, R):
    with ExitStack() as ctx:
        st = Stage(nc, ctx, "lru")
        ln, head, tail = Norm(nc, st, R, by_act=True), Head(nc, st, R), Tail(nc, st, R, bias="lru_b")
        u = [st.bank("u_re"), st.bank("u_im")]
        v = [[st.sb(f"v{i}{p}", [128, W]) for i in range(2)] for p in range(2)]
        a = [st.sb(f"a{i}", [128, W]) for i in range(2)]
        m = [st.sb(f"m{i}", [128, W]) for i in range(4)]
        g = [st.sb(f"g{i}", [128, W]) for i in range(2)]
        out = [[st.sb(f"out{k}{p}", [128, W]) for k in range(4)] for p in range(2)]
        u_ready, v_ready = st.sem("u_ready"), st.sem("v_ready")
        pool_in, scanned, pool_out = st.sem("pool_in"), st.sem("scanned"), st.sem("pool_out")
        states = st.sem("states")
        block = ctx.enter_context(nc.Block())
        two = lambda ap: split(ap[:, 0:W], t=2)
        table = lambda t: t[:, 0:T].unsqueeze(1).to_broadcast([128, 2, T])
        COS, SIN = table(R.cos), table(R.sin)

        @block.vector
        def _(dve):
            def rotate(n, q):
                dve.wait_ge(v_ready, n + 1)
                nc.vector.tensor_tensor(two(m[0]), two(v[q][0]), COS, ALU.mult)
                nc.vector.tensor_tensor(two(m[1]), two(v[q][1]), SIN, ALU.mult)
                nc.vector.tensor_tensor(two(m[2]), two(v[q][1]), COS, ALU.mult)
                dve.drain()
                nc.vector.tensor_tensor(a[0][:], m[0][:], m[1][:], ALU.add)
                dve.wait_ge(pool_in, n + 1)
                nc.vector.tensor_tensor(a[1][:], m[2][:], m[3][:], ALU.subtract)
                dve.drain()

            def scan(n, q):
                nc.vector.tensor_tensor_scan(g[0][:], R.decay[:], a[0][:], 0.0, ALU.mult, ALU.add)
                nc.vector.tensor_tensor_scan(g[1][:], R.decay[:], a[1][:], 0.0, ALU.mult, ALU.add).then_inc(scanned, 1)
                dve.drain()
                nc.vector.tensor_tensor(two(out[q][0]), two(g[0]), COS, ALU.mult)
                nc.vector.tensor_tensor(two(out[q][1]), two(g[1]), SIN, ALU.mult)
                nc.vector.tensor_tensor(two(out[q][2]), two(g[0]), SIN, ALU.mult).then_inc(states, 1)

            def pro():
                tail.first(dve)
                head.xn_dve(dve, 0, 0)
                head.xn_dve(dve, 1, 1)
                head.low_dve(dve, 0, 0)
                head.low_dve(dve, 1, 1)
                rotate(0, 0)
                scan(0, 0)

            def body(n, p, more):
                if more > 1:
                    head.xn_dve(dve, n + 2, p)
                if more:
                    rotate(n + 1, 1 - p)
                if more > 1:
                    head.low_dve(dve, n + 2, p)
                if more:
                    scan(n + 1, 1 - p)
                tail.residual(dve, n, p, ln)

            pipelined(dve, pro, body)

        @block.gpsimd
        def _(pool):
            def front(n, q):
                pool.wait_ge(v_ready, n + 1)
                nc.gpsimd.tensor_tensor(two(m[3]), two(v[q][0]), SIN, ALU.mult).then_inc(pool_in, 1)
                pool.wait_ge(scanned, n + 1)
                nc.gpsimd.tensor_tensor(two(out[q][3]), two(g[1]), COS, ALU.mult).then_inc(pool_out, 1)

            def body(n, p, more):
                if more:
                    front(n + 1, 1 - p)
                ln.rstd(pool, n, p)

            pool.sem_inc(ln.rstd_done, 2)
            pipelined(pool, lambda: front(0, 0), body)

        @block.scalar
        def _(act):
            def front(n, q):
                head.high_act(act, n, q)
                act.wait_ge(u_ready, n + 1)
                nc.scalar.activation(v[q][0][:], u[0][:, 0:W], ACT.Identity, bias=R.lru[:, 2:3], scale=R.lru[:, 1:2])
                nc.scalar.activation(v[q][1][:], u[1][:, 0:W], ACT.Identity, bias=R.lru[:, 3:4], scale=R.lru[:, 1:2])\
                    .then_inc(v_ready, 1)

            def pro():
                front(0, 0)
                front(1, 1)

            def body(n, p, more):
                tail.act(act, n)
                if more > 1:
                    front(n + 2, p)
                ln.squares(act, n, p)

            pipelined(act, pro, body)

        @block.tensor
        def _(pe):
            def front(n, q):
                head.pe(pe, n, q)
                pe.wait_ge(head.x_ready, n + 1)
                wait_reuse(pe, v_ready, n)
                for i, w in enumerate(("B_reT", "B_imT")):
                    mm = product64(nc, u[i][:, 0:W], R, w, head.x2[q][:])
                mm.then_inc(u_ready, 1)

            def pro():
                front(0, 0)
                front(1, 1)

            def body(n, p, more):
                product64(nc, tail.yT[:, 0:W], R, "DT2", head.x2[p][:], stop=False)
                pe.wait_ge(states, n + 1)
                pe.wait_ge(pool_out, n + 1)
                C = [R.c128("C_re2"), R.negC[:, 0:2 * D], R.negC[:, 2 * D:4 * D], R.negC[:, 2 * D:4 * D]]
                for k in range(4):
                    mm = add(nc, tail.yT[:, 0:W], C[k], out[p][k][:], stop=k == 3)
                mm.then_inc(tail.yT_ready, 1)
                if more > 1:
                    front(n + 2, p)
                tail.pe(pe, n)

            pipelined(pe, pro, body)


def top1(nc, R):
    with ExitStack() as ctx:
        st = Stage(nc, ctx, "top1")
        ln, head, tail = Norm(nc, st, R, by_pool=True), Head(nc, st, R), Tail(nc, st, R)
        NC, NB = 4, 3
        lg, ohT = st.bank("logits"), st.bank("chosenT")
        hb = [st.bank(f"hidden{c}") for c in range(NB)]
        hid = [st.sb(f"hid{c}", [128, W]) for c in range(NC)]
        picked = [st.sb(f"picked{p}", [128, W], F32R) for p in range(2)]
        lgs, eq, top = st.sb("lgs", [128, NT * E1]), st.sb("eq", [128, NT * E1]), st.sb("top", [128, 2, NT])
        oh = st.sb("chosen", [128, NT, 128])
        lg_ready, oh_ready, ohT_ready, picked_ready = (st.sem(k) for k in ("lg_ready", "oh_ready", "ohT_ready",
                                                                           "picked_ready"))
        h_ready, relu_act, relu_dve = st.sem("h_ready"), st.sem("relu_act"), st.sem("relu_dve")
        block = ctx.enter_context(nc.Block())
        desc = split(R.c128("desc32", 0, HT), t=NT)
        o_pick = lambda a, n: R.pick[:, a:a + n]

        @block.vector
        def _(dve):
            def choose(n):
                dve.wait_ge(lg_ready, n + 1)
                l4, e4 = split(lgs[0:HT, :], t=NT), split(eq[0:HT, :], t=NT)
                nc.vector.tensor_tensor(lgs[0:HT, :], lg[0:HT, 0:NT * E1], R.c128("router_b", 0, HT), ALU.add)
                dve.drain()
                nc.vector.reduce_max(top[0:HT, 0, :], l4, axis=AX_X)
                dve.drain()
                nc.vector.tensor_tensor(e4, l4, spread(top[0:HT, 0, :], E1), ALU.is_equal)
                dve.drain()
                nc.vector.tensor_tensor(e4, e4, desc, ALU.mult)
                dve.drain()
                nc.vector.reduce_max(top[0:HT, 1, :], e4, axis=AX_X)
                dve.drain()
                for copy in range(2):
                    done = nc.vector.tensor_tensor(oh[0:HT, :, copy * E1:(copy + 1) * E1], e4,
                                                   spread(top[0:HT, 1, :], E1), ALU.is_equal)
                done.then_inc(oh_ready, 1)

            def pro():
                tail.first(dve)
                nc.vector.memset(oh[:], 0.0)
                head.xn_dve(dve, 0, 0)
                head.xn_dve(dve, 1, 1)
                head.low_dve(dve, 0, 0)
                choose(0)

            def body(n, p, more):
                if more > 1:
                    head.xn_dve(dve, n + 2, p)
                if more:
                    head.low_dve(dve, n + 1, 1 - p)
                for c in (1, 3):
                    dve.wait_ge(h_ready, n * NC + c + 1)
                    nc.vector.tensor_scalar(hid[c][:], hb[c % NB][:, 0:W], 0.0, None, ALU.max).then_inc(relu_dve, 1)
                if more:
                    choose(n + 1)
                tail.residual(dve, n, p, ln, relu=True)

            pipelined(dve, pro, body)

        @block.gpsimd
        def _(pool):
            ln.finish(pool)

        @block.scalar
        def _(act):
            def put(n, q):
                act.wait_ge(ohT_ready, n + 1)
                nc.scalar.copy(picked[q][:], ohT[:, 0:W]).then_inc(picked_ready, 1)

            def pro():
                head.high_act(act, 0, 0)
                put(0, 0)

            def body(n, p, more):
                if more:
                    head.high_act(act, n + 1, 1 - p)
                for c in (0, 2):
                    act.wait_ge(h_ready, n * NC + c + 1)
                    nc.scalar.activation(hid[c][:], hb[c % NB][:, 0:W], ACT.Relu).then_inc(relu_act, 1)
                tail.act(act, n)
                if more:
                    put(n + 1, 1 - p)

            pipelined(act, pro, body)

        @block.tensor
        def _(pe):
            def logits(n, q):
                pe.wait_ge(head.x_ready, n + 1)
                for t in range(NT):
                    mm = product64T(nc, lg[0:HT, t * E1:(t + 1) * E1], R, "routerT",
                                    head.x2[q][:, t * HT:(t + 1) * HT])
                mm.then_inc(lg_ready, 1)

            def turn_choice(n):
                pe.wait_ge(oh_ready, n + 1)
                for t in range(NT):
                    mm = nc.tensor.transpose(ohT[:, t * HT:(t + 1) * HT], oh[0:HT, t, :], R.c128("ident", 0, HT, 0, HT))
                mm.then_inc(ohT_ready, 1)

            def pro():
                head.pe(pe, 0, 0)
                logits(0, 0)
                turn_choice(0)

            def body(n, p, more):
                if more:
                    head.pe(pe, n + 1, 1 - p)
                pe.wait_ge(picked_ready, n + 1)
                for c in range(NC):
                    if c == NB:
                        pe.wait_ge(relu_act, 2 * n + 1)
                    product64(nc, hb[c % NB][:, 0:W], R, "L0W1", head.x2[p][:], stop=False, a=c * 128)
                    add(nc, hb[c % NB][:, 0:W], o_pick(c * 128, 128), picked[p][:], stop=True).then_inc(h_ready, 1)
                if more:
                    logits(n + 1, 1 - p)
                nc.tensor.matmul(tail.yT[:, 0:W], o_pick(E1 * H1, 128), picked[p][:], start=True, stop=False,
                                 skip_group_check=True)
                pe.wait_ge(relu_act, 2 * n + 2)
                pe.wait_ge(relu_dve, 2 * n + 2)
                for c in range(NC):
                    mm = add(nc, tail.yT[0:D, 0:W], R.c128("L0W2", 0, 128, c * D, D), hid[c][:], stop=c == NC - 1)
                mm.then_inc(tail.yT_ready, 1)
                if more:
                    turn_choice(n + 1)
                tail.pe(pe, n)

            pipelined(pe, pro, body)


class Contexts:

    def __init__(self, nc, st, ctx_dram):
        self.dram = ctx_dram
        self.sb = [st.sb(f"c{p}", [128, 2, 4, T]) for p in range(2)]
        self.loaded = [st.sem(f"loaded{p}") for p in range(2)]

    def load(self, sp, n, p):
        for smp in range(2):
            sp.dma_start(self.sb[p][:, smp], self.dram[bass.ds(2 * n + smp, 1)]
                         .rearrange("s two t c -> s (two t c)")
                         .rearrange("s (c p t) -> p (s c) t", p=128, t=T)).then_inc(self.loaded[p], 16)


def attention(nc, R, v_dram, ctx_dram):
    with ExitStack() as ctx:
        contexts = Contexts(nc, Stage(nc, ctx, "attn"), ctx_dram)
        mqa(nc, R, v_dram, ctx_dram, contexts)
        mqa_out(nc, R, contexts)


def mqa(nc, R, v_dram, ctx_dram, contexts):
    with ExitStack() as ctx:
        st = Stage(nc, ctx, "mqa")
        head = Head(nc, st, R)
        s = [st.bank(f"s{i}") for i in range(3)]
        pt = [st.bank(f"pt{i}") for i in range(2)]
        cxT, cx = st.bank("cxT"), st.bank("cx")
        kh = [st.sb(f"kh{p}", [128, W], F32R) for p in range(2)]
        kl = [st.sb(f"kl{p}", [128, W], F32R) for p in range(2)]
        q2 = [[st.sb(f"q{h}{p}", [128, W], F32R) for h in range(NH)] for p in range(2)]
        vT = st.sb("vT", [64, W])
        v = [st.sb(f"v{p}", [128, 2, 2, KD]) for p in range(2)]
        prob = [st.sb(f"prob{i}", [128, 2 * T]) for i in range(2)]
        probT = [st.sb(f"probT{i}", [128, 2 * T]) for i in range(2)]
        negm = [st.sb(f"negm{i}", [128, 2]) for i in range(3)]
        sums = [st.sb(f"sums{i}", [128, NH]) for i in range(2)]
        inv = st.sb("inv", [128, NH])
        cxTs = [st.sb(f"cxTs{i}", [128, T]) for i in range(2)]
        cxs = [st.sb(f"cxs{i}", [128, NH * KD]) for i in range(2)]
        f_ready, f_act, f_dve = st.sem("front_ready"), st.sem("front_act"), st.sem("front_dve")
        v_out, v_in = st.sem("v_out"), st.sem("v_in")
        s_ready, m_ready, e_ready = st.sem("s_ready"), st.sem("m_ready"), st.sem("e_ready")
        pt_ready, pts_ready, av_done = st.sem("pt_ready"), st.sem("pts_ready"), st.sem("av_done")
        pts_act = st.sem("pts_act")
        cxT_done, cx_turned = st.sem("cxT_done"), st.sem("cx_turned")
        cx_ready, cx_stored = st.sem("cx_ready"), [st.sem(f"cx_stored{i}") for i in range(2)]
        block = ctx.enter_context(nc.Block())
        UNITS, SCALE = 16, 1.0 / float(np.sqrt(np.float32(KD // NH)))
        heads = lambda hp: [hp // 2 * 4 + hp % 2, hp // 2 * 4 + hp % 2 + 2]
        FIRST, LATER = [cxT, cx, s[0], s[1], s[2], pt[0]], [head.turned] * 6
        STEPS = [0, 2, 5, 7, 9, 11]
        FA, FD = 10, 9
        BY_ACT = [2, 6, 10, 14]
        AHEAD = 3

        def unit(n, p, u):
            return (n, p, u) if u < UNITS else (n + 1, 1 - p, u - UNITS)

        @block.tensor
        def _(pe):
            def front(n, p, i, bank):
                name, a = (("WkT2", 0), ("WvT2", 0))[i] if i < 2 else ("WqT", (i - 2) * 128)
                product64(nc, bank[i][:, 0:W], R, name, head.x2[p][:], a=a).then_inc(f_ready, 1)

            def front_later(n, p, i):
                if i == 0:
                    pe.wait_ge(head.x_ready, n + 1)
                elif i == 2:
                    pe.wait_ge(f_act, FA * n + 2)
                else:
                    pe.wait_ge(f_dve, FD * n + (1 if i == 1 else 2 * i - 3))
                front(n, p, i, LATER)

            def front_done(n):
                pe.wait_ge(f_act, FA * (n + 1))
                pe.wait_ge(f_dve, FD * (n + 1))

            def scores(n, p, u):
                t, hp = u // 4, u % 4
                smp = t // 2
                for k in range(2):
                    o, q = s[u % 3][0:HT, k * T:(k + 1) * T], q2[p][heads(hp)[k]][:, t * HT:(t + 1) * HT]
                    nc.tensor.matmul(o, q, kh[p][:, smp * T:(smp + 1) * T], start=True, stop=False,
                                     skip_group_check=True)
                    mm = add(nc, o, q, kl[p][:, smp * T:(smp + 1) * T], stop=True)
                mm.then_inc(s_ready, 1)

            def turn(n, p, u):
                pe.wait_ge(e_ready, UNITS * n + u + 1)
                for k in range(2):
                    for c in range(2):
                        mm = nc.tensor.transpose(pt[u % 2][0:HT, (2 * c + k) * HT:(2 * c + k + 1) * HT],
                                                 prob[u % 2][0:HT, (2 * k + c) * HT:(2 * k + c + 1) * HT],
                                                 R.c128("ident", 0, HT, 0, HT))
                mm.then_inc(pt_ready, 1)

            def values(n, p, u):
                smp = u // 8
                if u in BY_ACT:
                    pe.wait_ge(pts_act, len(BY_ACT) * n + BY_ACT.index(u) + 1)
                else:
                    pe.wait_ge(pts_ready, (UNITS - len(BY_ACT)) * n + u + 1 - sum(a < u for a in BY_ACT))
                if u == 0:
                    pe.wait_ge(v_in, 32 * (n + 1))
                if u >= 2 and u % 2 == 0:
                    pe.wait_ge(cxT_done, UNITS // 2 * n + u // 2)
                for c in range(2):
                    mm = nc.tensor.matmul(cxT[u % 2 * KD:(u % 2 + 1) * KD, 0:T], v[p][0:HT, smp, c, :],
                                          probT[u % 2][0:HT, c * T:(c + 1) * T], start=c == 0, stop=c == 1,
                                          skip_group_check=True)
                mm.then_inc(av_done, 1)

            def turn_back(n, u):
                t, m = u // 4, u % 4 // 2
                pe.wait_ge(cxT_done, UNITS // 2 * n + (u + 1) // 2)
                if m == 0 and t > 0:
                    pe.wait_ge(cx_ready, NT * n + t)
                for k in range(2):
                    mm = nc.tensor.transpose(cx[0:HT, (2 * m + k) * 2 * KD:(2 * m + k + 1) * 2 * KD],
                                             cxTs[u // 2 % 2][:, k * HT:(k + 1) * HT], R.c128("ident"))
                mm.then_inc(cx_turned, 1)

            def pro():
                head.pe(pe, 0, 0)
                pe.wait_ge(head.x_ready, 1)
                for i in range(6):
                    front(0, 0, i, FIRST)
                front_done(0)
                for u in range(AHEAD):
                    scores(0, 0, u)
                turn(0, 0, 0)
                scores(0, 0, AHEAD)

            def body(n, p, more):
                if more:
                    head.pe(pe, n + 1, 1 - p)
                for u in range(UNITS):
                    if u == UNITS - 1:
                        values(n, p, u)
                    if u + 1 < UNITS or more:
                        turn(*unit(n, p, u + 1))
                        if u + 1 + AHEAD < UNITS or u == UNITS - 1:
                            scores(*unit(n, p, u + 1 + AHEAD))
                    if u == UNITS - 2 and more:
                        front_done(n + 1)
                        for first in range(AHEAD):
                            scores(n + 1, 1 - p, first)
                    if u in STEPS and more:
                        front_later(n + 1, 1 - p, STEPS.index(u))
                    if u < UNITS - 1:
                        values(n, p, u)
                    if u >= 2 and u % 2 == 0:
                        turn_back(n, u - 1)
                turn_back(n, UNITS - 1)

            pipelined(pe, pro, body)

        @block.scalar
        def _(act):
            def front(n, p, i, bank):
                act.wait_ge(f_ready, 6 * n + i + 1)
                if i == 0:
                    nc.scalar.copy(kh[p][:], bank[i][:, 0:W]).then_inc(f_act, 1)
                elif i == 1:
                    wait_reuse(act, v_out, 16 * n)
                    nc.scalar.copy(vT[:], bank[i][0:KD, 0:W]).then_inc(f_act, 1)
                else:
                    for k in range(2):
                        nc.scalar.activation(q2[p][2 * (i - 2) + k][0:KD, :], bank[i][k * KD:(k + 1) * KD, 0:W],
                                             ACT.Copy, scale=-SCALE).then_inc(f_act, 1)

            def exps(n, p, u):
                t, hp = u // 4, u % 4
                act.wait_ge(m_ready, UNITS * n + u + 1)
                if u >= 2:
                    act.wait_ge(pt_ready, UNITS * n + u - 1)
                for k in range(2):
                    h = heads(hp)[k]
                    e = nc.scalar.activation(prob[u % 2][0:HT, k * T:(k + 1) * T], s[u % 3][0:HT, k * T:(k + 1) * T],
                                             ACT.Exp, bias=negm[u % 3][0:HT, k:k + 1], scale=-1.0,
                                             accum_out=sums[t % 2][0:HT, h:h + 1])
                e.then_inc(e_ready, 1)

            def take(n, u):
                act.wait_ge(pt_ready, UNITS * n + u + 1)
                nc.scalar.copy(probT[u % 2][0:HT, :], pt[u % 2][0:HT, 0:W]).then_inc(pts_act, 1)

            def take_context(n, u):
                act.wait_ge(av_done, UNITS * n + u + 1)
                nc.scalar.copy(cxTs[u // 2 % 2][:], cxT[:, 0:T]).then_inc(cxT_done, 1)

            def pro():
                head.high_act(act, 0, 0)
                for i in range(6):
                    front(0, 0, i, FIRST)
                exps(0, 0, 0)

            def body(n, p, more):
                if more:
                    head.high_act(act, n + 1, 1 - p)
                for u in range(UNITS):
                    if u + 1 < UNITS or more:
                        exps(*unit(n, p, u + 1))
                    if u in BY_ACT:
                        take(n, u)
                    if u - 1 in STEPS and more:
                        front(n + 1, 1 - p, STEPS.index(u - 1), LATER)
                    if u >= 2 and u % 2 == 0:
                        take_context(n, u - 1)
                take_context(n, UNITS - 1)

            pipelined(act, pro, body)

        @block.vector
        def _(dve):
            def front(n, p, i, bank):
                if i == 0:
                    dve.wait_ge(f_act, FA * n + 1)
                    nc.vector.tensor_tensor(kl[p][:], bank[i][:, 0:W], kh[p][:].bitcast(F32), ALU.subtract)\
                        .then_inc(f_dve, 1)
                elif i >= 2:
                    for k in range(2):
                        q = q2[p][2 * (i - 2) + k]
                        dve.wait_ge(f_act, FA * n + 3 + 2 * (i - 2) + k)
                        nc.vector.scalar_tensor_tensor(out=q[KD:2 * KD, :], in0=bank[i][k * KD:(k + 1) * KD, 0:W],
                                                       scalar=-SCALE, in1=q[0:KD, :].bitcast(F32), op0=ALU.mult,
                                                       op1=ALU.subtract).then_inc(f_dve, 1)

            def maxima(n, p, u):
                dve.wait_ge(s_ready, UNITS * n + u + 1)
                nc.vector.tensor_reduce(negm[u % 3][0:HT, :], split(s[u % 3][0:HT, 0:W], t=2), op=ALU.min, axis=AX_X)\
                    .then_inc(m_ready, 1)

            def take(n, u):
                dve.wait_ge(pt_ready, UNITS * n + u + 1)
                nc.vector.tensor_copy(probT[u % 2][0:HT, :], pt[u % 2][0:HT, 0:W]).then_inc(pts_ready, 1)

            def context(n, t):
                dve.wait_ge(cx_turned, UNITS // 2 * n + 2 * t + 2)
                dve.wait_ge(cx_stored[t % 2], 16 * (2 * n + t // 2 + 1))
                nc.vector.reciprocal(inv[0:HT, :], sums[t % 2][0:HT, :])
                dve.drain()
                nc.vector.tensor_tensor(cxs[t % 2][0:HT, :].rearrange("p (h d) -> p h d", h=NH),
                                        cx[0:HT, :].rearrange("p (h d) -> p h d", h=NH),
                                        spread(inv[0:HT, :], KD), ALU.mult).then_inc(cx_ready, 1)

            def pro():
                for stored in cx_stored:
                    dve.sem_inc(stored, 16)
                head.xn_dve(dve, 0, 0)
                head.xn_dve(dve, 1, 1)
                head.low_dve(dve, 0, 0)
                for i in range(6):
                    front(0, 0, i, FIRST)
                for u in range(AHEAD):
                    maxima(0, 0, u)

            def body(n, p, more):
                if more:
                    head.low_dve(dve, n + 1, 1 - p)
                for u in range(UNITS):
                    if u not in BY_ACT:
                        take(n, u)
                    if u % 4 == 1 and u > 1:
                        context(n, u // 4 - 1)
                    if u + AHEAD < UNITS:
                        maxima(n, p, u + AHEAD)
                    elif more:
                        for first in ((), (0,), (1, 2))[u + AHEAD - UNITS]:
                            maxima(n + 1, 1 - p, first)
                    if u - 1 in STEPS and more:
                        front(n + 1, 1 - p, STEPS.index(u - 1), LATER)
                if more > 1:
                    head.xn_dve(dve, n + 2, p)
                context(n, NT - 1)

            pipelined(dve, pro, body)

        @block.sync
        def _(sp):
            def v_round(n, p):
                sp.wait_ge(f_act, FA * n + 2)
                sp.dma_start(v_dram[bass.ds(2 * n, 2)].rearrange("s (c t) -> c s t", c=KD),
                             split(vT[:], t=2)).then_inc(v_out, 16)
                sp.wait_ge(v_out, 16 * (n + 1))
                for smp in range(2):
                    sp.dma_start(v[p][0:HT, smp], v_dram[bass.ds(2 * n + smp, 1)]
                                 .rearrange("s (c t d) -> t (s c) d", c=2, d=KD)).then_inc(v_in, 16)

            def body(n, p, more):
                for t in range(NT):
                    sp.wait_ge(cx_ready, NT * n + t + 1)
                    sp.dma_start(ctx_dram[bass.ds(2 * n + t // 2, 1), t % 2].rearrange("s t c -> (s t) c"),
                                 cxs[t % 2][0:HT, :]).then_inc(cx_stored[t % 2], 16)
                    if t == 0 and more:
                        v_round(n + 1, 1 - p)
                if more == 1:
                    for stored in cx_stored:
                        sp.wait_ge(stored, 16 * (2 * 2 + 1))
                    for q in range(2):
                        contexts.load(sp, q, q)

            pipelined(sp, lambda: v_round(0, 0), body)
            for stored in cx_stored:
                sp.wait_ge(stored, 16 * (2 * PAIRS + 1))


def mqa_out(nc, R, contexts):
    with ExitStack() as ctx:
        st = Stage(nc, ctx, "mqao")
        ln, tail = Norm(nc, st, R, keep_var=True), Tail(nc, st, R)
        c, loaded = contexts.sb, contexts.loaded
        block = ctx.enter_context(nc.Block())

        @block.sync
        def _(sp):
            sp.sem_inc(tail.yT_ready, 1)

            def load(n, p):
                sp.wait_ge(tail.yT_ready, n)
                contexts.load(sp, n, p)

            with sp.Fori(1, PAIRS // 2) as j:
                load(2 * j, 0)
                load(2 * j + 1, 1)

        @block.tensor
        def _(pe):
            def products(n, p, turn):
                pe.wait_ge(loaded[p], 32 * turn)
                wait_reuse(pe, tail.flat_ready, n)
                for k in range(4):
                    mm = nc.tensor.matmul(tail.yT[0:D, 0:W], R.c128("WoT", 0, 128, k * D, D), c[p][:, :, k, :],
                                          start=k == 0, stop=k == 3, skip_group_check=True)
                mm.then_inc(tail.yT_ready, 1)

            products(0, 0, 1)
            with pe.Fori(0, PAIRS // 2 - 1) as j:
                products(2 * j + 1, 1, j + 1)
                tail.pe(pe, 2 * j)
                products(2 * j + 2, 0, j + 2)
                tail.pe(pe, 2 * j + 1)
            products(PAIRS - 1, 1, PAIRS // 2)
            tail.pe(pe, PAIRS - 2)
            tail.pe(pe, PAIRS - 1)

        @block.scalar
        def _(act):
            tail.act(act, 1)
            with act.Fori(1, PAIRS) as n:
                act.wait_ge(tail.y_ready, n)
                tail.act(act, n + 1)

        @block.vector
        def _(dve):
            tail.first(dve)

            with dve.Fori(0, PAIRS // 2) as j:
                tail.residual(dve, 2 * j, 0, ln)
                tail.residual(dve, 2 * j + 1, 1, ln)

        @block.gpsimd
        def _(pool):
            ln.finish(pool)


def top2_route(nc, R, name, gate, biases, own_norm):
    with ExitStack() as ctx:
        st = Stage(nc, ctx, name)
        xn = [st.sb(f"xn{p}", [128, PAIR]) for p in range(2)]
        turned = [st.bank(f"turned{p}") for p in range(2)]
        lg = [st.bank(f"logits{p}") for p in range(2)]
        xT = [st.sb(f"xT{p}", [64, W]) for p in range(2)]
        x2 = [st.sb(f"x2{p}", [128, W], F32R) for p in range(2)]
        ALL = PAIRS * NT
        factor, var = st.sb("factor", [128, ALL]), st.sb("var", [128, ALL])
        lga, eq, o1, o2 = (st.sb(k, [128, ALL * E2]) for k in ("all", "eq", "first", "second"))
        m1, m2, kk, dl, ex, w1, w2 = (st.sb(k, [128, ALL]) for k in ("m1", "m2", "kk", "dl", "ex", "w1", "w2"))
        high = st.sb("gates_high", [128, ALL * E2], F32R)
        xn_ready, turned_ready, high_ready, x_ready = (st.sem(k) for k in ("xn_ready", "turned_ready", "high_ready",
                                                                           "x_ready"))
        lg_ready, var_ready, rs_ready = st.sem("lg_ready"), st.sem("var_ready"), st.sem("rs_ready")
        diff_ready, exp_ready = st.sem("diff_ready"), st.sem("exp_ready")
        block = ctx.enter_context(nc.Block())

        @block.vector
        def _(dve):
            def make(n, p):
                scale = factor if own_norm else R.rstd
                nc.vector.tensor_tensor(split(xn[p][0:HT, :], t=NT), split(R.hc[0:HT, bass.ds(n * PAIR, PAIR)], t=NT),
                                        spread(scale[0:HT, bass.ds(n * NT, NT)], D), ALU.mult).then_inc(xn_ready, 1)

            def low(n, p):
                dve.wait_ge(high_ready, n + 1)
                if own_norm:
                    nc.vector.tensor_tensor(x2[p][D:2 * D, :], xT[p][:], x2[p][0:D, :].bitcast(F32), ALU.subtract)\
                        .then_inc(x_ready, 1)
                    return
                for half in range(2):
                    out, in_ = half_columns(x2[p][D:2 * D, :], turned[p], half)
                    hi, _ = half_columns(x2[p][0:D, :].bitcast(F32), turned[p], half)
                    done = nc.vector.tensor_tensor(out, in_, hi, ALU.subtract)
                done.then_inc(x_ready, 1)

            def keep(n, p):
                dve.wait_ge(lg_ready, n + 1)
                out = lga[0:HT, bass.ds(n * NT * E2, NT * E2)]
                bias = [R.c128(b, 0, HT).unsqueeze(1).to_broadcast([HT, NT, E2]) for b in biases]
                dve.nop(nofuse=True)
                nc.vector.tensor_tensor(split(out, t=NT), split(lg[p][0:HT, 0:NT * E2], t=NT), bias[0], ALU.add)
                for b in bias[1:]:
                    dve.drain()
                    nc.vector.tensor_tensor(split(out, t=NT), split(out, t=NT), b, ALU.add)

            def pro():
                if own_norm:
                    nc.vector.tensor_tensor(factor[0:HT, :], R.rstd[0:HT, :], R.rstd[0:HT, :], ALU.mult)
                    dve.drain()
                    nc.vector.tensor_tensor(factor[0:HT, :], R.var[0:HT, :], factor[0:HT, :], ALU.mult)
                    dve.drain()
                    nc.vector.tensor_scalar(var[0:HT, :], factor[0:HT, :], EPS, None, ALU.add).then_inc(var_ready, 1)
                    dve.wait_ge(rs_ready, 1)
                    nc.vector.tensor_tensor(factor[0:HT, :], var[0:HT, :], R.rstd[0:HT, :], ALU.mult)
                    dve.drain()
                make(0, 0)
                make(1, 1)
                low(0, 0)

            def body(n, p, more):
                if more > 1:
                    make(n + 2, p)
                if more:
                    low(n + 1, 1 - p)
                keep(n, p)

            pipelined(dve, pro, body)
            dve.drain()

            l3, e3 = (split(t[0:HT, :], e=E2) for t in (lga, eq))
            desc = split(R.c128("desc8", 0, HT), e=E2)

            def first_of_highest(src, top, out):
                nc.vector.reduce_max(top[0:HT, :], src, axis=AX_X)
                dve.drain()
                nc.vector.tensor_tensor(e3, src, spread(top[0:HT, :], E2), ALU.is_equal)
                dve.drain()
                nc.vector.tensor_tensor(e3, e3, desc, ALU.mult)
                dve.drain()
                nc.vector.reduce_max(kk[0:HT, :], e3, axis=AX_X)
                dve.drain()
                nc.vector.tensor_tensor(out, e3, spread(kk[0:HT, :], E2), ALU.is_equal)
                dve.drain()

            first, second = (split(t[0:HT, :], e=E2) for t in (o1, o2))
            first_of_highest(l3, m1, first)
            nc.vector.scalar_tensor_tensor(out=l3, in0=first, scalar=LOWEST, in1=l3, op0=ALU.mult, op1=ALU.add)
            dve.drain()
            first_of_highest(l3, m2, second)
            nc.vector.tensor_tensor(dl[0:HT, :], m2[0:HT, :], m1[0:HT, :], ALU.subtract).then_inc(diff_ready, 1)
            dve.wait_ge(exp_ready, 1)
            nc.vector.tensor_scalar(w2[0:HT, :], ex[0:HT, :], 1.0, None, ALU.add)
            dve.drain()
            nc.vector.reciprocal(w1[0:HT, :], w2[0:HT, :])
            dve.drain()
            nc.vector.tensor_tensor(w2[0:HT, :], ex[0:HT, :], w1[0:HT, :], ALU.mult)
            nc.vector.tensor_tensor(first, first, spread(w1[0:HT, :], E2), ALU.mult)
            dve.drain()
            nc.vector.tensor_tensor(second, second, spread(w2[0:HT, :], E2), ALU.mult)
            dve.drain()
            nc.vector.tensor_tensor(first, first, second, ALU.add)
            dve.drain()
            nc.vector.tensor_copy(high[0:HT, :], o1[0:HT, :])
            dve.drain()
            by_pair = lambda ap: ap.rearrange("p (n g) -> p n g", n=PAIRS)
            nc.vector.tensor_copy(R.gates[0:HT, 0:PAIRS, 0, :], by_pair(high[0:HT, :].bitcast(F32)))
            nc.vector.tensor_tensor(R.gates[0:HT, 0:PAIRS, 1, :], by_pair(o1[0:HT, :]),
                                    by_pair(high[0:HT, :].bitcast(F32)), ALU.subtract)

        @block.gpsimd
        def _(pool):
            if own_norm:
                pool.wait_ge(var_ready, 1)
                nc.gpsimd.tensor_tensor(var[0:HT, :], var[0:HT, :],
                                        R.neghalf[0:HT, 0:1].to_broadcast([HT, ALL]), ALU.pow).then_inc(rs_ready, 1)

        @block.scalar
        def _(act):
            def put(n, p):
                act.wait_ge(turned_ready, n + 1)
                for half in range(2):
                    if own_norm:
                        out, in_ = half_columns(xT[p][:], turned[p], half)
                        nc.scalar.activation(out, in_, ACT.Identity, bias=R.c128("beta", 0, D),
                                             scale=R.c128("gamma", 0, D))
                    else:
                        out, in_ = half_columns(x2[p][0:D, :], turned[p], half)
                        done = nc.scalar.copy(out, in_)
                if own_norm:
                    act.drain()
                    done = nc.scalar.copy(x2[p][0:D, :], xT[p][:])
                done.then_inc(high_ready, 1)

            def store(n, p):
                act.wait_ge(x_ready, n + 1)
                act.nop(nofuse=True)
                nc.scalar.copy(R.x2[:, bass.ds(n * W, W)], x2[p][:].bitcast(F32))
                act.drain()

            def pro():
                put(0, 0)
                put(1, 1)

            def body(n, p, more):
                store(n, p)
                if more > 1:
                    put(n + 2, p)

            pipelined(act, pro, body)
            act.wait_ge(diff_ready, 1)
            nc.scalar.activation(ex[0:HT, :], dl[0:HT, :], ACT.Exp).then_inc(exp_ready, 1)

        @block.tensor
        def _(pe):
            def turn(n, p):
                pe.wait_ge(xn_ready, n + 1)
                turn_pair(nc, R, turned[p], xn[p]).then_inc(turned_ready, 1)

            def logits(n, p):
                pe.wait_ge(x_ready, n + 1)
                for t in range(NT):
                    mm = product64T(nc, lg[p][0:HT, t * E2:(t + 1) * E2], R, gate, x2[p][:, t * HT:(t + 1) * HT])
                mm.then_inc(lg_ready, 1)

            def pro():
                turn(0, 0)
                turn(1, 1)

            def body(n, p, more):
                logits(n, p)
                if more > 1:
                    turn(n + 2, p)

            pipelined(pe, pro, body)


def top2(nc, R, name, w1, b1, w2, b2, func):
    with ExitStack() as ctx:
        st = Stage(nc, ctx, name)
        ln, tail = Norm(nc, st, R, by_pool=True), Tail(nc, st, R)
        hb, gb = ([st.bank(f"{k}{i}") for i in range(2)] for k in ("hidden", "gates"))
        gT = st.bank("gatesT")
        G = [st.sb(f"G{p}", [128, W], F32R) for p in range(2)]
        hid = [st.sb(f"hid{i}", [128, W]) for i in range(2)]
        gs = st.sb("gates", [128, 128])
        NG = 4
        gated = [st.sb(f"gated{i}", [128, W]) for i in range(NG)]
        gs_ready, gT_ready, G_ready, h_ready, gb_ready, hid_ready, gated_ready = (
            st.sem(k) for k in ("gs_ready", "gT_ready", "G_ready", "h_ready", "gb_ready", "hid_ready", "gated_ready"))
        block = ctx.enter_context(nc.Block())
        AHEAD = 3
        b2_at = {"L1b2": 0, "L2b2": D}[b2]

        @block.tensor
        def _(pe):
            def turn_gates(n):
                pe.wait_ge(gs_ready, n + 1)
                nc.tensor.transpose(gT[:, 0:HT], gs[0:HT, :],
                                    R.c128("ident", 0, HT, 0, HT)).then_inc(gT_ready, 1)

            def hidden(n, p, e):
                pe.wait_ge(gated_ready, n * E2 + e + 1)
                pe.nop(nofuse=True)
                product64(nc, hb[e % 2][:, 0:W], R, w1, R.x2[:, bass.ds(n * W, W)], a=e * H2).then_inc(h_ready, 1)
                if e == 0:
                    pe.wait_ge(G_ready, n + 1)
                nc.tensor.matmul(gb[e % 2][:, 0:W], R.pick_expert[:, e * 128:(e + 1) * 128], G[p][:],
                                 start=True, stop=True).then_inc(gb_ready, 1)

            def pro():
                turn_gates(0)
                for e in range(AHEAD):
                    hidden(0, 0, e)

            def body(n, p, more):
                for k, b in enumerate((R.b2h, R.b2l)):
                    nc.tensor.matmul(tail.yT[:, 0:W], b[:, b2_at:b2_at + 128], G[p][:], start=k == 0, stop=False,
                                     skip_group_check=True)
                for e in range(E2):
                    pe.wait_ge(gated_ready, n * E2 + e + 3)
                    mm = add(nc, tail.yT[0:D, 0:W], R.c128(w2, 0, 128, e * D, D), gated[e % NG][:], stop=e == E2 - 1)
                    if e == 1 and more:
                        turn_gates(n + 1)
                    if e == E2 - 1:
                        mm.then_inc(tail.yT_ready, 1)
                    if e + AHEAD < E2:
                        hidden(n, p, e + AHEAD)
                    elif more:
                        hidden(n + 1, 1 - p, e + AHEAD - E2)
                tail.pe(pe, n)

            pipelined(pe, pro, body)

        @block.scalar
        def _(act):
            def unit(n, e):
                act.wait_ge(h_ready, n * E2 + e + 1)
                nc.scalar.activation(hid[e % 2][:], hb[e % 2][:, 0:W], func, bias=R.c128(b1, 0, 128, e, 1))\
                    .then_inc(hid_ready, 1)

            def take_gates(n):
                nc.scalar.copy(gs[0:HT, :], R.gates[0:HT, bass.ds(n, 2)].rearrange("p n two g -> p (n two g)"))\
                    .then_inc(gs_ready, 1)

            def pro():
                take_gates(0)
                unit(0, 0)
                unit(0, 1)

            def body(n, p, more):
                if more:
                    act.wait_ge(gT_ready, n + 1)
                    act.nop(nofuse=True)
                    take_gates(n + 1)
                for e in range(E2):
                    if e + 2 < E2:
                        unit(n, e + 2)
                    elif more:
                        unit(n + 1, e + 2 - E2)
                tail.act(act, n)

            pipelined(act, pro, body)

        @block.vector
        def _(dve):
            def own_tiles(n, p):
                dve.wait_ge(gT_ready, n + 1)
                nc.vector.tensor_tensor(split(G[p][:], t=NT), gT[:, 0:HT].unsqueeze(1).to_broadcast([128, NT, HT]),
                                        split(R.c128("same_tile"), t=NT), ALU.mult).then_inc(G_ready, 1)

            def weight(n, e):
                dve.wait_ge(hid_ready, n * E2 + e + 1)
                dve.wait_ge(gb_ready, n * E2 + e + 1)
                nc.vector.tensor_tensor(gated[e % NG][:], hid[e % 2][:], gb[e % 2][:, 0:W], ALU.mult)\
                    .then_inc(gated_ready, 1)

            def pro():
                dve.sem_inc(gated_ready, 2)
                tail.first(dve)
                own_tiles(0, 0)
                for e in range(AHEAD):
                    weight(0, e)

            def body(n, p, more):
                for e in range(E2):
                    if e == 2 and more:
                        own_tiles(n + 1, 1 - p)
                    if e + AHEAD < E2:
                        weight(n, e + AHEAD)
                    elif more and e < E2 - 1:
                        weight(n + 1, e + AHEAD - E2)
                tail.residual(dve, n, p, ln)
                if more:
                    weight(n + 1, AHEAD - 1)

            pipelined(dve, pro, body)

        @block.gpsimd
        def _(pool):
            ln.finish(pool)


def quadratic(nc, R):
    with ExitStack() as ctx:
        st = Stage(nc, ctx, "quad")
        ln, head, tail = Norm(nc, st, R, by_pool=True), Head(nc, st, R, twice=True), Tail(nc, st, R)
        fb = [st.bank(f"f{i}") for i in range(2)]
        ob = [st.bank(f"o{i}") for i in range(3)]
        q2 = st.sb("q2", [128, NH, W], F32R)
        es = [[st.sb(f"es{t}{p}", [128, NH * D]) for t in range(NT)] for p in range(2)]
        LATE = HT + 1
        om = [[st.sb(f"om{s}{i}", [128, 2 * T if i < 4 else 4 * LATE]) for i in range(6)] for s in range(2)]
        f_ready, f_act, f_dve, o_ready, o_done = (st.sem(k) for k in ("f_ready", "f_act", "f_dve", "o_ready", "o_done"))
        block = ctx.enter_context(nc.Block())
        F, U, FD = 8, 12, 4

        @block.tensor
        def _(pe):
            def front(n, p, i):
                if 2 <= i < 6:
                    pe.wait_ge(f_act, F * n + i - 1)
                elif i >= 6:
                    pe.wait_ge(f_dve, FD * n + i - 5)
                if i < 4:
                    o, tile, (e, _) = fb[i % 2][0:HT, :], slice(i * HT, (i + 1) * HT), R.atqe["ET"]
                    args = [(x[p][:, tile], R.qe[:, e:e + NH * D]) for x in (head.xh, head.xl)]
                else:
                    o, c = fb[i % 2][:, 0:W], R.atqe["Q"][0] + (i - 4) * 128
                    args = [(R.qe[:, c:c + 128], x[p][:]) for x in (head.xh, head.xl)]
                nc.tensor.matmul(o, *args[0], start=True, stop=False)
                nc.tensor.matmul(o, *args[1], start=False, stop=True).then_inc(f_ready, 1)

            def omega(n, p, smp, i):
                u = smp * 6 + i
                pe.wait_ge(o_done, n * U + u + 1)
                if i < 4:
                    tile, q = 2 * smp, q2[:, 2 * i:2 * i + 2, smp * T:(smp + 1) * T]
                else:
                    tile, q = 2 * smp + 1, q2[:, 4 * (i - 4):4 * (i - 3), (smp + 1) * T - LATE:(smp + 1) * T]
                o = split(ob[u % 3][0:HT, 0:q.shape[1] * q.shape[2]], t=q.shape[1])
                tile = slice(tile * HT, (tile + 1) * HT)
                nc.tensor.matmul(o, head.xh[p][:, tile], q, start=True, stop=False)
                nc.tensor.matmul(o, head.xl[p][:, tile], q, start=False, stop=True).then_inc(o_ready, 1)

            def result(p, smp, h):
                first, late = om[smp][h // 2], om[smp][4 + h // 4]
                nc.tensor.matmul(tail.yT[0:D, smp * T:(smp + 1) * T], es[p][2 * smp][0:HT, h * D:(h + 1) * D],
                                 first[0:HT, h % 2 * T:(h % 2 + 1) * T], start=h == 0, stop=False,
                                 skip_group_check=True)
                return add(nc, tail.yT[0:D, (smp + 1) * T - LATE:(smp + 1) * T],
                           es[p][2 * smp + 1][0:HT, h * D:(h + 1) * D],
                           late[0:HT, h % 4 * LATE:(h % 4 + 1) * LATE], stop=h == NH - 1)

            def first_sample(n, p):
                pe.wait_ge(f_dve, FD * (n + 1))
                for i in range(6):
                    omega(n, p, 0, i)

            def pro():
                head.pe(pe, 0, 0)
                pe.wait_ge(head.x_ready, 1)
                for i in range(F):
                    front(0, 0, i)
                first_sample(0, 0)

            def body(n, p, more):
                if more:
                    head.pe(pe, n + 1, 1 - p)
                for i in range(6):
                    omega(n, p, 1, i)
                    if i == 1:
                        pe.wait_ge(o_done, n * U + 6 + 3)
                    for h in ((), (0,), (1, 2), (3, 4), (5, 6), (7,))[i]:
                        result(p, 0, h)
                    if i >= 2 and more:
                        if i == 2:
                            pe.wait_ge(head.x_ready, n + 2)
                        front(n + 1, 1 - p, i - 2)
                for i in range(4):
                    if more:
                        front(n + 1, 1 - p, 4 + i)
                    if i == 0:
                        pe.wait_ge(o_done, n * U + 12 + 3)
                    for h in (2 * i, 2 * i + 1):
                        mm = result(p, 1, h)
                mm.then_inc(tail.yT_ready, 1)
                if more:
                    first_sample(n + 1, 1 - p)
                tail.pe(pe, n)

            pipelined(pe, pro, body)

        @block.scalar
        def _(act):
            def front(n, p):
                for i in range(F):
                    act.wait_ge(f_ready, n * F + i + 1)
                    if i < 4:
                        nc.scalar.copy(es[p][i][0:HT, :], fb[i % 2][0:HT, :]).then_inc(f_act, 1)
                    else:
                        nc.scalar.copy(q2[0:D, 2 * (i - 4), :], fb[i % 2][0:D, 0:W])
                        nc.scalar.copy(q2[0:D, 2 * (i - 4) + 1, :], fb[i % 2][D:2 * D, 0:W]).then_inc(f_act, 1)

            def pro():
                head.high_act(act, 0, 0)
                front(0, 0)

            def body(n, p, more):
                if more:
                    head.high_act(act, n + 1, 1 - p)
                    front(n + 1, 1 - p)
                tail.act(act, n)

            pipelined(act, pro, body)

        @block.vector
        def _(dve):
            causal = R.c128("causal", 0, HT)

            def q_low(n):
                for i in range(4):
                    dve.wait_ge(f_act, n * F + 4 + i + 1)
                    for k in range(2):
                        done = nc.vector.tensor_tensor(q2[D:2 * D, 2 * i + k, :], fb[i % 2][k * D:(k + 1) * D, 0:W],
                                                       q2[0:D, 2 * i + k, :].bitcast(F32), ALU.subtract)
                    done.then_inc(f_dve, 1)

            def masks(n, smp):
                for i in range(6):
                    u = smp * 6 + i
                    dve.wait_ge(o_ready, n * U + u + 1)
                    k, mask = (2, causal[:, 1:T + 1]) if i < 4 else (4, causal[:, 0:LATE])
                    cols = mask.shape[1]
                    nc.vector.tensor_tensor(split(om[smp][i][0:HT, :], t=k), split(ob[u % 3][0:HT, 0:k * cols], t=k),
                                            mask.unsqueeze(1).to_broadcast([HT, k, cols]), ALU.mult).then_inc(o_done, 1)

            def pro():
                dve.sem_inc(o_done, 3)
                tail.first(dve)
                head.xn_dve(dve, 0, 0)
                head.xn_dve(dve, 1, 1)
                head.low_dve(dve, 0, 0)
                q_low(0)
                masks(0, 0)

            def body(n, p, more):
                if more > 1:
                    head.xn_dve(dve, n + 2, p)
                if more:
                    head.low_dve(dve, n + 1, 1 - p)
                masks(n, 1)
                if more:
                    q_low(n + 1)
                    masks(n + 1, 0)
                tail.residual(dve, n, p, ln)

            pipelined(dve, pro, body)

        @block.gpsimd
        def _(pool):
            ln.finish(pool)


def sigmoid_attention(nc, R):
    with ExitStack() as ctx:
        st = Stage(nc, ctx, "sig")
        ln, head, tail = Norm(nc, st, R, by_pool=True), Head(nc, st, R), Tail(nc, st, R)
        qb = st.bank("q")
        ab = [[st.bank(f"a{s}{p}") for s in range(2)] for p in range(2)]
        qh, ql = ([st.sb(f"{k}{p}", [128, W], F32R) for p in range(2)] for k in ("qh", "ql"))
        att = [[st.sb(f"att{s}{p}", [128, W]) for s in range(2)] for p in range(2)]
        q_ready, qh_ready, ql_ready, a_ready, a_done = (
            st.sem(k) for k in ("q_ready", "qh_ready", "ql_ready", "a_ready", "a_done"))
        xv = [st.sb(f"xv{p}", [128, PAIR]) for p in range(2)]
        xv_ready = st.sem("xv_ready")
        block = ctx.enter_context(nc.Block())

        @block.tensor
        def _(pe):
            def query(n, p):
                pe.wait_ge(head.x_ready, n + 1)
                product64(nc, qb[:, 0:W], R, "qw2", head.x2[p][:]).then_inc(q_ready, 1)

            def scores(n, p):
                pe.wait_ge(ql_ready, n + 1)
                for smp in range(2):
                    for i in range(2):
                        tile = 2 * smp + i
                        o, x = ab[p][smp][0:HT, i * T:(i + 1) * T], head.x2[p][:, tile * HT:(tile + 1) * HT]
                        nc.tensor.matmul(o, x, qh[p][:, smp * T:(smp + 1) * T], start=True, stop=False,
                                         skip_group_check=True)
                        mm = add(nc, o, x, ql[p][:, smp * T:(smp + 1) * T], stop=True)
                    mm.then_inc(a_ready, 1)

            def values(n, p):
                pe.wait_ge(xv_ready, n + 1)
                for smp in range(2):
                    pe.wait_ge(a_done, 2 * n + smp + 1)
                    for i in range(2):
                        tile = 2 * smp + i
                        mm = nc.tensor.matmul(tail.yT[0:D, smp * T:(smp + 1) * T],
                                              xv[p][0:HT, tile * D:(tile + 1) * D],
                                              att[p][smp][0:HT, i * T:(i + 1) * T], start=i == 0, stop=i == 1,
                                              skip_group_check=True)
                mm.then_inc(tail.yT_ready, 1)

            def pro():
                head.pe(pe, 0, 0)
                query(0, 0)
                head.pe(pe, 1, 1)
                scores(0, 0)
                query(1, 1)
                head.pe(pe, 2, 0)

            def body(n, p, more):
                values(n, p)
                if more:
                    scores(n + 1, 1 - p)
                if more > 1:
                    query(n + 2, p)
                tail.pe(pe, n)
                if more > 2:
                    head.pe(pe, n + 3, 1 - p)

            pipelined(pe, pro, body, last=4)

        @block.scalar
        def _(act):
            def query(n, p):
                act.wait_ge(q_ready, n + 1)
                nc.scalar.copy(qh[p][:], qb[:, 0:W]).then_inc(qh_ready, 1)

            def sigmoid(n, p):
                for smp in range(2):
                    act.wait_ge(a_ready, 2 * n + smp + 1)
                    nc.scalar.activation(att[p][smp][0:HT, :], ab[p][smp][0:HT, 0:W], ACT.Sigmoid).then_inc(a_done, 1)

            def pro():
                head.high_act(act, 0, 0)
                query(0, 0)
                head.high_act(act, 1, 1)
                sigmoid(0, 0)
                query(1, 1)
                head.high_act(act, 2, 0)

            def body(n, p, more):
                tail.act(act, n)
                if more:
                    sigmoid(n + 1, 1 - p)
                if more > 1:
                    query(n + 2, p)
                if more > 2:
                    head.high_act(act, n + 3, 1 - p)

            pipelined(act, pro, body, last=4)

        @block.vector
        def _(dve):
            def query_low(n, p):
                dve.wait_ge(qh_ready, n + 1)
                nc.vector.tensor_tensor(ql[p][:], qb[:, 0:W], qh[p][:].bitcast(F32), ALU.subtract).then_inc(ql_ready, 1)

            def pro():
                tail.first(dve)
                head.xn_dve(dve, 0, 0)
                head.xn_dve(dve, 1, 1)
                for n in range(2):
                    head.low_dve(dve, n, n)
                    query_low(n, n)
                dve.wait_ge(xv_ready, 1)
                head.xn_dve(dve, 2, 0)

            def body(n, p, more):
                if more > 1:
                    head.low_dve(dve, n + 2, p)
                if more > 2:
                    dve.wait_ge(xv_ready, n + 2)
                    dve.nop(nofuse=True)
                    head.xn_dve(dve, n + 3, 1 - p)
                tail.residual(dve, n, p, ln)
                if more > 1:
                    query_low(n + 2, p)

            pipelined(dve, pro, body, last=4)

        @block.gpsimd
        def _(pool):
            def copy(n, p):
                pool.wait_ge(head.xn_ready, n + 1)
                pool.nop(nofuse=True)
                nc.gpsimd.tensor_copy(xv[p][0:HT, :], head.xn[p][0:HT, :]).then_inc(xv_ready, 1)

            def pro():
                pool.sem_inc(ln.rstd_done, 2)
                copy(0, 0)
                copy(1, 1)

            def body(n, p, more):
                if more > 1:
                    pool.wait_ge(tail.yT_ready, n + 1)
                    copy(n + 2, p)
                ln.rstd(pool, n, p)

            pipelined(pool, pro, body, last=4)


def depths(nc, R, out):
    with ExitStack() as ctx:
        st = Stage(nc, ctx, "mod")
        head, tail = Head(nc, st, R), Tail(nc, st, R, bias="L3b2")
        wb, wcolumn = st.bank("weights"), [st.bank(f"wcolumn{p}") for p in range(2)]
        hb = [st.bank(f"hidden{i}") for i in range(2)]
        hid = [st.sb(f"hid{i}", [128, W]) for i in range(2)]
        wrow = [st.sb(f"wrow{p}", [128, W]) for p in range(2)]
        scr = [st.sb(f"scr{i}", [128, T]) for i in range(2)]
        wcol, hi, ties, rank, f = (st.sb(k, [128, NT]) for k in ("wcol", "higher", "ties", "rank", "factor"))
        x_and_h = [st.sb(f"x_and_h{p}", [128, PAIR]) for p in range(2)]
        o = [st.sb(f"o{p}", [128, PAIR]) for p in range(2)]
        w_ready, wrow_ready, wcol_ready, h_ready, h_done, sum_ready, o_ready = (
            st.sem(k) for k in ("w_ready", "wrow_ready", "wcol_ready", "h_ready", "h_done", "sum_ready", "o_ready"))
        stored = [st.sem(f"stored{p}") for p in range(2)]
        block = ctx.enter_context(nc.Block())

        @block.tensor
        def _(pe):
            def front(n, p):
                pe.wait_ge(head.x_ready, n + 1)
                product64(nc, wb[:, 0:W], R, "wr_rep", head.x2[p][:]).then_inc(w_ready, 1)
                for i in range(2):
                    product64(nc, hb[i][:, 0:W], R, "L3w1", head.x2[p][:], a=i * 128).then_inc(h_ready, 1)

            def columns(n, p):
                pe.wait_ge(wrow_ready, n + 1)
                for t in range(NT):
                    mm = nc.tensor.transpose(wcolumn[p][0:HT, t * HT:(t + 1) * HT],
                                             wrow[p][0:HT, t * HT:(t + 1) * HT], R.c128("ident", 0, HT, 0, HT))
                mm.then_inc(wcol_ready, 1)

            def pro():
                head.pe(pe, 0, 0)
                front(0, 0)
                head.pe(pe, 1, 1)
                columns(0, 0)

            def body(n, p, more):
                pe.wait_ge(h_done, 2 * n + 2)
                for i in range(2):
                    mm = nc.tensor.matmul(tail.yT[0:D, 0:W], R.c128("L3w2", 0, 128, i * D, D), hid[i][:],
                                          start=i == 0, stop=i == 1, skip_group_check=True)
                mm.then_inc(tail.yT_ready, 1)
                if more:
                    front(n + 1, 1 - p)
                tail.pe(pe, n)
                if more > 1:
                    head.pe(pe, n + 2, p)
                if more:
                    columns(n + 1, 1 - p)

            pipelined(pe, pro, body)

        @block.scalar
        def _(act):
            def front(n, p):
                act.wait_ge(w_ready, n + 1)
                wait_reuse(act, tail.y_used, n)
                nc.scalar.activation(wrow[p][0:HT, :], wb[0:HT, 0:W], ACT.Identity, bias=R.c128("L3br", 0, HT))\
                    .then_inc(wrow_ready, 1)
                for i in range(2):
                    act.wait_ge(h_ready, 2 * n + i + 1)
                    nc.scalar.activation(hid[i][:], hb[i][:, 0:W], ACT.Gelu_apprx_tanh,
                                         bias=R.c128("L3b1", 0, 128, i, 1)).then_inc(h_done, 1)

            def pro():
                head.high_act(act, 0, 0)
                front(0, 0)
                head.high_act(act, 1, 1)

            def body(n, p, more):
                tail.act(act, n)
                if more:
                    front(n + 1, 1 - p)
                if more > 1:
                    head.high_act(act, n + 2, p)

            pipelined(act, pro, body)

        @block.vector
        def _(dve):
            def pro():
                tail.first(dve)
                dve.sem_inc(o_ready, 2)
                for s in stored:
                    dve.sem_inc(s, 16)
                head.xn_dve(dve, 0, 0)
                head.xn_dve(dve, 1, 1)
                head.low_dve(dve, 0, 0)

            def body(n, p, more):
                if more:
                    head.low_dve(dve, n + 1, 1 - p)
                dve.wait_ge(sum_ready, n + 1)
                if more > 1:
                    dve.nop(nofuse=True)
                    head.xn_dve(dve, n + 2, p)
                dve.wait_ge(wcol_ready, n + 1)
                dve.nop(nofuse=True)
                nc.vector.tensor_copy(wcol[0:HT, :], wcolumn[p][0:HT, 0:W:HT])
                dve.drain()
                for t in range(NT):
                    row = wrow[p][0:HT, (t // 2) * T:(t // 2 + 1) * T]
                    nc.vector.tensor_scalar(scr[0][0:HT, :], row, wcol[0:HT, t:t + 1], None, ALU.is_gt, ALU.add,
                                            accum_out=hi[0:HT, t:t + 1])
                    nc.vector.scalar_tensor_tensor(out=scr[1][0:HT, :], in0=row, scalar=wcol[0:HT, t:t + 1],
                                                   in1=R.c128("earlier", 0, HT, (t % 2) * T, T), op0=ALU.is_equal,
                                                   op1=ALU.mult, accum_out=ties[0:HT, t:t + 1])
                    dve.drain()
                nc.vector.tensor_tensor(rank[0:HT, :], hi[0:HT, :], ties[0:HT, :], ALU.add)
                dve.drain()
                nc.vector.scalar_tensor_tensor(out=f[0:HT, :], in0=rank[0:HT, :], scalar=float(KEEP),
                                               in1=wcol[0:HT, :], op0=ALU.is_lt, op1=ALU.mult)
                dve.drain()
                dve.wait_ge(stored[p], 8 * (n - p) + 16)
                dve.wait_ge(tail.y_ready, n + 1)
                nc.vector.tensor_tensor(split(o[p][0:HT, :], t=NT), split(tail.y[0:HT, 0:PAIR], t=NT),
                                        spread(f[0:HT, :], D), ALU.mult).then_inc(tail.y_used, 1)
                dve.drain()
                nc.vector.tensor_tensor(o[p][0:HT, :], o[p][0:HT, :], x_and_h[p][0:HT, :], ALU.add).then_inc(o_ready, 1)

            pipelined(dve, pro, body)

        @block.gpsimd
        def _(pool):
            def body(n, p, more):
                pool.wait_ge(head.xn_ready, n + 1)
                pool.wait_ge(o_ready, n + 1)
                pool.nop(nofuse=True)
                nc.gpsimd.tensor_tensor(x_and_h[p][0:HT, :], head.xn[p][0:HT, :], hpair(R, n), ALU.add)\
                    .then_inc(sum_ready, 1)

            pipelined(pool, lambda: None, body)

        @block.sync
        def _(sp):
            def store(n, p):
                sp.wait_ge(o_ready, n + 3)
                sp.dma_start(out[bass.ds(2 * n, 2)].rearrange("s (two t) d -> t (s two) d", two=2),
                             split(o[p][0:HT, :], t=NT)).then_inc(stored[p], 16)

            with sp.Fori(0, PAIRS // 2) as j:
                store(2 * j, 0)
                store(2 * j + 1, 1)
            for s in stored:
                sp.wait_ge(s, 16 * (PAIRS // 2) + 16)


class Resident:
    pass


def fusion_kernel(nc, x, txt, p128, p1, tokw, p64, pqe, pc, others, out):
    with ExitStack() as ctx:
        st = Stage(nc, ctx, "all")
        R = Resident()
        R.h, R.hc = st.sb("h", [128, PAIRS * PAIR]), st.sb("centred", [128, PAIRS * PAIR])
        R.rstd = st.sb("rstd", [128, PAIRS * NT])
        R.neghalf, R.half = st.sb("neghalf", [128, NT]), st.sb("half", [128, 1])
        R.ones = st.sb("ones", [1, 128])
        R.lru = st.sb("lru_consts", [128, 4])
        R.cos, R.sin, R.decay = st.sb("cos", [128, T]), st.sb("sin", [128, T]), st.sb("decay", [128, W])
        R.negC = st.sb("negC", [128, 4 * D])
        R.var = st.sb("var", [128, PAIRS * NT])
        R.gates = st.sb("gates", [128, PAIRS + 1, 2, NT * E2])
        R.x2 = st.sb("x2", [128, PAIRS * W], F32R)
        R.wh, R.wl = (st.sb(k, [128, offsets(PACK64)[1]], F32R) for k in ("w_high", "w_low"))
        R.qe = st.sb("quadratic_w", [128, offsets(PACKQE)[1]], F32R)
        R.pick = st.sb("top1_pick", [128, offsets(PACKC)[1]], F32R)
        R.pick_expert = st.sb("picks", [128, E2 * 128], F32R)
        R.b2h, R.b2l = (st.sb(k, [128, 3 * D], F32R) for k in ("b2_high", "b2_low"))
        R.at64, R.atqe = offsets(PACK64)[0], offsets(PACKQE)[0]
        t128, t1 = st.sb("p128", [128, offsets(PACK128)[1]]), st.sb("p1", [1, offsets(PACK1)[1]])
        R.c128, R.c1 = Named(t128, PACK128), Named(t1, PACK1)
        v_dram = nc.dram_tensor("v_scratch", [B, KD * T], F32).ap()
        ctx_dram = nc.dram_tensor("ctx_scratch", [B, 2, HT, NH * KD], F32).ap()

        tokenizer(nc, R, x, txt, [(t128[:], p128), (t1[:], p1)], tokw, p64, pqe, pc, others)
        lru(nc, R)
        top1(nc, R)
        attention(nc, R, v_dram, ctx_dram)
        top2_route(nc, R, "rg", "L1WrT", ["L1br"], own_norm=True)
        top2(nc, R, "gelu2", "L1W1", "L1b1", "L1W2", "L1b2", ACT.Gelu)
        quadratic(nc, R)
        top2_route(nc, R, "rr", "L2WgT", ["L2bg", "L2bias"], own_norm=False)
        top2(nc, R, "relu2", "L2W1", "L2b1", "L2W2", "L2b2", ACT.Relu)
        sigmoid_attention(nc, R)
        depths(nc, R, out)


def pack(spec, parts, rows):
    for name, n in spec:
        assert parts[name].shape == (rows, n), (name, parts[name].shape, n)
    return np.ascontiguousarray(np.concatenate([parts[name] for name, _ in spec], axis=1))


def laid_out(i):
    f = np.float32
    rep = lambda v, n: np.tile(v.reshape(1, -1), (1, n))
    experts_in = lambda w: w.transpose(1, 0, 2).reshape(w.shape[1], -1)
    x = i["x"].reshape(PAIRS, 2, D, XM, 2).transpose(0, 4, 2, 1, 3).reshape(PAIRS, 128, 2, XM)
    w = i["L0_tok_weight"].reshape(D, 25, D)
    w = np.concatenate([w, np.zeros((D, 1, D), f)], axis=1).reshape(D, KPAR, 2, D)
    tokw = w.transpose(2, 0, 1, 3).reshape(128, KPAR * D)
    twice = lambda w: np.tile(w, (1, 2))
    p64 = {"L0W1": experts_in(i["L0_ffn_W1"]), "B_reT": i["L0_attn_B_re"].T, "B_imT": i["L0_attn_B_im"].T,
           "DT2": twice(i["L0_attn_D"].T), "routerT": i["L0_ffn_router_w"].T, "WqT": i["L1_attn_Wq"].T,
           "WkT2": twice(i["L1_attn_Wk"].T), "WvT2": twice(i["L1_attn_Wv"].T), "L1WrT": i["L1_ffn_Wr"],
           "L1W1": experts_in(i["L1_ffn_W1"]), "L2WgT": i["L2_ffn_Wg"], "L2W1": experts_in(i["L2_ffn_W1"]),
           "qw2": twice(i["L3_attn_q_weight"]), "wr_rep": np.tile(i["L3_ffn_wr"], (1, 128)), "L3w1": i["L3_ffn_w1"]}
    pqe = {"Q": experts_in(i["L2_attn_Q"]), "ET": i["L2_attn_E"].transpose(2, 0, 1).reshape(D, -1)}
    chunks = lambda w: w.reshape(-1, 128, D).transpose(1, 0, 2).reshape(128, -1)
    column = lambda v: np.concatenate([v.reshape(-1, 1), np.zeros((128 - v.size, 1), f)])
    rows = lambda v: np.tile(v.reshape(1, -1), (128, 1))
    part = np.arange(128)[:, None]
    cols = np.arange(T)[None, :]
    gate_row = (part < 2 * NT * E2)
    by_gate = lambda b2: np.concatenate([np.tile(b2, (2 * NT, 1)), np.zeros((128 - 2 * NT * E2, D), f)])
    p128 = {"nu_log": i["L0_attn_nu_log"][:, None], "theta_log": i["L0_attn_theta_log"][:, None],
            "bh_re": i["L0_attn_bh_re"][:, None], "bh_im": i["L0_attn_bh_im"][:, None],
            "C_re2": twice(i["L0_attn_C_re"].T), "C_im2": twice(i["L0_attn_C_im"].T),
            "L0W2": chunks(i["L0_ffn_W2"].reshape(E1 * H1, D)), "WoT": chunks(np.ascontiguousarray(i["L1_attn_Wo"].T)),
            "L1W2": chunks(i["L1_ffn_W2"].reshape(-1, D)), "L1b1": i["L1_ffn_b1"].T,
            "L2W2": chunks(i["L2_ffn_W2"].reshape(-1, D)), "L2b1": i["L2_ffn_b1"].T,
            "L3w2": chunks(i["L3_ffn_w2"]), "L3b1": i["L3_ffn_b1"].reshape(2, 128).T,
            "ident": np.eye(128, dtype=f),
            "desc8": np.tile(np.arange(E2, 0, -1, dtype=f), (128, PAIRS * NT)),
            "desc32": np.tile(np.arange(E1, 0, -1, dtype=f), (128, NT)),
            "causal": (part < np.arange(T + 1)[None, :]).astype(f),
            "earlier": np.concatenate([(cols < part + k * HT).astype(f) for k in range(2)], axis=1),
            "same_tile": (gate_row & (part // E2 % NT == np.arange(W)[None, :] // HT)).astype(f),
            "pick_expert": (gate_row & (part % E2 == np.arange(E2 * 128)[None, :] // 128)).astype(f),
            "L1b2": by_gate(i["L1_ffn_b2"]), "L2b2": by_gate(i["L2_ffn_b2"]),
            "router_b": rows(np.tile(i["L0_ffn_router_b"], NT)), "L1br": rows(i["L1_ffn_br"]),
            "L2bg": rows(i["L2_ffn_bg"]), "L2bias": rows(i["L2_ffn_bias"]), "L3br": rows(i["L3_ffn_br"]),
            "lru_b": column(i["L0_attn_bias_output"]), "L3b2": column(i["L3_ffn_b2"]),
            "gamma": column(i["L1_ffn_gamma"]), "beta": column(i["L1_ffn_beta"])}
    p1 = {"tok_b": rep(i["L0_tok_bias"], 2)}
    mine = np.kron(np.eye(E1, dtype=f), np.ones((1, H1), f))
    b1 = np.zeros((E1, E1, H1), f)
    b1[np.arange(E1), np.arange(E1)] = i["L0_ffn_b1"]
    pc = {"L0b1": b1.reshape(E1, -1), "L0b2_2": twice(i["L0_ffn_b2"])}
    return {"x": np.ascontiguousarray(x), "txt": i["txt"], "p128": pack(PACK128, p128, 128), "p1": pack(PACK1, p1, 1),
            "tokw": np.ascontiguousarray(tokw), "p64": pack(PACK64, p64, 64), "pqe": pack(PACKQE, pqe, 64),
            "pc": pack(PACKC, pc, E1), "others": (mine - 1) * f(BIG)}


def kernel(**inputs):
    import numpy as _np
    import concourse.bacc as _bacc
    from concourse.bass_utils import run_bass_kernel_spmd as _run

    arrays = laid_out({k: _np.asarray(v) for k, v in inputs.items()})
    nc = _bacc.Bacc("TRN2", target_bir_lowering=False, num_devices=1)
    args = [nc.dram_tensor(f"in_{k}", a.shape, F32, kind="ExternalInput").ap() for k, a in arrays.items()]
    out = nc.dram_tensor("out", (B, T, D), F32, kind="ExternalOutput").ap()
    fusion_kernel(nc, *args, out)
    r = _run(nc, [{f"in_{k}": a for k, a in arrays.items()}], core_ids=[0])
    return r.results[0]["out"]
```
